# Optimizing a Trainium2 kernel written in Bass

```python
import numpy as np
import jax
import jax.numpy as jnp

def _softmax(x, axis=-1):
    return jax.nn.softmax(x, axis=axis)

def _gelu(x):
    return jax.nn.gelu(x, approximate=True)

def _silu(x):
    return jax.nn.silu(x)

def _sigmoid(x):
    return jax.nn.sigmoid(x)

def _layernorm(x, axis=-1, eps=1e-05):
    m = jnp.mean(x, axis=axis, keepdims=True)
    v = jnp.var(x, axis=axis, keepdims=True)
    return (x - m) / jnp.sqrt(v + eps)

def _scatter_add(tgt, idx, src, axis=0):
    return tgt.at[idx].add(src)

def _segment_sum(src, seg, n):
    return jax.ops.segment_sum(src, seg, n)
kernel_name = 'mk_gnn_resnorm_d4_gnn_r64_ee92e2'

def setup_inputs(seed: int=0):
    np.random.seed(seed)
    _w = jnp.asarray

    def _rec_inputs():
        import jax
        import jax.numpy as jnp
        _gk = jax.random.key(seed)
        x = -0.0003713 + 1 * jax.random.normal(jax.random.fold_in(_gk, 1), (50000, 128), jnp.float32)
        src = jax.random.randint(jax.random.fold_in(_gk, 2), (25000,), 0, 50000, jnp.int32)
        dst = jnp.minimum((50000 * jax.random.uniform(jax.random.fold_in(_gk, 3), (25000,)) ** 2.0).astype(jnp.int32), 49999)
        _o = jnp.argsort(dst, stable=True)
        src = src[_o]
        dst = dst[_o]
        edge_type_16 = jax.random.randint(jax.random.fold_in(_gk, 12), (25000,), 0, 16, jnp.int32)
        edge_type_8 = jax.random.randint(jax.random.fold_in(_gk, 13), (25000,), 0, 8, jnp.int32)
        return (x, src, dst, edge_type_16, edge_type_8)
    x, src, dst, edge_type_16, edge_type_8 = _rec_inputs()

    def _L0_gnn_setup():
        import jax, jax.numpy as jnp
        import numpy as np

        def _gcn_conv(x, W, b, src, dst, dinv, n_nodes):
            h = x @ W
            norm = dinv[src] * dinv[dst]
            msgs = h[src] * norm[:, None]
            out = jax.ops.segment_sum(msgs, dst, num_segments=n_nodes)
            return out + b
        key = jax.random.key(seed)
        k1, k2, k3, k4 = jax.random.split(key, 4)
        N, E, C = (100000, 25000, 128)
        x = jax.random.normal(k1, (N, C), dtype=jnp.float32)
        edge_index = jax.random.randint(k2, (2, E), 0, N, dtype=jnp.int32)
        s = 1.0 / np.sqrt(C)
        W1 = jax.random.normal(k3, (C, C), dtype=jnp.float32) * s
        W2 = jax.random.normal(k4, (C, C), dtype=jnp.float32) * s
        b1 = jnp.zeros((C,), dtype=jnp.float32)
        b2 = jnp.zeros((C,), dtype=jnp.float32)
        return {'x': x, 'edge_index': edge_index, 'W1': W1, 'b1': b1, 'W2': W2, 'b2': b2}
    _L0_gnn_all = _L0_gnn_setup()
    _L0_gnn_in = {k: v for k, v in _L0_gnn_all.items() if k in ('W1', 'b1', 'W2', 'b2')}
    del _L0_gnn_all

    def _L1_gnn_setup():
        import jax, jax.numpy as jnp
        import numpy as np
        N, E, D, R = (50000, 9375, 128, 8)
        key = jax.random.key(seed)
        k1, k2, k3, k4, k5 = jax.random.split(key, 5)
        x = jax.random.normal(k1, (N, D), dtype=jnp.float32)
        edge_index = jax.random.randint(k2, (2, E), 0, N, dtype=jnp.int64)
        edge_type = jax.random.randint(k3, (E,), 0, R, dtype=jnp.int64)
        scale = 1.0 / np.sqrt(D)
        W = jax.random.normal(k4, (R, D, D), dtype=jnp.float32) * scale
        root = jax.random.normal(k5, (D, D), dtype=jnp.float32) * scale
        bias = jnp.zeros((D,), dtype=jnp.float32)
        return {'x': x, 'edge_index': edge_index, 'edge_type': edge_type, 'W': W, 'root': root, 'bias': bias}
    _L1_gnn_all = _L1_gnn_setup()
    _L1_gnn_in = {k: v for k, v in _L1_gnn_all.items() if k in ('W', 'root', 'bias')}
    del _L1_gnn_all

    def _L2_gnn_setup():
        import jax, jax.numpy as jnp
        import numpy as np
        NUM_RELATIONS = 8
        key = jax.random.key(seed)
        k1, k2, k3, k4 = jax.random.split(key, 4)
        N, E, D = (50000, 9375, 128)
        x = jax.random.normal(k1, (N, D), dtype=jnp.float32)
        scale = float(np.sqrt(6.0 / (D + D)))
        W = jax.random.uniform(k2, (NUM_RELATIONS, D, D), dtype=jnp.float32, minval=-scale, maxval=scale)
        edge_index = jax.random.randint(k3, (2, E), 0, N, dtype=jnp.int64)
        edge_type = jax.random.randint(k4, (E,), 0, NUM_RELATIONS, dtype=jnp.int64)
        return {'x': x, 'W': W, 'edge_index': edge_index, 'edge_type': edge_type}
    _L2_gnn_all = _L2_gnn_setup()
    _L2_gnn_in = {k: v for k, v in _L2_gnn_all.items() if k in ('W',)}
    del _L2_gnn_all

    def _L3_gnn_setup():
        import jax, jax.numpy as jnp
        import numpy as np
        N_NODES = 50000
        N_EDGES = 500000
        IN_FEAT = 128
        OUT_FEAT = 128
        N_REL = 16
        key = jax.random.key(seed)
        k1, k2, k3, k4 = jax.random.split(key, 4)
        entity_embeddings = jax.random.normal(k1, (N_NODES, IN_FEAT), dtype=jnp.float32)
        limit = (6.0 / (IN_FEAT + OUT_FEAT)) ** 0.5
        weight = jax.random.uniform(k2, (N_REL, IN_FEAT, OUT_FEAT), dtype=jnp.float32, minval=-limit, maxval=limit)
        edge_index = jax.random.randint(k3, (2, N_EDGES), 0, N_NODES, dtype=jnp.int64)
        edge_type = jax.random.randint(k4, (N_EDGES,), 0, N_REL, dtype=jnp.int64)
        return {'entity_embeddings': entity_embeddings, 'weight': weight, 'edge_index': edge_index, 'edge_type': edge_type}
    _L3_gnn_all = _L3_gnn_setup()
    _L3_gnn_in = {k: v for k, v in _L3_gnn_all.items() if k in ('weight',)}
    del _L3_gnn_all
    return {'x': x, 'src': src, 'dst': dst, 'edge_type_16': edge_type_16, 'edge_type_8': edge_type_8, 'L0_gnn_W1': _L0_gnn_in['W1'], 'L0_gnn_b1': _L0_gnn_in['b1'], 'L0_gnn_W2': _L0_gnn_in['W2'], 'L0_gnn_b2': _L0_gnn_in['b2'], 'L1_gnn_W': _L1_gnn_in['W'], 'L1_gnn_root': _L1_gnn_in['root'], 'L1_gnn_bias': _L1_gnn_in['bias'], 'L2_gnn_W': _L2_gnn_in['W'], 'L3_gnn_weight': _L3_gnn_in['weight']}

def reference(x, src, dst, edge_type_16, edge_type_8, L0_gnn_W1, L0_gnn_b1, L0_gnn_W2, L0_gnn_b2, L1_gnn_W, L1_gnn_root, L1_gnn_bias, L2_gnn_W, L3_gnn_weight):
    import jax
    import jax.numpy as jnp

    def _L0_gnn_ref(x, edge_index, W1, b1, W2, b2):
        import jax, jax.numpy as jnp
        import numpy as np

        def _gcn_conv(x, W, b, src, dst, dinv, n_nodes):
            h = x @ W
            norm = dinv[src] * dinv[dst]
            msgs = h[src] * norm[:, None]
            out = jax.ops.segment_sum(msgs, dst, num_segments=n_nodes)
            return out + b
        n_nodes = x.shape[0]
        loops = jnp.arange(n_nodes, dtype=edge_index.dtype)
        src = jnp.concatenate([edge_index[0], loops])
        dst = jnp.concatenate([edge_index[1], loops])
        deg = jax.ops.segment_sum(jnp.ones_like(dst, dtype=x.dtype), dst, num_segments=n_nodes)
        dinv = jnp.where(deg > 0, jax.lax.rsqrt(jnp.maximum(deg, 1e-12)), 0.0)
        h = _gcn_conv(x, W1, b1, src, dst, dinv, n_nodes)
        h = jax.nn.relu(h)
        out = _gcn_conv(h, W2, b2, src, dst, dinv, n_nodes)
        return out

    def _L1_gnn_ref(x, edge_index, edge_type, W, root, bias):
        import jax, jax.numpy as jnp
        import numpy as np
        N, E, D, R = (50000, 9375, 128, 8)
        n_nodes = x.shape[0]
        num_rels = W.shape[0]
        src, dst = (edge_index[0], edge_index[1])
        out = x @ root + bias
        for r in range(num_rels):
            mask = (edge_type == r).astype(x.dtype)
            h = x @ W[r]
            msg = h[src] * mask[:, None]
            agg = jax.ops.segment_sum(msg, dst, num_segments=n_nodes)
            deg = jax.ops.segment_sum(mask, dst, num_segments=n_nodes)
            out = out + agg / jnp.maximum(deg, 1.0)[:, None]
        return out

    def _L2_gnn_ref(x, W, edge_index, edge_type):
        import jax, jax.numpy as jnp
        import numpy as np
        NUM_RELATIONS = 8
        N = x.shape[0]
        R = W.shape[0]
        h = jnp.einsum('nd,rde->rne', x, W)
        src, dst = (edge_index[0], edge_index[1])
        h_src = h[edge_type, src]
        h_dst = h[edge_type, dst]
        attn = jnp.sum(h_src * h_dst, axis=-1)
        attn = jax.nn.leaky_relu(attn, negative_slope=0.2)
        seg_max = jax.ops.segment_max(attn, edge_type, num_segments=R)
        ex = jnp.exp(attn - seg_max[edge_type])
        denom = jax.ops.segment_sum(ex, edge_type, num_segments=R)
        a = ex / denom[edge_type]
        out = jax.ops.segment_sum(h_src * a[:, None], dst, num_segments=N)
        return out

    def _L3_gnn_ref(entity_embeddings, weight, edge_index, edge_type):
        import jax, jax.numpy as jnp
        import numpy as np
        N_NODES = 50000
        N_EDGES = 500000
        IN_FEAT = 128
        OUT_FEAT = 128
        N_REL = 16
        num_entities = entity_embeddings.shape[0]
        src = edge_index[0]
        tgt = edge_index[1]
        transformed = jnp.einsum('ni,rio->rno', entity_embeddings, weight)
        msg = transformed[edge_type, src]
        messages = jax.ops.segment_sum(msg, tgt, num_segments=num_entities)
        return jax.nn.relu(messages)
    edge_index = jnp.stack([src, dst])
    x = _layernorm(x + _L0_gnn_ref(x, edge_index, L0_gnn_W1, L0_gnn_b1, L0_gnn_W2, L0_gnn_b2), axis=-1)
    x = _layernorm(x + _L1_gnn_ref(x, edge_index, edge_type_8, L1_gnn_W, L1_gnn_root, L1_gnn_bias), axis=-1)
    x = _layernorm(x + _L2_gnn_ref(x, L2_gnn_W, edge_index, edge_type_8), axis=-1)
    x = _layernorm(x + _L3_gnn_ref(x, L3_gnn_weight, edge_index, edge_type_16), axis=-1)
    return x

_drawn_inputs = setup_inputs


def setup_inputs(seed=0):
    import zlib

    import numpy as np

    out = dict(_drawn_inputs(seed))
    spreads = {'L0_gnn_b1': (0.0, 0.1), 'L0_gnn_b2': (0.0, 0.1), 'L1_gnn_bias': (0.0, 0.1)}
    factors = {}
    for name, (base, spread) in spreads.items():
        noise = np.random.default_rng([zlib.crc32(name.encode()), seed]).standard_normal(out[name].shape)
        drawn = base * np.exp(spread * noise) if base else spread * noise
        out[name] = jnp.asarray(drawn.astype(out[name].dtype))
    for name, factor in factors.items():
        out[name] = (out[name] * factor).astype(out[name].dtype)
    return out
```

```python
from contextlib import ExitStack

import concourse.bass as bass
from concourse import mybir
from concourse.alu_op_type import AluOpType as ALU

F32 = mybir.dt.float32
BF16 = mybir.dt.bfloat16
I32 = mybir.dt.int32
ACT = mybir.ActivationFunctionType
AX = mybir.AxisListType

N, D, E = 50000, 128, 25000
P = 128
TE = P
BT = 4
BE = BT * TE
NB = -(-E // BE)
EP = NB * BE
KT = EP // TE
RPP = -(-N // (P * BT)) * BT
NP = P * RPP
NCH = RPP // BT
QR = EP // 256
R8, R16 = 8, 16
FAR = 65536
PAD_DST, PAD_SRC, PAD_TYPE = 60000, 0, -1
EPS = 1e-5
SLOPE = 0.2
LOW = -1.0e30
SRC, DST, T8, T16 = range(4)


def static(b):
    return isinstance(b, int)


def runs(b, first=0, last=NB - 1):
    return not static(b) or first <= b <= last


def bc(ap, width):
    return ap.rearrange("p (n o) -> p n o", o=1).to_broadcast([ap.shape[0], ap.shape[1], width])


def hold(eng, sem, value):
    eng.wait_ge(sem, value)
    if not static(value):
        eng.nop(nofuse=True)


def of_slot(b, q, inc):
    return (b - q) * (inc // 2) + inc


def pipeline(eng, body, first, last, ahead, behind):
    lo = behind + 2 + (behind % 2)
    hi = NB - ahead
    hi -= (hi - lo) % 2
    for b in range(first, lo):
        body(b, b % 2)
    with eng.Fori(lo // 2, hi // 2) as pair:
        body(pair * 2, 0)
        body(pair * 2 + 1, 1)
    for b in range(hi, last + 1):
        body(b, b % 2)


class Semaphores:

    def __init__(self, nc, prefix):
        self.nc, self.prefix, self.mine = nc, prefix, []

    def __call__(self, name):
        self.mine.append(self.nc.alloc_semaphore(self.prefix + name))
        return self.mine[-1]

    def of_pool(self, name):
        return [self.nc.alloc_semaphore(f"{self.prefix}{name}_{slot}") for slot in ("even", "odd")]

    def clear(self):
        with self.nc.Block() as block:
            @block.gpsimd
            def _(pool):
                for s in self.mine:
                    pool.sem_clear(s)
        for s in self.mine:
            self.nc.release_semaphore(s)


class Memory:
    pass


def at(col, b, n=BT):
    return col[:, bass.ds(b * n, n)]


def constants_stage(nc, m):
    with ExitStack() as ctx:
        sem = Semaphores(nc, "co_")
        consts = sem("consts")
        ctx.callback(sem.clear)
        block = ctx.enter_context(nc.Block())

        @block.gpsimd
        def _(pool):
            pool.memset(m.ident[:, :], 0.0).then_inc(consts, 1)
            hold(pool, consts, 1)
            pool.affine_select(out=m.ident[:, :], in_=m.ident[:, :], compare_op=ALU.not_equal, fill=1.0,
                               base=0, pattern=[[-1, P]], channel_multiplier=1).then_inc(consts, 1)
            pool.iota(m.iota[:, :], pattern=[[1, RPP]], base=0, channel_multiplier=0,
                      allow_small_or_imprecise_dtypes=True).then_inc(consts, 1)
            pool.memset(m.ones[:, :], 1.0).then_inc(consts, 1)
            pool.memset(m.eps[:, :], EPS).then_inc(consts, 1)


def order_stage(nc, io, m):
    with ExitStack() as ctx:
        sb = lambda n, s, d=F32: ctx.enter_context(nc.sbuf_tensor("or_" + n, s, d))
        sem = Semaphores(nc, "or_")
        halof = sb("halof", [QR, 257])
        falls = sb("falls", [QR, 256])
        fell = sb("fell", [QR, 1])
        unsorted = sb("unsorted", [1, 1], I32)
        rowf = sb("rowf", [QR, 4, 256])
        col = sb("col", [P, 4, KT])
        number = sb("number", [P, KT])
        place = sb("place", [P, KT])
        others = sb("others", [P, BE], I32)
        othersf = sb("othersf", [P, BE])
        numbers = sb("numbers", [P, BE])
        less, equal, before = (sb(n, [P, BT, BE]) for n in ("less", "equal", "before"))
        count = sb("count", [P, BT])
        record = sb("record", [P, 4], I32)
        where = sb("where", [P, 1], I32)
        packed = sb("packed", [QR, 256, 4], I32)
        loaded, prep, counted, flagged, turned, copied = (
            sem(n) for n in ("loaded", "prep", "counted", "flagged", "turned", "copied"))
        spread, used, numbered, staged, sorted_rows, unpacked, halo_set = (
            sem(n) for n in ("spread", "used", "numbered", "staged", "sorted_rows", "unpacked", "halo_set"))
        placed, vc = sem.of_pool("placed")[0], sem("chain")
        edges, halo, rows, ps = io["edges"], m.halo, m.rows, m.psum
        ctx.callback(sem.clear)
        block = ctx.enter_context(nc.Block())

        def neighbours(sp, dst, done):
            with nc.allow_non_contiguous_dma(reason="one element per partition"):
                sp.dma_start(halo[1:QR, 0:1], dst[255:EP - 1:256].rearrange("(q n) -> q n", n=1)).then_inc(done, 16)
                sp.dma_start(halo[0:QR - 1, 257:258], dst[256:EP:256].rearrange("(q n) -> q n", n=1)).then_inc(done, 16)

        def out_of_order(eng):
            eng.wait_ge(flagged, 1)
            return eng.value_load(unsorted[0:1, 0:1], min_val=0, max_val=1) > 0

        @block.sync
        def _(sp):
            sp.wait_ge(prep, 1)
            neighbours(sp, edges[DST, :], loaded)
            sp.dma_start(halo[:, 1:257], edges[DST, :].rearrange("(q n) -> q n", n=256)).then_inc(loaded, 16)
            for f in range(4):
                sp.dma_start(rows[:, f, :], edges[f, :].rearrange("(q n) -> q n", n=256)).then_inc(loaded, 16)
            sp.wait_ge(loaded, 16 * 7)
            with sp.If(out_of_order(sp)):
                with sp.Fori(0, NB) as b:
                    hold(sp, used, b + 1)
                    sp.dma_start(others[:, :], edges[DST, bass.ds(b * BE, BE)].rearrange("(a n) -> a n", a=1)
                                 .to_broadcast([P, BE])).then_inc(spread, 16)
                sp.wait_ge(placed, 16 * KT)
                sp.dma_start(packed[:, :, :], m.records.rearrange("(q n) f -> q n f", n=256)).then_inc(sorted_rows, 16)
                sp.wait_ge(unpacked, 1)
                sp.dma_start(m.sorted_dst.rearrange("(q n) -> q n", n=256), rows[:, DST, :]).then_inc(sorted_rows, 16)
                sp.wait_ge(sorted_rows, 32)
                neighbours(sp, m.sorted_dst, halo_set)
                sp.wait_ge(halo_set, 32)

        @block.gpsimd
        def _(pool):
            pool.iota(number[:, :], pattern=[[TE, KT]], base=0, channel_multiplier=1,
                      allow_small_or_imprecise_dtypes=True).then_inc(numbered, 1)
            pool.iota(numbers[:, :], pattern=[[1, BE]], base=0, channel_multiplier=0,
                      allow_small_or_imprecise_dtypes=True).then_inc(numbered, 1)
            with pool.If(out_of_order(pool)):
                with pool.Fori(0, KT) as k:
                    hold(pool, staged, k + 1)
                    pool.indirect_dma_start(m.records, bass.IndirectOffsetOnAxis(ap=where[:, 0:1], axis=0),
                                            record[:, :], None, bounds_check=EP - 1, oob_is_err=False)\
                        .then_inc(placed, 16)

        @block.tensor
        def _(pe):
            pe.wait_ge(counted, 1)
            pe.matmul(ps[0][0:1, 0:1], fell[:, :], m.ones[0:QR, 0:1], start=True, stop=True).then_inc(turned, 1)
            with pe.If(out_of_order(pe)):
                pe.wait_ge(counted, 2)
                for f in range(4):
                    for b in range(2):
                        last = pe.transpose(ps[1 + f][:, b * QR:(b + 1) * QR], rowf[:, f, b * TE:(b + 1) * TE],
                                            m.ident[0:QR, 0:QR])
                last.then_inc(turned, 1)

        @block.vector
        def _(v):
            n = [0]

            def link(ins):
                n[0] += 1
                ins.then_inc(vc, 1)
                v.wait_ge(vc, n[0])

            v.memset(halo[:, 257:258], FAR)
            v.memset(halo[:, 0:1], -1).then_inc(prep, 1)
            v.wait_ge(loaded, 16 * 7)
            link(v.tensor_copy(halof[:, :], halo[:, 1:258]))
            link(v.tensor_tensor(falls[:, :], halof[:, 1:257], halof[:, 0:256], ALU.is_lt))
            v.tensor_reduce(fell[:, :], falls[:, :], AX.X, ALU.add).then_inc(counted, 1)
            v.wait_ge(turned, 1)
            v.tensor_scalar(unsorted[:, :], ps[0][0:1, 0:1], 0.0, None, ALU.is_gt).then_inc(flagged, 1)
            with v.If(out_of_order(v)):
                v.tensor_copy(rowf[:, :, :], rows[:, :, :]).then_inc(counted, 1)
                v.wait_ge(turned, 2)
                for f in range(4):
                    v.tensor_copy(col[:, f, :].rearrange("p (q b) -> p b q", b=2),
                                  ps[1 + f][:, 0:2 * QR].rearrange("p (b q) -> p b q", b=2))
                v.wait_ge(numbered, 2)
                v.memset(place[:, :], 0.0)
                v.drain()
                v.tensor_copy(count[:, :], place[:, 0:BT]).then_inc(used, 1)
                wide_others = othersf[:, :].unsqueeze(1).to_broadcast([P, BT, BE])
                wide_numbers = numbers[:, :].unsqueeze(1).to_broadcast([P, BT, BE])
                with v.Fori(0, NB) as b:
                    hold(v, spread, b * 16 + 16)
                    v.tensor_copy(othersf[:, :], others[:, :])
                    v.drain()
                    v.tensor_copy(count[:, :], place[:, 0:BT]).then_inc(used, 1)
                    with v.Fori(0, NB) as own:
                        dst = bc(col[:, DST, bass.ds(own * BT, BT)], BE)
                        v.drain()
                        v.tensor_tensor(less[:, :, :], wide_others, dst, ALU.is_lt)
                        v.tensor_tensor(equal[:, :, :], wide_others, dst, ALU.is_equal)
                        v.tensor_tensor(before[:, :, :], wide_numbers, bc(at(number, own), BE), ALU.is_lt)
                        v.drain()
                        v.tensor_tensor(equal[:, :, :], equal[:, :, :], before[:, :, :], ALU.mult)
                        v.drain()
                        v.tensor_tensor(less[:, :, :], less[:, :, :], equal[:, :, :], ALU.add)
                        v.drain()
                        v.tensor_reduce(count[:, :], less[:, :, :], AX.X, ALU.add)
                        v.drain()
                        v.tensor_tensor(at(place, own), at(place, own), count[:, :], ALU.add)
                    v.drain()
                    v.tensor_scalar(numbers[:, :], numbers[:, :], float(BE), None, ALU.add)
                    v.drain()
                with v.Fori(0, KT) as k:
                    v.tensor_copy(where[:, :], place[:, bass.ds(k, 1)])
                    v.tensor_copy(record[:, :], col[:, :, bass.ds(k, 1)].rearrange("p f o -> p (f o)")).then_inc(staged, 1)
                    hold(v, placed, k * 16 + 16)
                v.wait_ge(sorted_rows, 16)
                v.tensor_copy(rows[:, :, :], packed[:, :, :].rearrange("q n f -> q f n")).then_inc(unpacked, 1)
                v.wait_ge(unpacked, 1)
                v.tensor_copy(halo[:, 1:257], rows[:, DST, :])
                v.drain()


def setup_stage(nc, io, m):
    with ExitStack() as ctx:
        sb = lambda n, s, d=F32: ctx.enter_context(nc.sbuf_tensor("su_" + n, s, d))
        sem = Semaphores(nc, "su_")
        halo, rows = m.halo, m.rows
        rowf = sb("rowf", [QR, 4, 256])
        dstf = sb("dstf", [QR, 258])
        same = sb("same", [QR, 256])
        nxt = sb("nxt", [QR, 256])
        flag = sb("flag", [QR, 2, 256])
        through = sb("through", [QR, 2, 256])
        zero = sb("zero", [QR, 256])
        relid = sb("relid", [QR, R8 + 1, 256])
        cnt = sb("cnt", [QR, 2, R8 + 1, 256])
        ends = sb("ends", [QR, 2, 2, R8 + 1])
        endT = sb("endT", [R8 + 1, 2, 2, QR])
        carryT = sb("carryT", [R8 + 1, 2, QR + 1])
        carry = sb("carry", [QR, 2, R8 + 1])
        field = sb("field", [QR, 6, 256])
        typ = sb("typ", [QR, 3, 256], BF16)
        own = sb("own", [QR, 256])
        wgt = sb("wgt", [QR, 256])
        root_of = sb("root_of", [QR, 256])
        rooted = sem("rooted")
        ps = m.psum
        lin, prep = sem("lin"), sem("prep")
        tr, back, colT, colC, stored = sem("tr"), sem("back"), sem("colT"), sem("colC"), sem("stored")
        wl = sem("wl")
        vc = sem("chain")
        SRC_F, CL_F, LAST_F, DINV_F, T8_F, DST_F = range(6)
        ctx.callback(sem.clear)
        block = ctx.enter_context(nc.Block())

        @block.sync
        def _(sp):
            for dst, src in ((m.w1, io["W1"]), (m.w2, io["W2"]), (m.root, io["root"])):
                sp.dma_start(dst[:, :], src).then_inc(wl, 16)
            sp.dma_start(m.b1[:, :], io["b1"].rearrange("(p n) -> p n", n=1)).then_inc(wl, 16)
            for dst, src in ((m.b2, io["b2"]), (m.bias, io["bias"])):
                sp.dma_start(dst[:, :], src.rearrange("(a n) -> a n", a=1).to_broadcast([P, D])).then_inc(wl, 16)
            hold(sp, lin, 1)
            for f, plane in enumerate((m.same_plane, m.type_plane[R8], m.type_plane[R16])):
                sp.dma_start(plane.rearrange("(q n) -> q n", n=256), typ[:, f, :]).then_inc(stored, 16)
            hold(sp, lin, 2)
            sp.dma_start(m.weight_plane.rearrange("(q n) -> q n", n=256), wgt[:, :]).then_inc(stored, 16)
            hold(sp, stored, 64)
            hold(sp, wl, 96)

        @block.vector
        def _(v):
            n = [0]

            def link(ins):
                n[0] += 1
                ins.then_inc(vc, 1)
                v.wait_ge(vc, n[0])

            v.memset(zero[:, :], 0.0)
            v.memset(carryT[:, :, :], 0.0)
            link(v.memset(relid[:, R8, :], 1.0))
            v.tensor_copy(dstf[:, :], halo[:, :])
            link(v.tensor_copy(rowf[:, :, :], rows[:, :, :]))
            v.tensor_tensor(same[:, :], dstf[:, 1:257], dstf[:, 0:256], ALU.is_equal)
            link(v.tensor_tensor(nxt[:, :], dstf[:, 1:257], dstf[:, 2:258], ALU.is_equal))
            v.tensor_copy(typ[:, 0, :], same[:, :])
            v.tensor_copy(typ[:, 1:3, :], rowf[:, T8:T16 + 1, :]).then_inc(lin, 1)
            v.tensor_copy(flag[:, 0, :], same[:, :])
            v.tensor_copy(flag[:, 1, :], nxt[:, :])
            v.tensor_copy(field[:, SRC_F, :], rowf[:, SRC, :])
            v.tensor_copy(field[:, T8_F, :], rowf[:, T8, :])
            v.tensor_copy(field[:, DST_F, :], rowf[:, DST, :])
            v.tensor_scalar(field[:, CL_F, :], rowf[:, DST, :], float(N - 1), None, ALU.min)
            v.scalar_tensor_tensor(out=field[:, LAST_F, :], in0=nxt[:, :], scalar=float(FAR), in1=rowf[:, DST, :],
                                   op0=ALU.mult, op1=ALU.add)
            for r in range(R8):
                last = v.tensor_scalar(relid[:, r, :], rowf[:, T8, :], float(r), None, ALU.is_equal)
            link(last)
            v.memset(flag[:, 0, 0:1], 0.0)
            link(v.memset(flag[:, 1, 255:256], 0.0))
            v.tensor_tensor_scan(through[:, 0, :], same[:, :], zero[:, :], 1.0, ALU.mult, ALU.max)
            v.tensor_tensor_scan(through[:, 1, ::-1], nxt[:, ::-1], zero[:, :], 1.0, ALU.mult, ALU.max)
            for r in range(R8 + 1):
                v.tensor_tensor_scan(cnt[:, 0, r, :], flag[:, 0, :], relid[:, r, :], 0.0, ALU.mult, ALU.add)
                last = v.tensor_tensor_scan(cnt[:, 1, r, ::-1], flag[:, 1, ::-1], relid[:, r, ::-1], 0.0,
                                            ALU.mult, ALU.add)
            link(last)
            v.tensor_copy(ends[:, 0, 0, :], cnt[:, 0, :, 255])
            v.tensor_copy(ends[:, 1, 0, :], cnt[:, 1, :, 0])
            v.tensor_copy(ends[:, 0, 1, :], through[:, 0, 255:256].to_broadcast([QR, R8 + 1]))
            v.tensor_copy(ends[:, 1, 1, :], through[:, 1, 0:1].to_broadcast([QR, R8 + 1])).then_inc(prep, 1)
            v.wait_ge(tr, 1)
            link(v.tensor_copy(endT[:, :, :, :].rearrange("r a b q -> r (a b q)"), ps[0][0:R8 + 1, 0:4 * QR]))
            v.tensor_tensor_scan(carryT[:, 0, 1:QR + 1], endT[:, 0, 1, :], endT[:, 0, 0, :], 0.0, ALU.mult, ALU.add)
            v.tensor_tensor_scan(carryT[:, 1, QR - 1::-1], endT[:, 1, 1, ::-1], endT[:, 1, 0, ::-1], 0.0,
                                 ALU.mult, ALU.add).then_inc(prep, 1)
            v.wait_ge(back, 1)
            link(v.tensor_copy(carry[:, :, :].rearrange("q a r -> q (a r)"), ps[1][0:QR, 0:2 * (R8 + 1)]))
            for d in range(2):
                for r in range(R8 + 1):
                    last = v.scalar_tensor_tensor(out=cnt[:, d, r, :], in0=through[:, d, :], scalar=carry[:, d, r:r + 1],
                                                  in1=cnt[:, d, r, :], op0=ALU.mult, op1=ALU.add)
            link(last)
            v.tensor_tensor(cnt[:, 0, :, :], cnt[:, 0, :, :], cnt[:, 1, :, :], ALU.add).then_inc(prep, 1)
            v.wait_ge(prep, 3)
            v.wait_ge(rooted, 1)
            v.reciprocal(field[:, DINV_F, :], root_of[:, :])
            link(v.tensor_tensor(cnt[:, 1, 0:R8, :], cnt[:, 0, 0:R8, :], relid[:, 0:R8, :], ALU.mult))
            link(v.tensor_reduce(own[:, :], cnt[:, 1, 0:R8, :].rearrange("q r n -> q n r"), AX.X, ALU.add))
            link(v.tensor_scalar(own[:, :], own[:, :], -1.0, None, ALU.add))
            v.reciprocal(wgt[:, :], own[:, :]).then_inc(lin, 1)
            for f, col in ((SRC_F, m.src_col), (CL_F, m.dst_col), (LAST_F, m.last_col),
                           (DINV_F, m.dinv_col), (T8_F, m.type_col), (DST_F, m.dstraw_col)):
                v.wait_ge(colT, f + 1)
                v.tensor_copy(col[:, :].rearrange("p (q b) -> p b q", b=2),
                              ps[2 + f][:, 0:2 * QR].rearrange("p (b q) -> p b q", b=2)).then_inc(colC, 1)
            v.wait_ge(colC, 6)
            link(v.tensor_copy(m.dst_int[:, :], m.dstraw_col[:, :]))
            v.tensor_scalar(m.hi_int[:, :], m.dst_int[:, :], 7, None, ALU.arith_shift_right)
            link(v.tensor_scalar(m.lo_int[:, :], m.dst_int[:, :], 127, None, ALU.bitwise_and))
            v.tensor_copy(m.hi_col[:, :], m.hi_int[:, :])
            v.tensor_copy(m.lo_col[:, :], m.lo_int[:, :])

        @block.scalar
        def _(act):
            act.wait_ge(prep, 3)
            act.activation(root_of[:, :], cnt[:, 0, R8, :], ACT.Sqrt).then_inc(rooted, 1)

        @block.tensor
        def _(pe):
            pe.wait_ge(prep, 1)
            for i in range(4):
                last = pe.transpose(ps[0][0:R8 + 1, i * QR:(i + 1) * QR], ends[:, i // 2, i % 2, :], m.ident[0:QR, 0:QR])
            last.then_inc(tr, 1)
            pe.wait_ge(prep, 2)
            pe.transpose(ps[1][0:QR, 0:R8 + 1], carryT[:, 0, 0:QR], m.ident[0:R8 + 1, 0:R8 + 1])
            pe.transpose(ps[1][0:QR, R8 + 1:2 * (R8 + 1)], carryT[:, 1, 1:QR + 1],
                         m.ident[0:R8 + 1, 0:R8 + 1]).then_inc(back, 1)
            pe.wait_ge(lin, 2)
            for f in range(6):
                for b in range(2):
                    last = pe.transpose(ps[2 + f][:, b * QR:(b + 1) * QR], field[:, f, b * TE:(b + 1) * TE],
                                        m.ident[0:QR, 0:QR])
                last.then_inc(colT, 1)


def degree_stage(nc, io, m):
    with ExitStack() as ctx:
        sb = lambda n, s, d=F32: ctx.enter_context(nc.sbuf_tensor("dg_" + n, s, d))
        sem = Semaphores(nc, "dg_")
        lo1 = sb("lo1", [P, 2, P], BF16)
        hi1 = sb("hi1", [P, 2, RPP], BF16)
        cnt = sb("cnt", [P, RPP])
        turned = sb("turned", [RPP // 4, 4, P])
        root_of = sb("root_of", [P, RPP])
        rooted = sem("rooted")
        made, used, copied, tr, out, stored = (sem(x) for x in ("made", "used", "copied", "tr", "out", "stored"))
        ps = m.psum
        ctx.callback(sem.clear)
        block = ctx.enter_context(nc.Block())
        HB = RPP // 4

        @block.vector
        def _(v):
            def body(k, q):
                if not static(k) or k >= 2:
                    v.wait_ge(used, k - 1)
                v.tensor_scalar(lo1[:, q, :], m.iota[:, 0:P], m.lo_col[:, bass.ds(k, 1)], None, ALU.is_equal)
                v.tensor_scalar(hi1[:, q, :], m.iota[:, :], m.hi_col[:, bass.ds(k, 1)], None, ALU.is_equal)\
                    .then_inc(made, 1)
            body(0, 0)
            body(1, 1)
            with v.Fori(1, KT // 2) as j:
                body(j * 2, 0)
                body(j * 2 + 1, 1)
            v.wait_ge(rooted, 1)
            v.reciprocal(cnt[:, :], root_of[:, :]).then_inc(copied, 1)
            v.wait_ge(tr, 1)
            v.tensor_copy(turned[:, :, :].rearrange("p a b -> p (a b)"), ps[1][0:HB, 0:4 * P]).then_inc(out, 1)

        @block.scalar
        def _(act):
            act.wait_ge(used, KT)
            act.activation(root_of[:, :], ps[0][:, 0:RPP], ACT.Sqrt, bias=m.ones[:, 0:1]).then_inc(rooted, 1)

        @block.tensor
        def _(pe):
            def body(k, q, first=False, last=False):
                pe.wait_ge(made, k + 1)
                mm = pe.matmul(ps[0][:, 0:RPP], lo1[:, q, :], hi1[:, q, :], start=first, stop=last,
                               skip_group_check=True)
                mm.then_inc(used, 1)
            body(0, 0, first=True)
            body(1, 1)
            with pe.Fori(1, KT // 2 - 1) as j:
                body(j * 2, 0)
                body(j * 2 + 1, 1)
            body(KT - 2, 0)
            body(KT - 1, 1, last=True)
            pe.wait_ge(copied, 1)
            for g in range(4):
                last = pe.transpose(ps[1][0:HB, g * P:(g + 1) * P], cnt[:, g * HB:(g + 1) * HB], m.ident[:, :])
            last.then_inc(tr, 1)

        @block.sync
        def _(sp):
            hold(sp, out, 1)
            sp.dma_start(m.dinv_table.rearrange("(g p l) o -> p g (l o)", g=4, l=P), turned[:, :, :]).then_inc(stored, 16)
            hold(sp, stored, 16)


def row_stats(v, z, norm, chain, base):
    stats, mv = norm
    for j in range(BT):
        last = v.bn_stats(stats[:, j, :], z[:, j, :])
    last.then_inc(chain, 1)
    hold(v, chain, base + 1)
    for j in range(BT):
        last = v.bn_aggr(mv[:, j, :], stats[:, j, :])
    return last


def apply_norm(v, out, z, mv, rstd):
    for j in range(BT):
        last = v.tensor_scalar(out[:, j, :], z[:, j, :], mv[:, j, 0:1], rstd[:, j:j + 1], ALU.subtract, ALU.mult)
    return last


def prefill_stage(nc, io, m):
    with ExitStack() as ctx:
        sb = lambda n, s, d=F32: ctx.enter_context(nc.sbuf_tensor("pf_" + n, s, d))
        sem = Semaphores(nc, "pf_")
        pair = lambda n: [sem(n + "_even"), sem(n + "_odd")]
        xc = sb("xc", [P, 2, BT, D])
        xT = sb("xT", [P, 2, BE])
        hT = sb("hT", [P, 2, BE])
        g1 = sb("g1", [P, 2, BT, D])
        z1 = sb("z1", [P, BT, D])
        x1 = sb("x1", [P, 2, BT, D])
        xb = sb("xb", [P, BT, D])
        x1b = sb("x1b", [P, BT, D])
        x1T = sb("x1T", [P, 2, BE])
        z2 = sb("z2", [P, BT, D])
        x2 = sb("x2", [P, 2, BT, D])
        x3 = sb("x3", [P, 2, BT, D])
        x4 = sb("x4", [P, 2, BT, D])
        norm1 = (sb("st1", [P, BT, 6]), sb("mv1", [P, BT, 2]))
        norm2 = (sb("st2", [P, BT, 6]), sb("mv2", [P, BT, 2]))
        sd1, rs1 = sb("sd1", [P, BT]), sb("rs1", [P, BT])
        var, sd, rs = (sb(n, [P, 3, BT]) for n in ("var", "sd", "rs"))
        ratio = sb("ratio", [P, 2, 2, BT])
        gi = sb("gi", [P, 2, 2, 2], I32)
        xs = sb("xs", [P, 2, 2, D])
        ds = sb("ds", [P, 2, 2])
        loaded, gathered = pair("loaded"), sem.of_pool("gathered")
        g1_stored, x1_stored, x2_stored, x3_stored, x4_stored = (
            pair(n) for n in ("g1_stored", "x1_stored", "x2_stored", "x3_stored", "x4_stored"))
        x_turned, xT_copied, xw1_done, hT_ready, hw2_done, g1_ready, z1_ready = (
            sem(n) for n in ("x_turned", "xT_copied", "xw1_done", "hT_ready", "hw2_done", "g1_ready", "z1_ready"))
        x1_ready, x1_turned, x1T_copied, root_done, x2_ready, x3_ready, x4_ready = (
            sem(n) for n in ("x1_ready", "x1_turned", "x1T_copied", "root_done", "x2_ready", "x3_ready", "x4_ready"))
        chain1, chain2, idx_ready, kept = (sem(n) for n in ("chain1", "chain2", "idx_ready", "kept"))
        var1_ready, sd1_ready, var_ready, sd_ready, ratio_ready = (
            sem(n) for n in ("var1_ready", "sd1_ready", "var_ready", "sd_ready", "ratio_ready"))
        T, H, U, Y = m.psum[0:2], m.psum[2:4], m.psum[4:6], m.psum[6:8]
        rows_of = lambda t, c: t.rearrange("(p r) d -> p r d", p=P)[:, bass.ds(c * BT, BT), :]
        C1, C2 = 3, 7
        END = NCH - 1
        flat = lambda t: t.rearrange("p b d -> p (b d)")
        wide = lambda t: t.rearrange("p (b d) -> p b d", d=D)
        ctx.callback(sem.clear)
        block = ctx.enter_context(nc.Block())

        def chunks(eng, body, first, last):
            for c in range(first, 6):
                body(c, c % 2)
            with eng.Fori(3, NCH // 2) as j:
                body(j * 2, 0)
                body(j * 2 + 1, 1)
            for c in range(NCH, last + 1):
                body(c, c % 2)

        @block.sync
        def _(sp):
            def store(c, ready, name, buf, stored):
                if runs(c, 0, END):
                    q = store.parity
                    hold(sp, ready, c + 1)
                    sp.dma_start(rows_of(m.tables[name], c), buf[:, q]).then_inc(stored[q], 16)

            def body(c, q):
                if runs(c, 0, END):
                    if runs(c, 2, END):
                        hold(sp, z1_ready, c - 1)
                    sp.dma_start(xc[:, q], rows_of(io["x"], c)).then_inc(loaded[q], 16)
                store.parity = q
                store(c - 2, g1_ready, "G1", g1, g1_stored)
                store(c - 2, x1_ready, "X1", x1, x1_stored)
                store.parity = 1 - q
                store(c - 3, x2_ready, "X2", x2, x2_stored)
                store(c - 3, x4_ready, "OUT", x4, x4_stored)
                store.parity = q
                store(c - 4, x3_ready, "X3", x3, x3_stored)
            chunks(sp, body, 0, NCH + 3)
            for stored in (g1_stored, x1_stored, x2_stored, x3_stored, x4_stored):
                for s in stored:
                    hold(sp, s, NCH // 2 * 16)

        @block.gpsimd
        def _(pool):
            def body(c, q):
                if not runs(c, 0, END):
                    return
                hold(pool, idx_ready, c + 1)
                if runs(c, 2, END):
                    hold(pool, kept, c - 1)
                for t in range(2):
                    pool.indirect_dma_start(xs[:, q, t, :], None, io["x"],
                                            bass.IndirectOffsetOnAxis(ap=gi[:, q, 0, t:t + 1], axis=0))\
                        .then_inc(gathered[q], 16)
                    pool.indirect_dma_start(ds[:, q, t:t + 1], None, m.dinv_table,
                                            bass.IndirectOffsetOnAxis(ap=gi[:, q, 1, t:t + 1], axis=0))\
                        .then_inc(gathered[q], 16)
            chunks(pool, body, 0, END)

        @block.tensor
        def _(pe):
            def body(c, q):
                o = 1 - q
                if runs(c, 0, END):
                    pe.wait_ge(loaded[q], of_slot(c, q, 16))
                    if runs(c, 2, END):
                        pe.wait_ge(xT_copied, c - 1)
                    for j in range(BT):
                        last = pe.transpose(T[q][:, j * D:(j + 1) * D], xc[:, q, j, :], m.ident[:, :])
                    last.then_inc(x_turned, 1)
                    pe.wait_ge(xT_copied, c + 1)
                    if runs(c, 2, END):
                        pe.wait_ge(hT_ready, c - 1)
                    pe.matmul(H[q][:, :], m.w1[:, :], xT[:, q, :], start=True, stop=True).then_inc(xw1_done, 1)
                p = c - 1
                if runs(p, 0, END):
                    pe.wait_ge(hT_ready, p + 1)
                    if runs(p, 2, END):
                        pe.wait_ge(g1_ready, p - 1)
                    for j in range(BT):
                        last = pe.matmul(U[o][:, j * D:(j + 1) * D], hT[:, o, j * D:(j + 1) * D], m.w2[:, :],
                                         start=True, stop=True)
                    last.then_inc(hw2_done, 1)
                p = c - 2
                if runs(p, 0, END):
                    pe.wait_ge(x1_ready, p + 1)
                    if runs(p, 2, END):
                        pe.wait_ge(chain2, (p - 2) * C2 + 2)
                    for j in range(BT):
                        last = pe.transpose(Y[q][:, j * D:(j + 1) * D], x1[:, q, j, :], m.ident[:, :])
                    last.then_inc(x1_turned, 1)
                    pe.wait_ge(x1T_copied, p + 1)
                    for j in range(BT):
                        last = pe.matmul(Y[q][:, j * D:(j + 1) * D], x1T[:, q, j * D:(j + 1) * D], m.root[:, :],
                                         start=True, stop=True)
                    last.then_inc(root_done, 1)
            chunks(pe, body, 0, NCH + 1)

        @block.scalar
        def _(act):
            def body(c, q):
                o = 1 - q
                if runs(c, 0, END):
                    if runs(c, 2, END):
                        act.wait_ge(gathered[q], of_slot(c - 2, q, 64))
                    act.activation(gi[:, q, 0, :], at(m.dst_col, c, 2), ACT.Copy)
                    act.activation(gi[:, q, 1, :], at(m.src_col, c, 2), ACT.Copy).then_inc(idx_ready, 1)
                    act.wait_ge(x_turned, c + 1)
                    if runs(c, 2, END):
                        act.wait_ge(xw1_done, c - 1)
                    act.activation(xT[:, q, :], T[q][:, :], ACT.Copy).then_inc(xT_copied, 1)
                p = c - 2
                if runs(p, 0, END):
                    act.wait_ge(x1_turned, p + 1)
                    if runs(p, 2, END):
                        act.wait_ge(root_done, p - 1)
                    act.activation(x1T[:, q, :], Y[q][:, :], ACT.Copy).then_inc(x1T_copied, 1)
                p = c - 3
                if runs(p, 0, END):
                    act.wait_ge(x2_ready, p + 1)
                    act.wait_ge(ratio_ready, p + 1)
                    if runs(p, 2, END):
                        act.wait_ge(x3_stored[o], of_slot(p - 2, o, 16))
                    for j in range(BT):
                        last = act.activation(x3[:, o, j, :], x2[:, o, j, :], ACT.Copy, scale=ratio[:, o, 0, j:j + 1])
                    last.then_inc(x3_ready, 1)

            def relu(c, q):
                if runs(c, 0, END):
                    act.wait_ge(xw1_done, c + 1)
                    if runs(c, 2, END):
                        act.wait_ge(hw2_done, c - 1)
                    act.activation(hT[:, q, :], H[q][:, :], ACT.Relu, bias=m.b1[:, 0:1]).then_inc(hT_ready, 1)

            def keep(p, o):
                if runs(p, 0, END):
                    act.wait_ge(hw2_done, p + 1)
                    if runs(p, 2, END):
                        act.wait_ge(g1_stored[o], of_slot(p - 2, o, 16))
                        act.wait_ge(z1_ready, p - 1)
                    act.activation(flat(g1[:, o]), U[o][:, :], ACT.Copy).then_inc(g1_ready, 1)
                    act.wait_ge(gathered[o], of_slot(p, o, 64))
                    act.activation(m.xd[:, bass.ds(p * (2 * D), 2 * D)], flat(xs[:, o]), ACT.Copy)
                    act.activation(at(m.ds_col, p, 2), ds[:, o, :], ACT.Copy).then_inc(kept, 1)

            def roots(c):
                if runs(c - 1, 0, END):
                    act.wait_ge(var1_ready, c)
                    if runs(c - 1, 1, END):
                        act.wait_ge(chain1, (c - 2) * C1 + 3)
                    act.activation(sd1[:, :], norm1[1][:, :, 1], ACT.Sqrt, bias=m.eps[:, 0:1]).then_inc(sd1_ready, 1)
                if runs(c - 2, 0, END):
                    act.wait_ge(var_ready, c - 1)
                    if runs(c - 2, 1, END):
                        act.wait_ge(ratio_ready, c - 2)
                    act.activation(sd[:, :, :], var[:, :, :], ACT.Sqrt).then_inc(sd_ready, 1)

            def whole(c, q):
                body(c, q)
                relu(c, q)
                keep(c - 1, 1 - q)
                roots(c)
            chunks(act, whole, 0, NCH + 2)

        @block.vector
        def _(v):
            def layer0(p, q):
                if not runs(p, 0, END):
                    return
                base = p * C1
                v.wait_ge(loaded[q], of_slot(p, q, 16))
                v.tensor_tensor(xb[:, :, :], xc[:, q], m.b2_rows, ALU.add).then_inc(chain1, 1)
                v.wait_ge(chain1, base + 1)
                v.wait_ge(g1_ready, p + 1)
                v.tensor_tensor(z1[:, :, :], g1[:, q], xb[:, :, :], ALU.add).then_inc(z1_ready, 1)
                v.wait_ge(z1_ready, p + 1)
                row_stats(v, z1, norm1, chain1, base + 1).then_inc(var1_ready, 1)

            def layer1(p, q):
                if not runs(p, 0, END):
                    return
                base = p * C2
                v.tensor_tensor(x1b[:, :, :], x1[:, q], m.bias_rows, ALU.add).then_inc(chain2, 1)
                v.wait_ge(chain2, base + 1)
                v.wait_ge(root_done, p + 1)
                v.tensor_tensor(z2[:, :, :], wide(Y[q][:, :]), x1b[:, :, :], ALU.add).then_inc(chain2, 1)
                v.wait_ge(chain2, base + 2)
                row_stats(v, z2, norm2, chain2, base + 2).then_inc(chain2, 1)
                v.wait_ge(chain2, base + 4)
                mv = norm2[1]
                v.tensor_scalar(var[:, 0, :], mv[:, :, 1], EPS, None, ALU.add).then_inc(chain2, 1)
                for i in range(1, 3):
                    v.wait_ge(chain2, base + 4 + i)
                    last = v.scalar_tensor_tensor(out=var[:, i, :], in0=var[:, i - 1, :], scalar=EPS, in1=mv[:, :, 1],
                                                  op0=ALU.mult, op1=ALU.add)
                    last.then_inc(chain2 if i == 1 else var_ready, 1)

            def apply0(p, q):
                if not runs(p, 0, END):
                    return
                v.wait_ge(sd1_ready, p + 1)
                v.reciprocal(rs1[:, :], sd1[:, :]).then_inc(chain1, 1)
                v.wait_ge(chain1, p * C1 + 3)
                if runs(p, 2, END):
                    v.wait_ge(x1_stored[q], of_slot(p - 2, q, 16))
                apply_norm(v, x1[:, q], z1, norm1[1], rs1).then_inc(x1_ready, 1)
                v.wait_ge(x1_ready, p + 1)

            def apply1(p, q):
                if not runs(p, 0, END):
                    return
                v.wait_ge(sd_ready, p + 1)
                v.reciprocal(rs[:, :, :], sd[:, :, :]).then_inc(chain2, 1)
                v.wait_ge(chain2, p * C2 + 7)
                if runs(p, 2, END):
                    v.wait_ge(x3_ready, p - 1)
                    v.wait_ge(x2_stored[q], of_slot(p - 2, q, 16))
                v.tensor_tensor(ratio[:, q], rs[:, 1:3, :], sd[:, 0, :].unsqueeze(1).to_broadcast([P, 2, BT]), ALU.mult)\
                    .then_inc(ratio_ready, 1)
                apply_norm(v, x2[:, q], z2, norm2[1], rs[:, 0, :]).then_inc(x2_ready, 1)
                v.wait_ge(x2_ready, p + 1)
                v.wait_ge(ratio_ready, p + 1)
                if runs(p, 2, END):
                    v.wait_ge(x4_stored[q], of_slot(p - 2, q, 16))
                v.tensor_tensor(x4[:, q], x2[:, q], bc(ratio[:, q, 1, :], D), ALU.mult).then_inc(x4_ready, 1)

            def body(c, q):
                layer0(c - 1, 1 - q)
                layer1(c - 2, q)
                apply0(c - 1, 1 - q)
                apply1(c - 2, q)
            chunks(v, body, 0, NCH + 1)


CONV1, CONV2, MEAN, ATTEND, SUM = "c1", "c2", "mean", "att", "sum"


def edge_stage(nc, io, m, kind, source, out, weights=None, n_rel=0):
    conv = kind in (CONV1, CONV2)
    lag = 4 if kind == CONV1 else 3
    with ExitStack() as ctx:
        sb = lambda n, s, d=F32: ctx.enter_context(nc.sbuf_tensor(f"{kind}_{n}", s, d))
        sem = Semaphores(nc, f"{kind}_")
        pair = lambda n: [sem(n + "_even"), sem(n + "_odd")]
        flat = lambda t: t.rearrange("p b d -> p (b d)")
        wide = lambda t: t.rearrange("p (b d) -> p b d", d=D)
        gi = sb("gi", [P, 2, BT], I32)
        rows = sb("rows", [P, 2, BT, D])
        scaled = sb("scaled", [P, 2, BT, D]) if kind == CONV1 else rows
        same = sb("same", [P, 2, BE], BF16)
        typ = sb("typ", [P, 2, BE], BF16)
        wgt = sb("wgt", [P, 2, BE])
        col = sb("col", [P, 2, BE])
        masked = sb("masked", [P, 4, BE])
        run = sb("run", [P, 2, BE])
        t1, t2, t3, t4, z, y = (sb(n, [P, BT, D]) for n in ("t1", "t2", "t3", "t4", "z", "y"))
        yT, hT = sb("yT", [P, BE]), sb("hT", [P, BE])
        norm = (sb("st", [P, BT, 6]), sb("mv", [P, BT, 2]))
        sd, rs = sb("sd", [P, BT]), sb("rs", [P, BT])
        new = sb("new", [P, 2, BT, D])
        si = sb("si", [P, 2, BT], I32)
        w = sb("w", [P, n_rel, D]) if n_rel else None
        w_loaded = sem("w_loaded")
        gathered, scattered = sem.of_pool("gathered"), sem.of_pool("scattered")
        same_loaded, typ_loaded, wgt_loaded, col_loaded = (
            pair(n) for n in ("same_loaded", "typ_loaded", "wgt_loaded", "col_loaded"))
        idx_ready, scaled_ready, turned, col_ready, mask_ready, mask_used, related, scanned = (
            sem(n) for n in ("idx_ready", "scaled_ready", "turned", "col_ready", "mask_ready", "mask_used",
                             "related", "scanned"))
        rows_back, y_ready, y_turned, yT_copied, yw1_done, hT_ready, post_done, new_ready, xd_ready = (
            sem(n) for n in ("rows_back", "y_ready", "y_turned", "yT_copied", "yw1_done", "hT_ready",
                             "post_done", "new_ready", "xd_ready"))
        chain, chain2, si_ready = sem("chain"), sem("chain2"), sem("si_ready")
        var_ready, sd_ready = sem("var_ready"), sem("sd_ready")
        steps = {CONV1: 2, CONV2: 4}.get(kind, 3)
        sums_used = {CONV1: 2}.get(kind, 1)
        T, H, B, S = m.psum[0:2], m.psum[2:4], m.psum[4:6], m.psum[6:8]
        E2 = NB - 1
        xd_at = lambda s: m.xd[:, bass.ds(s * BE, BE)]
        dinv = lambda s: bc(at(m.dinv_col, s), D)
        ctx.callback(sem.clear)
        block = ctx.enter_context(nc.Block())
        go = lambda eng, body: pipeline(eng, body, -2, NB + 3, 2, 4)

        @block.sync
        def _(sp):
            if n_rel:
                sp.dma_start(w[:, :, :], weights.rearrange("r i o -> i r o")).then_inc(w_loaded, 16)

            def spread(plane, s):
                return plane[bass.ds(s * BE, BE)].rearrange("(a n) -> a n", a=1).to_broadcast([P, BE])

            def body(b, q):
                s = b + 2
                if runs(s, 0, E2):
                    if n_rel:
                        if runs(s, 2):
                            hold(sp, mask_ready, (s - 1) * n_rel)
                        sp.dma_start(typ[:, q, :], spread(m.type_plane[n_rel], s)).then_inc(typ_loaded[q], 16)
                    if kind in (MEAN, ATTEND):
                        if runs(s, 2):
                            hold(sp, col_ready, s - 1)
                        plane = m.weight_plane if kind == MEAN else m.alpha_plane
                        sp.dma_start(wgt[:, q, :], spread(plane, s)).then_inc(wgt_loaded[q], 16)
                    if kind == ATTEND:
                        sp.dma_start(flat(rows[:, q]), m.message[:, bass.ds(s * BE, BE)]).then_inc(col_loaded[q], 16)
                s = b + 1
                if runs(s, 0, E2):
                    if runs(s, 2):
                        hold(sp, scanned, s - 1)
                    sp.dma_start(same[:, 1 - q, :], spread(m.same_plane, s)).then_inc(same_loaded[1 - q], 16)
            go(sp, body)

        @block.gpsimd
        def _(pool):
            def body(b, q):
                s = b + 2
                if kind != ATTEND and runs(s, 0, E2):
                    hold(pool, idx_ready, s + 1)
                    if runs(s, 2):
                        hold(pool, scaled_ready if kind == CONV1 else turned, s - 1)
                    for j in range(BT):
                        pool.indirect_dma_start(rows[:, q, j, :], None, source,
                                                bass.IndirectOffsetOnAxis(ap=gi[:, q, j:j + 1], axis=0))\
                            .then_inc(gathered[q], 16)
                s = b - lag
                qs = (q + lag) % 2
                if runs(s, 0, E2):
                    hold(pool, new_ready, s + 1)
                    for j in range(BT):
                        pool.indirect_dma_start(out, bass.IndirectOffsetOnAxis(ap=si[:, qs, j:j + 1], axis=0),
                                                new[:, qs, j, :], None, bounds_check=NP - 1, oob_is_err=False)\
                            .then_inc(scattered[qs], 16)
            go(pool, body)
            for q in range(2):
                hold(pool, scattered[q], of_slot(E2 - (E2 - q) % 2, q, 16 * BT))

        @block.scalar
        def _(act):
            def body(b, q):
                o = 1 - q
                s = b + 2
                if kind != ATTEND and runs(s, 0, E2):
                    if runs(s, 2):
                        act.wait_ge(gathered[q], of_slot(s - 2, q, 16 * BT))
                    act.activation(gi[:, q, :], at(m.src_col, s), ACT.Copy).then_inc(idx_ready, 1)
                s = b + 1
                if kind == CONV1 and runs(s, 0, E2):
                    act.wait_ge(gathered[o], of_slot(s, o, 16 * BT))
                    if runs(s, 2):
                        act.wait_ge(turned, s - 1)
                    for j in range(BT):
                        last = act.activation(scaled[:, o, j, :], rows[:, o, j, :], ACT.Copy,
                                              scale=m.ds_col[:, bass.ds(s * BT + j, 1)])
                    last.then_inc(scaled_ready, 1)
                if kind == SUM and runs(s, 0, E2):
                    act.wait_ge(turned, s + 1)
                    if runs(s, 2):
                        act.wait_ge(mask_ready, (s - 1) * n_rel)
                    act.activation(col[:, o, :], T[o][:, :], ACT.Copy).then_inc(col_ready, 1)
                s = b - 2
                if kind != CONV1 and runs(s, 0, E2):
                    act.wait_ge(var_ready, s + 1)
                    if runs(s, 1):
                        act.wait_ge(chain, s * steps)
                    act.activation(sd[:, :], norm[1][:, :, 1], ACT.Sqrt, bias=m.eps[:, 0:1]).then_inc(sd_ready, 1)
                if conv and runs(s, 0, E2):
                    act.wait_ge(y_turned, s + 1)
                    if runs(s, 1):
                        act.wait_ge(post_done, s)
                    act.activation(yT[:, :], S[0][:, :], ACT.Copy).then_inc(yT_copied, 1)
                    if kind == CONV1:
                        act.wait_ge(yw1_done, s + 1)
                        act.activation(hT[:, :], S[1][:, :], ACT.Relu, bias=m.b1[:, 0:1]).then_inc(hT_ready, 1)
            go(act, body)

        @block.tensor
        def _(pe):
            if n_rel:
                pe.wait_ge(w_loaded, 16)

            def body(b, q):
                o = 1 - q
                s = b + 1
                if kind != ATTEND and runs(s, 0, E2):
                    if kind == CONV1:
                        pe.wait_ge(scaled_ready, s + 1)
                    else:
                        pe.wait_ge(gathered[o], of_slot(s, o, 16 * BT))
                    if runs(s, 2):
                        pe.wait_ge(scanned if conv else col_ready, s - 1)
                    for j in range(BT):
                        last = pe.transpose(T[o][:, j * TE:(j + 1) * TE], scaled[:, o, j, :], m.ident[:, :])
                    last.then_inc(turned, 1)
                s = b
                if n_rel and runs(s, 0, E2):
                    if runs(s, 2):
                        pe.wait_ge(scanned, s - 1)
                    for r in range(n_rel):
                        pe.wait_ge(mask_ready, s * n_rel + r + 1)
                        mm = pe.matmul(H[q][:, :], w[:, r, :], masked[:, r % 4, :], start=(r == 0), stop=(r == n_rel - 1))
                        mm.then_inc(mask_used, 1)
                s = b - 1
                if runs(s, 0, E2):
                    pe.wait_ge(scanned, s + 1)
                    if runs(s, 2):
                        pe.wait_ge(chain, (s - 2) * steps + sums_used)
                    for j in range(BT):
                        last = pe.transpose(B[o][:, j * D:(j + 1) * D], run[:, o, j * TE:(j + 1) * TE], m.ident[:, :])
                    last.then_inc(rows_back, 1)
                s = b - 2
                if conv and runs(s, 0, E2):
                    pe.wait_ge(y_ready if kind == CONV1 else new_ready, s + 1)
                    y_rows = y if kind == CONV1 else new[:, q]
                    if runs(s, 1):
                        pe.wait_ge(xd_ready, s)
                    for j in range(BT):
                        last = pe.transpose(S[0][:, j * TE:(j + 1) * TE], y_rows[:, j, :], m.ident[:, :])
                    last.then_inc(y_turned, 1)
                    pe.wait_ge(yT_copied, s + 1)
                    if kind == CONV1:
                        pe.matmul(S[1][:, :], m.w1[:, :], yT[:, :], start=True, stop=True).then_inc(yw1_done, 1)
                        pe.wait_ge(hT_ready, s + 1)
                    lhs, rhs = (hT, m.w2) if kind == CONV1 else (yT, m.root)
                    for j in range(BT):
                        last = pe.matmul(S[0][:, j * D:(j + 1) * D], lhs[:, j * TE:(j + 1) * TE], rhs[:, :],
                                         start=True, stop=True)
                    last.then_inc(post_done, 1)
            go(pe, body)

        @block.vector
        def _(v):
            def relate(s, q):
                if not runs(s, 0, E2):
                    return
                if kind == MEAN:
                    v.wait_ge(turned, s + 1)
                    v.wait_ge(wgt_loaded[q], of_slot(s, q, 16))
                    v.tensor_tensor(col[:, q, :], T[q][:, :], wgt[:, q, :], ALU.mult).then_inc(col_ready, 1)
                if kind == ATTEND:
                    v.wait_ge(wgt_loaded[q], of_slot(s, q, 16))
                    v.wait_ge(col_loaded[q], of_slot(s, q, 16))
                    if runs(s, 2):
                        v.wait_ge(scanned, s - 1)
                    v.tensor_tensor(col[:, q, :], flat(rows[:, q]), wgt[:, q, :], ALU.mult).then_inc(col_ready, 1)
                if n_rel:
                    v.wait_ge(col_ready, s + 1)
                    v.wait_ge(typ_loaded[q], of_slot(s, q, 16))
                    for r in range(n_rel):
                        if r >= 4 or runs(s, 1):
                            v.wait_ge(mask_used, s * n_rel + r - 3)
                        v.scalar_tensor_tensor(out=masked[:, r % 4, :], in0=typ[:, q, :], scalar=float(r),
                                               in1=col[:, q, :], op0=ALU.is_equal, op1=ALU.mult).then_inc(mask_ready, 1)

            def scan(s, q):
                if not runs(s, 0, E2):
                    return
                v.wait_ge(same_loaded[q], of_slot(s, q, 16))
                if n_rel:
                    v.wait_ge(mask_used, (s + 1) * n_rel)
                    new_part = H[q][:, :]
                elif conv:
                    v.wait_ge(turned, s + 1)
                    new_part = T[q][:, :]
                else:
                    v.wait_ge(col_ready, s + 1)
                    new_part = col[:, q, :]
                if runs(s, 2):
                    v.wait_ge(rows_back, s - 1)
                if runs(s, 1):
                    v.wait_ge(scanned, s)
                start = 0.0 if static(s) and s == 0 else run[:, 1 - q, BE - 1:BE]
                v.tensor_tensor_scan(run[:, q, :], same[:, q, :], new_part, start, ALU.mult, ALU.add)\
                    .then_inc(scanned, 1)

            def destinations(s, q):
                if runs(s, 2):
                    hold(v, scattered[q], of_slot(s - 2, q, 16 * BT))
                v.tensor_copy(si[:, q, :], at(m.last_col, s)).then_inc(si_ready, 1)

            def update(s, q):
                if not runs(s, 0, E2):
                    return
                base = s * steps
                if runs(s, 1):
                    v.wait_ge(y_ready if kind == CONV1 else new_ready, s)
                    v.wait_ge(chain, base)
                if kind == CONV1:
                    v.tensor_tensor(t1[:, :, :], wide(xd_at(s)), dinv(s), ALU.mult).then_inc(chain, 1)
                    v.wait_ge(rows_back, s + 1)
                    v.wait_ge(chain, base + 1)
                    v.tensor_tensor(t2[:, :, :], wide(B[q][:, :]), t1[:, :, :], ALU.add).then_inc(chain, 1)
                    v.wait_ge(chain, base + 2)
                    if runs(s, 1):
                        v.wait_ge(y_turned, s)
                    v.tensor_tensor(y[:, :, :], t2[:, :, :], dinv(s), ALU.mult).then_inc(y_ready, 1)
                    return
                v.wait_ge(rows_back, s + 1)
                if kind == CONV2:
                    v.tensor_tensor(t1[:, :, :], wide(B[q][:, :]), dinv(s), ALU.mult).then_inc(chain, 1)
                    v.wait_ge(chain, base + 1)
                    v.tensor_tensor(z[:, :, :], t1[:, :, :], wide(xd_at(s)), ALU.add).then_inc(chain, 1)
                elif kind == SUM:
                    v.scalar_tensor_tensor(out=flat(z[:, :, :]), in0=B[q][:, :], scalar=0.0, in1=xd_at(s),
                                           op0=ALU.max, op1=ALU.add).then_inc(chain, 1)
                else:
                    v.tensor_tensor(z[:, :, :], wide(B[q][:, :]), wide(xd_at(s)), ALU.add).then_inc(chain, 1)
                v.wait_ge(chain, base + steps - 2)
                row_stats(v, z, norm, chain, base + steps - 2).then_inc(var_ready, 1)

            def normalise(s, q):
                if kind == CONV1 or not runs(s, 0, E2):
                    return
                destinations(s, q)
                v.wait_ge(sd_ready, s + 1)
                v.reciprocal(rs[:, :], sd[:, :]).then_inc(chain, 1)
                v.wait_ge(chain, (s + 1) * steps)
                v.wait_ge(si_ready, s + 1)
                apply_norm(v, new[:, q], z, norm[1], rs).then_inc(new_ready, 1)
                if kind in (MEAN, ATTEND):
                    hold(v, new_ready, s + 1)
                    v.tensor_copy(wide(xd_at(s)), new[:, q]).then_inc(xd_ready, 1)

            def finish(s, q):
                if not conv or not runs(s, 0, E2):
                    return
                if runs(s, 1):
                    v.wait_ge(xd_ready, s)
                if kind == CONV1:
                    destinations(s, q)
                    v.tensor_tensor(t3[:, :, :], wide(xd_at(s)), m.b2_rows, ALU.add).then_inc(chain2, 1)
                    v.wait_ge(si_ready, s + 1)
                    v.wait_ge(post_done, s + 1)
                    v.tensor_tensor(new[:, q], wide(S[0][:, :]), dinv(s), ALU.mult).then_inc(new_ready, 1)
                    v.wait_ge(new_ready, s + 1)
                    v.tensor_tensor(t4[:, :, :], new[:, q], dinv(s), ALU.mult).then_inc(chain2, 1)
                    v.wait_ge(chain2, s * 2 + 2)
                    v.tensor_tensor(wide(xd_at(s)), t3[:, :, :], t4[:, :, :], ALU.add).then_inc(xd_ready, 1)
                else:
                    v.tensor_tensor(t3[:, :, :], new[:, q], m.bias_rows, ALU.add).then_inc(chain2, 1)
                    v.wait_ge(chain2, s + 1)
                    v.wait_ge(post_done, s + 1)
                    v.tensor_tensor(wide(xd_at(s)), wide(S[0][:, :]), t3[:, :, :], ALU.add).then_inc(xd_ready, 1)

            def body(b, q):
                relate(b, q)
                update(b - 2, q)
                scan(b - 1, 1 - q)
                normalise(b - 2, q)
                finish(b - 3, 1 - q)
            go(v, body)


def attention_stage(nc, io, m):
    NR = R8
    with ExitStack() as ctx:
        sb = lambda n, s, d=F32: ctx.enter_context(nc.sbuf_tensor("at_" + n, s, d))
        sem = Semaphores(nc, "at_")
        pair = lambda n: [sem(n + "_even"), sem(n + "_odd")]
        gi = sb("gi", [P, 2, 2, BT], I32)
        rows = sb("rows", [P, 2, 2, BT, D])
        typ = sb("typ", [P, 2, BE], BF16)
        col = sb("col", [P, 2, 2, BE])
        masked = sb("masked", [P, 4, BE])
        msg = sb("msg", [P, 2, BE])
        prod = sb("prod", [P, 2, BE])
        w = sb("w", [P, NR, D])
        w_loaded = sem("w_loaded")
        gathered, typ_loaded, stored = sem.of_pool("gathered"), pair("typ_loaded"), pair("stored")
        idx_ready, turned, col_ready, mask_ready, mask_used, msg_ready, prod_ready, scored, kept = (
            sem(n) for n in ("idx_ready", "turned", "col_ready", "mask_ready", "mask_used", "msg_ready",
                             "prod_ready", "scored", "kept"))
        T, HS, HD, SC = m.psum[0:2], m.psum[2:4], m.psum[4:6], m.psum[6:8]
        MB = 2 * NR
        E2 = NB - 1
        ctx.callback(sem.clear)
        block = ctx.enter_context(nc.Block())
        go = lambda eng, body: pipeline(eng, body, -2, NB + 1, 2, 2)

        @block.sync
        def _(sp):
            sp.dma_start(w[:, :, :], io["W_att"].rearrange("r i o -> i r o")).then_inc(w_loaded, 16)

            def body(b, q):
                o = 1 - q
                s = b + 2
                if runs(s, 0, E2):
                    if runs(s, 2):
                        hold(sp, mask_ready, (s - 1) * MB)
                    plane = m.type_plane[NR][bass.ds(s * BE, BE)]
                    sp.dma_start(typ[:, q, :], plane.rearrange("(a n) -> a n", a=1).to_broadcast([P, BE]))\
                        .then_inc(typ_loaded[q], 16)
                s = b - 1
                if runs(s, 0, E2):
                    hold(sp, msg_ready, s + 1)
                    sp.dma_start(m.message[:, bass.ds(s * BE, BE)], msg[:, o, :]).then_inc(stored[o], 16)
            go(sp, body)
            for q in range(2):
                hold(sp, stored[q], of_slot(E2 - (E2 - q) % 2, q, 16))

        @block.gpsimd
        def _(pool):
            def body(b, q):
                s = b + 2
                if runs(s, 0, E2):
                    hold(pool, idx_ready, s + 1)
                    if runs(s, 2):
                        hold(pool, turned, s - 1)
                    for side in range(2):
                        for j in range(BT):
                            pool.indirect_dma_start(rows[:, q, side, j, :], None, m.tables["X2"],
                                                    bass.IndirectOffsetOnAxis(ap=gi[:, q, side, j:j + 1], axis=0))\
                                .then_inc(gathered[q], 16)
            go(pool, body)

        @block.scalar
        def _(act):
            def body(b, q):
                o = 1 - q
                s = b + 2
                if runs(s, 0, E2):
                    if runs(s, 2):
                        act.wait_ge(gathered[q], of_slot(s - 2, q, 32 * BT))
                    act.activation(gi[:, q, 0, :], at(m.src_col, s), ACT.Copy)
                    act.activation(gi[:, q, 1, :], at(m.dst_col, s), ACT.Copy).then_inc(idx_ready, 1)
                s = b + 1
                if runs(s, 0, E2):
                    act.wait_ge(turned, s + 1)
                    if runs(s, 2):
                        act.wait_ge(mask_ready, (s - 1) * MB)
                    act.activation(col[:, o, 0, :], T[0][:, :], ACT.Copy)
                    act.activation(col[:, o, 1, :], T[1][:, :], ACT.Copy).then_inc(col_ready, 1)
                s = b - 1
                if runs(s, 0, E2):
                    act.wait_ge(mask_used, (s + 1) * MB)
                    if runs(s, 2):
                        act.wait_ge(stored[o], of_slot(s - 2, o, 16))
                        act.wait_ge(prod_ready, s - 1)
                    act.activation(msg[:, o, :], HS[o][:, :], ACT.Copy).then_inc(msg_ready, 1)
                s = b - 2
                if runs(s, 0, E2):
                    act.wait_ge(scored, s + 1)
                    act.activation(at(m.score_col, s), SC[q][:, 0:BT], ACT.Copy).then_inc(kept, 1)
            go(act, body)

        @block.tensor
        def _(pe):
            pe.wait_ge(w_loaded, 16)

            def body(b, q):
                o = 1 - q
                s = b + 1
                if runs(s, 0, E2):
                    pe.wait_ge(gathered[o], of_slot(s, o, 32 * BT))
                    if runs(s, 1):
                        pe.wait_ge(col_ready, s)
                    for side in range(2):
                        for j in range(BT):
                            last = pe.transpose(T[side][:, j * TE:(j + 1) * TE], rows[:, o, side, j, :], m.ident[:, :])
                    last.then_inc(turned, 1)
                s = b
                if runs(s, 0, E2):
                    if runs(s, 2):
                        pe.wait_ge(msg_ready, s - 1)
                        pe.wait_ge(prod_ready, s - 1)
                    for i in range(MB):
                        pe.wait_ge(mask_ready, s * MB + i + 1)
                        bank = (HS if i % 2 == 0 else HD)[q]
                        pe.matmul(bank[:, :], w[:, i // 2, :], masked[:, i % 4, :], start=(i < 2), stop=(i >= MB - 2))\
                            .then_inc(mask_used, 1)
                s = b - 2
                if runs(s, 0, E2):
                    pe.wait_ge(prod_ready, s + 1)
                    if runs(s, 2):
                        pe.wait_ge(kept, s - 1)
                    for j in range(BT):
                        last = pe.matmul(SC[q][:, j:j + 1], prod[:, q, j * TE:(j + 1) * TE], m.ones[:, 0:1],
                                         start=True, stop=True)
                    last.then_inc(scored, 1)
            go(pe, body)

        @block.vector
        def _(v):
            def body(b, q):
                o = 1 - q
                s = b
                if runs(s, 0, E2):
                    v.wait_ge(col_ready, s + 1)
                    v.wait_ge(typ_loaded[q], of_slot(s, q, 16))
                    for i in range(MB):
                        if i >= 4 or runs(s, 1):
                            v.wait_ge(mask_used, s * MB + i - 3)
                        v.scalar_tensor_tensor(out=masked[:, i % 4, :], in0=typ[:, q, :], scalar=float(i // 2),
                                               in1=col[:, q, i % 2, :], op0=ALU.is_equal, op1=ALU.mult)\
                            .then_inc(mask_ready, 1)
                s = b - 1
                if runs(s, 0, E2):
                    v.wait_ge(msg_ready, s + 1)
                    if runs(s, 2):
                        v.wait_ge(scored, s - 1)
                    v.tensor_tensor(prod[:, o, :], msg[:, o, :], HD[o][:, :], ALU.mult).then_inc(prod_ready, 1)
            go(v, body)


def softmax_stage(nc, io, m):
    with ExitStack() as ctx:
        sb = lambda n, s, d=F32: ctx.enter_context(nc.sbuf_tensor("sm_" + n, s, d))
        sem = Semaphores(nc, "sm_")
        isrel = sb("isrel", [P, R8, KT])
        tmp = sb("tmp", [P, R8, KT])
        low = sb("low", [P, R8, KT])
        score = sb("score", [P, KT])
        best = sb("best", [P, R8])
        top = sb("top", [R8, 1])
        diag = sb("diag", [R8, R8])
        every = sb("every", [P, R8])
        own = sb("own", [P, KT])
        ex = sb("ex", [P, KT])
        part = sb("part", [P, R8])
        alpha = sb("alpha", [P, KT])
        turned = sb("turned", [QR, 2, TE])
        chain, ready, exped, pe_done, stored = (sem(n) for n in ("chain", "ready", "exped", "pe_done", "stored"))
        ps = m.psum
        ctx.callback(sem.clear)
        block = ctx.enter_context(nc.Block())

        @block.vector
        def _(v):
            n = [0]

            def link(ins):
                n[0] += 1
                ins.then_inc(chain, 1)
                v.wait_ge(chain, n[0])

            def over(col):
                return col.unsqueeze(1).to_broadcast([P, R8, KT])

            v.tensor_scalar(own[:, :], m.score_col[:, :], SLOPE, None, ALU.mult)
            for r in range(R8):
                last = v.tensor_scalar(isrel[:, r, :], m.type_col[:, :], float(r), None, ALU.is_equal)
            link(last)
            v.tensor_tensor(score[:, :], m.score_col[:, :], own[:, :], ALU.max)
            link(v.tensor_scalar(low[:, :, :], isrel[:, :, :], -LOW, LOW, ALU.mult, ALU.add))
            link(v.tensor_tensor(tmp[:, :, :], isrel[:, :, :], over(score[:, :]), ALU.mult))
            link(v.tensor_tensor(tmp[:, :, :], tmp[:, :, :], low[:, :, :], ALU.add))
            v.tensor_reduce(best[:, :], tmp[:, :, :], AX.X, ALU.max).then_inc(ready, 1)
            v.wait_ge(pe_done, 1)
            link(v.tensor_reduce(top[:, :], ps[0][0:R8, 0:P], AX.X, ALU.max))
            v.tensor_scalar(diag[:, :], m.ident[0:R8, 0:R8], top[:, 0:1], None, ALU.mult).then_inc(ready, 1)
            v.wait_ge(pe_done, 2)
            link(v.tensor_copy(every[:, :], ps[1][:, 0:R8]))
            link(v.tensor_tensor(tmp[:, :, :], isrel[:, :, :], bc(every[:, :], KT), ALU.mult))
            link(v.tensor_reduce(own[:, :], tmp[:, :, :].rearrange("p r k -> p k r"), AX.X, ALU.add))
            v.tensor_tensor(score[:, :], score[:, :], own[:, :], ALU.subtract).then_inc(ready, 1)
            v.wait_ge(exped, 1)
            link(v.tensor_tensor(tmp[:, :, :], isrel[:, :, :], over(ex[:, :]), ALU.mult))
            v.tensor_reduce(part[:, :], tmp[:, :, :], AX.X, ALU.add).then_inc(ready, 1)
            v.wait_ge(pe_done, 3)
            link(v.tensor_copy(every[:, :], ps[2][:, 0:R8]))
            link(v.tensor_tensor(tmp[:, :, :], isrel[:, :, :], bc(every[:, :], KT), ALU.mult))
            link(v.tensor_reduce(own[:, :], tmp[:, :, :].rearrange("p r k -> p k r"), AX.X, ALU.add))
            link(v.tensor_scalar(own[:, :], own[:, :], 1e-30, None, ALU.max))
            link(v.reciprocal(own[:, :], own[:, :]))
            v.tensor_tensor(alpha[:, :], ex[:, :], own[:, :], ALU.mult).then_inc(ready, 1)
            v.wait_ge(pe_done, 4)
            v.tensor_copy(turned[:, :, :].rearrange("q b e -> q (b e)"), ps[3][0:QR, 0:2 * TE]).then_inc(ready, 1)

        @block.scalar
        def _(act):
            act.wait_ge(ready, 3)
            act.activation(ex[:, :], score[:, :], ACT.Exp).then_inc(exped, 1)

        @block.tensor
        def _(pe):
            pe.wait_ge(ready, 1)
            pe.transpose(ps[0][0:R8, 0:P], best[:, :], m.ident[:, :]).then_inc(pe_done, 1)
            pe.wait_ge(ready, 2)
            pe.matmul(ps[1][:, 0:R8], m.ones[0:R8, :], diag[:, :], start=True, stop=True).then_inc(pe_done, 1)
            pe.wait_ge(ready, 4)
            pe.matmul(ps[2][:, 0:R8], m.ones[:, :], part[:, :], start=True, stop=True).then_inc(pe_done, 1)
            pe.wait_ge(ready, 5)
            for b in range(2):
                last = pe.transpose(ps[3][0:QR, b * TE:(b + 1) * TE], alpha[:, b * QR:(b + 1) * QR], m.ident[:, :])
            last.then_inc(pe_done, 1)

        @block.sync
        def _(sp):
            hold(sp, ready, 6)
            sp.dma_start(m.alpha_plane.rearrange("(b q n) -> q b n", b=2, n=TE), turned[:, :, :]).then_inc(stored, 16)
            hold(sp, stored, 16)


def build(nc, io):
    m = Memory()
    dram = lambda name, shape, dt=F32: nc.dram_tensor(name, shape, dt, kind="Internal").ap()
    m.tables = {"G1": dram("t_g1", (NP, D)), "X1": dram("t_x1", (NP, D)), "X2": dram("t_x2", (NP, D)),
                "X3": dram("t_x3", (NP, D)), "OUT": io["out"]}
    m.dinv_table = dram("t_dinv", (NP, 1))
    m.same_plane = dram("p_same", (EP,), BF16)
    m.type_plane = {R8: dram("p_type8", (EP,), BF16), R16: dram("p_type16", (EP,), BF16)}
    m.weight_plane = dram("p_weight", (EP,))
    m.alpha_plane = dram("p_alpha", (EP,))
    m.message = dram("p_message", (P, EP))
    m.records = dram("records", (EP, 4), I32)
    m.sorted_dst = dram("sorted_dst", (EP,), I32)
    with ExitStack() as ctx:
        sb = lambda n, s, d=F32: ctx.enter_context(nc.sbuf_tensor("m_" + n, s, d))
        m.psum = [ctx.enter_context(nc.psum_tensor(f"bank{i}", [P, 512], F32)) for i in range(8)]
        m.ident, m.ones, m.iota = sb("ident", [P, P]), sb("ones", [P, P]), sb("iota", [P, RPP])
        m.eps = sb("eps", [P, 1])
        m.w1, m.w2, m.root = sb("w1", [P, D]), sb("w2", [P, D]), sb("root", [P, D])
        m.b1, m.b2, m.bias = sb("b1", [P, 1]), sb("b2", [P, D]), sb("bias", [P, D])
        m.b2_rows, m.bias_rows = (t[:, :].unsqueeze(1).to_broadcast([P, BT, D]) for t in (m.b2, m.bias))
        column = lambda name: sb(name + "_col", [P, KT])
        m.src_col, m.dst_col, m.last_col, m.dinv_col, m.type_col = map(column, ("src", "dst", "last", "dinv", "type"))
        m.dstraw_col, m.hi_col, m.lo_col, m.ds_col, m.score_col = map(column, ("dstraw", "hi", "lo", "ds", "score"))
        m.dst_int, m.hi_int, m.lo_int = (sb(n, [P, KT], I32) for n in ("dst_int", "hi_int", "lo_int"))
        m.xd = sb("xd", [P, KT * D])
        m.halo = sb("halo", [QR, 258], I32)
        m.rows = sb("rows", [QR, 4, 256], I32)
        constants_stage(nc, m)
        order_stage(nc, io, m)
        setup_stage(nc, io, m)
        degree_stage(nc, io, m)
        prefill_stage(nc, io, m)
        edge_stage(nc, io, m, CONV1, io["x"], m.tables["G1"])
        edge_stage(nc, io, m, CONV2, m.tables["G1"], m.tables["X1"])
        edge_stage(nc, io, m, MEAN, m.tables["X1"], m.tables["X2"], io["W_mean"], R8)
        attention_stage(nc, io, m)
        softmax_stage(nc, io, m)
        edge_stage(nc, io, m, ATTEND, None, m.tables["X3"])
        edge_stage(nc, io, m, SUM, m.tables["X3"], m.tables["OUT"], io["W_sum"], R16)


def kernel(x, src, dst, edge_type_16, edge_type_8, L0_gnn_W1, L0_gnn_b1, L0_gnn_W2, L0_gnn_b2,
           L1_gnn_W, L1_gnn_root, L1_gnn_bias, L2_gnn_W, L3_gnn_weight):
    import numpy as np
    import concourse.bacc as bacc
    from concourse.bass_utils import run_bass_kernel_spmd

    def padded(a, n, fill):
        a = np.asarray(a)
        return np.concatenate([a, np.full((n - a.shape[0],) + a.shape[1:], fill, a.dtype)])

    arrays = {
        "x": padded(x, NP, 0),
        "edges": np.stack([padded(src, EP, PAD_SRC), padded(dst, EP, PAD_DST),
                           padded(edge_type_8, EP, PAD_TYPE), padded(edge_type_16, EP, PAD_TYPE)]),
        "W1": np.asarray(L0_gnn_W1), "b1": np.asarray(L0_gnn_b1),
        "W2": np.asarray(L0_gnn_W2), "b2": np.asarray(L0_gnn_b2),
        "W_mean": np.asarray(L1_gnn_W), "root": np.asarray(L1_gnn_root), "bias": np.asarray(L1_gnn_bias),
        "W_att": np.asarray(L2_gnn_W), "W_sum": np.asarray(L3_gnn_weight),
    }
    arrays = {k + "_dram": np.ascontiguousarray(a) for k, a in arrays.items()}
    nc = bacc.Bacc("TRN2", target_bir_lowering=False, num_devices=1)
    io = {k[:-5]: nc.dram_tensor(k, a.shape, mybir.dt.from_np(a.dtype), kind="ExternalInput").ap()
          for k, a in arrays.items()}
    io["out"] = nc.dram_tensor("out_dram", (NP, D), F32, kind="ExternalOutput").ap()
    build(nc, io)
    got = run_bass_kernel_spmd(nc, [arrays], core_ids=[0])
    return got.results[0]["out_dram"][:N]
```

```python
from contextlib import ExitStack

import concourse.bass as bass
from concourse import mybir
from concourse.alu_op_type import AluOpType as ALU

F32 = mybir.dt.float32
BF16 = mybir.dt.bfloat16
F16 = mybir.dt.float16
I32 = mybir.dt.int32
ACT = mybir.ActivationFunctionType
AX = mybir.AxisListType

N, D, E = 50000, 128, 25000
P = 128
TE = P
BT = 4
BE = BT * TE
NB = -(-E // BE)
EP = NB * BE
KT = EP // TE
RPP = -(-N // (P * BT)) * BT
NP = P * RPP
NCH = RPP // BT
QR = EP // 256
R8, R16 = 8, 16
FAR = 65536
PAD_DST, PAD_SRC, PAD_TYPE = 60000, 0, -1
EPS = 1e-5
SLOPE = 0.2
LOW = -1.0e30
SRC, DST, T8, T16 = range(4)


def static(b):
    return isinstance(b, int)


def runs(b, first=0, last=NB - 1):
    return not static(b) or first <= b <= last


def bc(ap, width):
    return ap.rearrange("p (n o) -> p n o", o=1).to_broadcast([ap.shape[0], ap.shape[1], width])


def hold(eng, sem, value):
    eng.wait_ge(sem, value)
    if not static(value):
        eng.nop(nofuse=True)


def of_slot(b, q, inc):
    return (b - q) * (inc // 2) + inc


def pipeline(eng, body, first, last, ahead, behind):
    lo = behind + 2 + (behind % 2)
    hi = NB - ahead
    hi -= (hi - lo) % 2
    for b in range(first, lo):
        body(b, b % 2)
    with eng.Fori(lo // 2, hi // 2) as pair:
        body(pair * 2, 0)
        body(pair * 2 + 1, 1)
    for b in range(hi, last + 1):
        body(b, b % 2)


class Semaphores:

    def __init__(self, nc, prefix):
        self.nc, self.prefix, self.mine = nc, prefix, []

    def __call__(self, name):
        self.mine.append(self.nc.alloc_semaphore(self.prefix + name))
        return self.mine[-1]

    def of_pool(self, name):
        return [self.nc.alloc_semaphore(f"{self.prefix}{name}_{slot}") for slot in ("even", "odd")]

    def clear(self):
        with self.nc.Block() as block:
            @block.gpsimd
            def _(pool):
                for s in self.mine:
                    pool.sem_clear(s)
        for s in self.mine:
            self.nc.release_semaphore(s)


class Memory:
    pass


def at(col, b, n=BT):
    return col[:, bass.ds(b * n, n)]


def constants_stage(nc, m):
    with ExitStack() as ctx:
        sem = Semaphores(nc, "co_")
        consts = sem("consts")
        ctx.callback(sem.clear)
        block = ctx.enter_context(nc.Block())

        @block.gpsimd
        def _(pool):
            pool.memset(m.ident[:, :], 0.0).then_inc(consts, 1)
            hold(pool, consts, 1)
            pool.affine_select(out=m.ident[:, :], in_=m.ident[:, :], compare_op=ALU.not_equal, fill=1.0,
                               base=0, pattern=[[-1, P]], channel_multiplier=1).then_inc(consts, 1)
            pool.iota(m.iota[:, :], pattern=[[1, RPP]], base=0, channel_multiplier=0,
                      allow_small_or_imprecise_dtypes=True).then_inc(consts, 1)
            pool.memset(m.ones[:, :], 1.0).then_inc(consts, 1)
            pool.memset(m.eps[:, :], EPS).then_inc(consts, 1)


def order_stage(nc, io, m):
    with ExitStack() as ctx:
        sb = lambda n, s, d=F32: ctx.enter_context(nc.sbuf_tensor("or_" + n, s, d))
        sem = Semaphores(nc, "or_")
        halof = sb("halof", [QR, 257])
        falls = sb("falls", [QR, 256])
        fell = sb("fell", [QR, 1])
        unsorted = sb("unsorted", [1, 1], I32)
        rowf = sb("rowf", [QR, 4, 256])
        col = sb("col", [P, 4, KT])
        number = sb("number", [P, KT])
        place = sb("place", [P, KT])
        others = sb("others", [P, BE], I32)
        othersf = sb("othersf", [P, BE])
        numbers = sb("numbers", [P, BE])
        less, equal, before = (sb(n, [P, BT, BE]) for n in ("less", "equal", "before"))
        count = sb("count", [P, BT])
        record = sb("record", [P, 4], I32)
        where = sb("where", [P, 1], I32)
        packed = sb("packed", [QR, 256, 4], I32)
        loaded, prep, counted, flagged, turned, copied = (
            sem(n) for n in ("loaded", "prep", "counted", "flagged", "turned", "copied"))
        spread, used, numbered, staged, sorted_rows, unpacked, halo_set = (
            sem(n) for n in ("spread", "used", "numbered", "staged", "sorted_rows", "unpacked", "halo_set"))
        placed, vc = sem.of_pool("placed")[0], sem("chain")
        edges, halo, rows, ps = io["edges"], m.halo, m.rows, m.psum
        ctx.callback(sem.clear)
        block = ctx.enter_context(nc.Block())

        def neighbours(sp, dst, done):
            with nc.allow_non_contiguous_dma(reason="one element per partition"):
                sp.dma_start(halo[1:QR, 0:1], dst[255:EP - 1:256].rearrange("(q n) -> q n", n=1)).then_inc(done, 16)
                sp.dma_start(halo[0:QR - 1, 257:258], dst[256:EP:256].rearrange("(q n) -> q n", n=1)).then_inc(done, 16)

        def out_of_order(eng):
            eng.wait_ge(flagged, 1)
            return eng.value_load(unsorted[0:1, 0:1], min_val=0, max_val=1) > 0

        @block.sync
        def _(sp):
            sp.wait_ge(prep, 1)
            neighbours(sp, edges[DST, :], loaded)
            sp.dma_start(halo[:, 1:257], edges[DST, :].rearrange("(q n) -> q n", n=256)).then_inc(loaded, 16)
            for f in range(4):
                sp.dma_start(rows[:, f, :], edges[f, :].rearrange("(q n) -> q n", n=256)).then_inc(loaded, 16)
            sp.wait_ge(loaded, 16 * 7)
            with sp.If(out_of_order(sp)):
                with sp.Fori(0, NB) as b:
                    hold(sp, used, b + 1)
                    sp.dma_start(others[:, :], edges[DST, bass.ds(b * BE, BE)].rearrange("(a n) -> a n", a=1)
                                 .to_broadcast([P, BE])).then_inc(spread, 16)
                sp.wait_ge(placed, 16 * KT)
                sp.dma_start(packed[:, :, :], m.records.rearrange("(q n) f -> q n f", n=256)).then_inc(sorted_rows, 16)
                sp.wait_ge(unpacked, 1)
                sp.dma_start(m.sorted_dst.rearrange("(q n) -> q n", n=256), rows[:, DST, :]).then_inc(sorted_rows, 16)
                sp.wait_ge(sorted_rows, 32)
                neighbours(sp, m.sorted_dst, halo_set)
                sp.wait_ge(halo_set, 32)

        @block.gpsimd
        def _(pool):
            pool.iota(number[:, :], pattern=[[TE, KT]], base=0, channel_multiplier=1,
                      allow_small_or_imprecise_dtypes=True).then_inc(numbered, 1)
            pool.iota(numbers[:, :], pattern=[[1, BE]], base=0, channel_multiplier=0,
                      allow_small_or_imprecise_dtypes=True).then_inc(numbered, 1)
            with pool.If(out_of_order(pool)):
                with pool.Fori(0, KT) as k:
                    hold(pool, staged, k + 1)
                    pool.indirect_dma_start(m.records, bass.IndirectOffsetOnAxis(ap=where[:, 0:1], axis=0),
                                            record[:, :], None, bounds_check=EP - 1, oob_is_err=False)\
                        .then_inc(placed, 16)

        @block.tensor
        def _(pe):
            pe.wait_ge(counted, 1)
            pe.matmul(ps[0][0:1, 0:1], fell[:, :], m.ones[0:QR, 0:1], start=True, stop=True).then_inc(turned, 1)
            with pe.If(out_of_order(pe)):
                pe.wait_ge(counted, 2)
                for f in range(4):
                    for b in range(2):
                        last = pe.transpose(ps[1 + f][:, b * QR:(b + 1) * QR], rowf[:, f, b * TE:(b + 1) * TE],
                                            m.ident[0:QR, 0:QR])
                last.then_inc(turned, 1)

        @block.vector
        def _(v):
            n = [0]

            def link(ins):
                n[0] += 1
                ins.then_inc(vc, 1)
                v.wait_ge(vc, n[0])

            v.memset(halo[:, 257:258], FAR)
            v.memset(halo[:, 0:1], -1).then_inc(prep, 1)
            v.wait_ge(loaded, 16 * 7)
            link(v.tensor_copy(halof[:, :], halo[:, 1:258]))
            link(v.tensor_tensor(falls[:, :], halof[:, 1:257], halof[:, 0:256], ALU.is_lt))
            v.tensor_reduce(fell[:, :], falls[:, :], AX.X, ALU.add).then_inc(counted, 1)
            v.wait_ge(turned, 1)
            v.tensor_scalar(unsorted[:, :], ps[0][0:1, 0:1], 0.0, None, ALU.is_gt).then_inc(flagged, 1)
            with v.If(out_of_order(v)):
                v.tensor_copy(rowf[:, :, :], rows[:, :, :]).then_inc(counted, 1)
                v.wait_ge(turned, 2)
                for f in range(4):
                    v.tensor_copy(col[:, f, :].rearrange("p (q b) -> p b q", b=2),
                                  ps[1 + f][:, 0:2 * QR].rearrange("p (b q) -> p b q", b=2))
                v.wait_ge(numbered, 2)
                v.memset(place[:, :], 0.0)
                v.drain()
                v.tensor_copy(count[:, :], place[:, 0:BT]).then_inc(used, 1)
                wide_others = othersf[:, :].unsqueeze(1).to_broadcast([P, BT, BE])
                wide_numbers = numbers[:, :].unsqueeze(1).to_broadcast([P, BT, BE])
                with v.Fori(0, NB) as b:
                    hold(v, spread, b * 16 + 16)
                    v.tensor_copy(othersf[:, :], others[:, :])
                    v.drain()
                    v.tensor_copy(count[:, :], place[:, 0:BT]).then_inc(used, 1)
                    with v.Fori(0, NB) as own:
                        dst = bc(col[:, DST, bass.ds(own * BT, BT)], BE)
                        v.drain()
                        v.tensor_tensor(less[:, :, :], wide_others, dst, ALU.is_lt)
                        v.tensor_tensor(equal[:, :, :], wide_others, dst, ALU.is_equal)
                        v.tensor_tensor(before[:, :, :], wide_numbers, bc(at(number, own), BE), ALU.is_lt)
                        v.drain()
                        v.tensor_tensor(equal[:, :, :], equal[:, :, :], before[:, :, :], ALU.mult)
                        v.drain()
                        v.tensor_tensor(less[:, :, :], less[:, :, :], equal[:, :, :], ALU.add)
                        v.drain()
                        v.tensor_reduce(count[:, :], less[:, :, :], AX.X, ALU.add)
                        v.drain()
                        v.tensor_tensor(at(place, own), at(place, own), count[:, :], ALU.add)
                    v.drain()
                    v.tensor_scalar(numbers[:, :], numbers[:, :], float(BE), None, ALU.add)
                    v.drain()
                with v.Fori(0, KT) as k:
                    v.tensor_copy(where[:, :], place[:, bass.ds(k, 1)])
                    v.tensor_copy(record[:, :], col[:, :, bass.ds(k, 1)].rearrange("p f o -> p (f o)")).then_inc(staged, 1)
                    hold(v, placed, k * 16 + 16)
                v.wait_ge(sorted_rows, 16)
                v.tensor_copy(rows[:, :, :], packed[:, :, :].rearrange("q n f -> q f n")).then_inc(unpacked, 1)
                v.wait_ge(unpacked, 1)
                v.tensor_copy(halo[:, 1:257], rows[:, DST, :])
                v.drain()


def setup_stage(nc, io, m):
    with ExitStack() as ctx:
        sb = lambda n, s, d=F32: ctx.enter_context(nc.sbuf_tensor("su_" + n, s, d))
        sem = Semaphores(nc, "su_")
        halo, rows = m.halo, m.rows
        rowf = sb("rowf", [QR, 4, 256])
        dstf = sb("dstf", [QR, 258])
        same = sb("same", [QR, 256])
        nxt = sb("nxt", [QR, 256])
        flag = sb("flag", [QR, 2, 256])
        through = sb("through", [QR, 2, 256])
        zero = sb("zero", [QR, 256])
        relid = sb("relid", [QR, R8 + 1, 256])
        cnt = sb("cnt", [QR, 2, R8 + 1, 256])
        ends = sb("ends", [QR, 2, 2, R8 + 1])
        endT = sb("endT", [R8 + 1, 2, 2, QR])
        carryT = sb("carryT", [R8 + 1, 2, QR + 1])
        carry = sb("carry", [QR, 2, R8 + 1])
        field = sb("field", [QR, 6, 256])
        typ = sb("typ", [QR, 3, 256], BF16)
        own = sb("own", [QR, 256])
        wgt = sb("wgt", [QR, 256])
        root_of = sb("root_of", [QR, 256])
        rooted = sem("rooted")
        ps = m.psum
        lin, prep = sem("lin"), sem("prep")
        tr, back, colT, colC, stored = sem("tr"), sem("back"), sem("colT"), sem("colC"), sem("stored")
        wl = sem("wl")
        vc = sem("chain")
        SRC_F, CL_F, LAST_F, DINV_F, T8_F, DST_F = range(6)
        ctx.callback(sem.clear)
        block = ctx.enter_context(nc.Block())

        @block.sync
        def _(sp):
            for dst, src in ((m.w1, io["W1"]), (m.w2, io["W2"]), (m.root, io["root"])):
                sp.dma_start(dst[:, :], src).then_inc(wl, 16)
            sp.dma_start(m.b1[:, :], io["b1"].rearrange("(p n) -> p n", n=1)).then_inc(wl, 16)
            for dst, src in ((m.b2, io["b2"]), (m.bias, io["bias"])):
                sp.dma_start(dst[:, :], src.rearrange("(a n) -> a n", a=1).to_broadcast([P, D])).then_inc(wl, 16)
            hold(sp, lin, 1)
            for f, plane in enumerate((m.same_plane, m.type_plane[R8], m.type_plane[R16])):
                sp.dma_start(plane.rearrange("(q n) -> q n", n=256), typ[:, f, :]).then_inc(stored, 16)
            hold(sp, lin, 2)
            sp.dma_start(m.weight_plane.rearrange("(q n) -> q n", n=256), wgt[:, :]).then_inc(stored, 16)
            hold(sp, stored, 64)
            hold(sp, wl, 96)

        @block.vector
        def _(v):
            n = [0]

            def link(ins):
                n[0] += 1
                ins.then_inc(vc, 1)
                v.wait_ge(vc, n[0])

            v.memset(zero[:, :], 0.0)
            v.memset(carryT[:, :, :], 0.0)
            link(v.memset(relid[:, R8, :], 1.0))
            v.tensor_copy(dstf[:, :], halo[:, :])
            link(v.tensor_copy(rowf[:, :, :], rows[:, :, :]))
            v.tensor_tensor(same[:, :], dstf[:, 1:257], dstf[:, 0:256], ALU.is_equal)
            link(v.tensor_tensor(nxt[:, :], dstf[:, 1:257], dstf[:, 2:258], ALU.is_equal))
            v.tensor_copy(typ[:, 0, :], same[:, :])
            v.tensor_copy(typ[:, 1:3, :], rowf[:, T8:T16 + 1, :]).then_inc(lin, 1)
            v.tensor_copy(flag[:, 0, :], same[:, :])
            v.tensor_copy(flag[:, 1, :], nxt[:, :])
            v.tensor_copy(field[:, SRC_F, :], rowf[:, SRC, :])
            v.tensor_copy(field[:, T8_F, :], rowf[:, T8, :])
            v.tensor_copy(field[:, DST_F, :], rowf[:, DST, :])
            v.tensor_scalar(field[:, CL_F, :], rowf[:, DST, :], float(N - 1), None, ALU.min)
            v.scalar_tensor_tensor(out=field[:, LAST_F, :], in0=nxt[:, :], scalar=float(FAR), in1=rowf[:, DST, :],
                                   op0=ALU.mult, op1=ALU.add)
            for r in range(R8):
                last = v.tensor_scalar(relid[:, r, :], rowf[:, T8, :], float(r), None, ALU.is_equal)
            link(last)
            v.memset(flag[:, 0, 0:1], 0.0)
            link(v.memset(flag[:, 1, 255:256], 0.0))
            v.tensor_tensor_scan(through[:, 0, :], same[:, :], zero[:, :], 1.0, ALU.mult, ALU.max)
            v.tensor_tensor_scan(through[:, 1, ::-1], nxt[:, ::-1], zero[:, :], 1.0, ALU.mult, ALU.max)
            for r in range(R8 + 1):
                v.tensor_tensor_scan(cnt[:, 0, r, :], flag[:, 0, :], relid[:, r, :], 0.0, ALU.mult, ALU.add)
                last = v.tensor_tensor_scan(cnt[:, 1, r, ::-1], flag[:, 1, ::-1], relid[:, r, ::-1], 0.0,
                                            ALU.mult, ALU.add)
            link(last)
            v.tensor_copy(ends[:, 0, 0, :], cnt[:, 0, :, 255])
            v.tensor_copy(ends[:, 1, 0, :], cnt[:, 1, :, 0])
            v.tensor_copy(ends[:, 0, 1, :], through[:, 0, 255:256].to_broadcast([QR, R8 + 1]))
            v.tensor_copy(ends[:, 1, 1, :], through[:, 1, 0:1].to_broadcast([QR, R8 + 1])).then_inc(prep, 1)
            v.wait_ge(tr, 1)
            link(v.tensor_copy(endT[:, :, :, :].rearrange("r a b q -> r (a b q)"), ps[0][0:R8 + 1, 0:4 * QR]))
            v.tensor_tensor_scan(carryT[:, 0, 1:QR + 1], endT[:, 0, 1, :], endT[:, 0, 0, :], 0.0, ALU.mult, ALU.add)
            v.tensor_tensor_scan(carryT[:, 1, QR - 1::-1], endT[:, 1, 1, ::-1], endT[:, 1, 0, ::-1], 0.0,
                                 ALU.mult, ALU.add).then_inc(prep, 1)
            v.wait_ge(back, 1)
            link(v.tensor_copy(carry[:, :, :].rearrange("q a r -> q (a r)"), ps[1][0:QR, 0:2 * (R8 + 1)]))
            for d in range(2):
                for r in range(R8 + 1):
                    last = v.scalar_tensor_tensor(out=cnt[:, d, r, :], in0=through[:, d, :], scalar=carry[:, d, r:r + 1],
                                                  in1=cnt[:, d, r, :], op0=ALU.mult, op1=ALU.add)
            link(last)
            v.tensor_tensor(cnt[:, 0, :, :], cnt[:, 0, :, :], cnt[:, 1, :, :], ALU.add).then_inc(prep, 1)
            v.wait_ge(prep, 3)
            v.wait_ge(rooted, 1)
            v.reciprocal(field[:, DINV_F, :], root_of[:, :])
            link(v.tensor_tensor(cnt[:, 1, 0:R8, :], cnt[:, 0, 0:R8, :], relid[:, 0:R8, :], ALU.mult))
            link(v.tensor_reduce(own[:, :], cnt[:, 1, 0:R8, :].rearrange("q r n -> q n r"), AX.X, ALU.add))
            link(v.tensor_scalar(own[:, :], own[:, :], -1.0, None, ALU.add))
            v.reciprocal(wgt[:, :], own[:, :]).then_inc(lin, 1)
            for f, col in ((SRC_F, m.src_col), (CL_F, m.dst_col), (LAST_F, m.last_col),
                           (DINV_F, m.dinv_col), (T8_F, m.type_col), (DST_F, m.dstraw_col)):
                v.wait_ge(colT, f + 1)
                v.tensor_copy(col[:, :].rearrange("p (q b) -> p b q", b=2),
                              ps[2 + f][:, 0:2 * QR].rearrange("p (b q) -> p b q", b=2)).then_inc(colC, 1)
            v.wait_ge(colC, 6)
            link(v.tensor_copy(m.dst_int[:, :], m.dstraw_col[:, :]))
            v.tensor_scalar(m.hi_int[:, :], m.dst_int[:, :], 7, None, ALU.arith_shift_right)
            link(v.tensor_scalar(m.lo_int[:, :], m.dst_int[:, :], 127, None, ALU.bitwise_and))
            v.tensor_copy(m.hi_col[:, :], m.hi_int[:, :])
            v.tensor_copy(m.lo_col[:, :], m.lo_int[:, :])

        @block.scalar
        def _(act):
            act.wait_ge(prep, 3)
            act.activation(root_of[:, :], cnt[:, 0, R8, :], ACT.Sqrt).then_inc(rooted, 1)

        @block.tensor
        def _(pe):
            pe.wait_ge(prep, 1)
            for i in range(4):
                last = pe.transpose(ps[0][0:R8 + 1, i * QR:(i + 1) * QR], ends[:, i // 2, i % 2, :], m.ident[0:QR, 0:QR])
            last.then_inc(tr, 1)
            pe.wait_ge(prep, 2)
            pe.transpose(ps[1][0:QR, 0:R8 + 1], carryT[:, 0, 0:QR], m.ident[0:R8 + 1, 0:R8 + 1])
            pe.transpose(ps[1][0:QR, R8 + 1:2 * (R8 + 1)], carryT[:, 1, 1:QR + 1],
                         m.ident[0:R8 + 1, 0:R8 + 1]).then_inc(back, 1)
            pe.wait_ge(lin, 2)
            for f in range(6):
                for b in range(2):
                    last = pe.transpose(ps[2 + f][:, b * QR:(b + 1) * QR], field[:, f, b * TE:(b + 1) * TE],
                                        m.ident[0:QR, 0:QR])
                last.then_inc(colT, 1)


def degree_stage(nc, io, m):
    with ExitStack() as ctx:
        sb = lambda n, s, d=F32: ctx.enter_context(nc.sbuf_tensor("dg_" + n, s, d))
        sem = Semaphores(nc, "dg_")
        number = sb("number", [P, RPP], F16)
        lo1 = sb("lo1", [P, 4, P], F16)
        hi1 = sb("hi1", [P, 4, RPP], F16)
        cnt = sb("cnt", [P, RPP])
        turned = sb("turned", [RPP // 4, 4, P])
        root_of = sb("root_of", [P, RPP])
        rooted, numbered = sem("rooted"), sem("numbered")
        made, used, copied, tr, out, stored = (sem(x) for x in ("made", "used", "copied", "tr", "out", "stored"))
        ps = m.psum
        ctx.callback(sem.clear)
        block = ctx.enter_context(nc.Block())
        HB = RPP // 4

        @block.vector
        def _(v):
            v.tensor_tensor(m.root1[:, :], m.root[:, :], m.ident[:, :], ALU.add)
            v.tensor_copy(number[:, :], m.iota[:, :]).then_inc(numbered, 1)
            v.wait_ge(numbered, 1)

            def body(k, slot):
                if not static(k):
                    v.wait_ge(used, k - 3)
                v.tensor_scalar(lo1[:, slot, :], number[:, 0:P], m.lo_col[:, bass.ds(k, 1)], None, ALU.is_equal)
                v.tensor_scalar(hi1[:, slot, :], number[:, :], m.hi_col[:, bass.ds(k, 1)], None, ALU.is_equal)\
                    .then_inc(made, 1)
            for k in range(4):
                body(k, k)
            with v.Fori(1, KT // 4) as j:
                for i in range(4):
                    body(j * 4 + i, i)
            v.wait_ge(rooted, 1)
            v.reciprocal(cnt[:, :], root_of[:, :]).then_inc(copied, 1)
            v.wait_ge(tr, 1)
            v.tensor_copy(turned[:, :, :].rearrange("p a b -> p (a b)"), ps[1][0:HB, 0:4 * P]).then_inc(out, 1)

        @block.scalar
        def _(act):
            act.wait_ge(used, KT)
            act.activation(root_of[:, :], ps[0][:, 0:RPP], ACT.Sqrt, bias=m.ones[:, 0:1]).then_inc(rooted, 1)

        @block.tensor
        def _(pe):
            def body(k, slot, first=False, last=False):
                pe.wait_ge(made, k + 1)
                pe.matmul(ps[0][:, 0:RPP], lo1[:, slot, :], hi1[:, slot, :], start=first, stop=last,
                          skip_group_check=True).then_inc(used, 1)
            for k in range(4):
                body(k, k, first=(k == 0))
            with pe.Fori(1, KT // 4 - 1) as j:
                for i in range(4):
                    body(j * 4 + i, i)
            for k in range(KT - 4, KT):
                body(k, k % 4, last=(k == KT - 1))
            pe.wait_ge(copied, 1)
            for g in range(4):
                last = pe.transpose(ps[1][0:HB, g * P:(g + 1) * P], cnt[:, g * HB:(g + 1) * HB], m.ident[:, :])
            last.then_inc(tr, 1)

        @block.sync
        def _(sp):
            hold(sp, out, 1)
            sp.dma_start(m.dinv_table.rearrange("(g p l) o -> p g (l o)", g=4, l=P), turned[:, :, :]).then_inc(stored, 16)
            hold(sp, stored, 16)


def row_stats(v, z, norm, chain, base):
    stats, mv = norm
    for j in range(BT):
        last = v.bn_stats(stats[:, j, :], z[:, j, :])
    last.then_inc(chain, 1)
    hold(v, chain, base + 1)
    for j in range(BT):
        last = v.bn_aggr(mv[:, j, :], stats[:, j, :])
    return last


def prefill_stage(nc, io, m):
    with ExitStack() as ctx:
        sb = lambda n, s, d=F32: ctx.enter_context(nc.sbuf_tensor("pf_" + n, s, d))
        sem = Semaphores(nc, "pf_")
        pair = lambda n: [sem(n + "_even"), sem(n + "_odd")]
        xc = sb("xc", [P, 4, BT, D])
        xT, hT = (sb(n, [P, 2, BE]) for n in ("xT", "hT"))
        g1, z1, x1 = (sb(n, [P, 2, BT, D]) for n in ("g1", "z1", "x1"))
        xb = sb("xb", [P, BT, D])
        stats1, mv1 = sb("stats1", [P, BT, 6]), sb("mv1", [P, BT, 2])
        sd1 = sb("sd1", [P, BT])
        scale1, shift1 = sb("scale1", [P, 2, BT]), sb("shift1", [P, 2, BT])
        gi = sb("gi", [P, 2, 2, 2], I32)
        xs = sb("xs", [P, 2, 2, D])
        ds = sb("ds", [P, 2, 2])
        loaded, gathered = [sem(f"loaded_{i}") for i in range(4)], sem.of_pool("gathered")
        g1_stored, x1_stored = pair("g1_stored"), pair("x1_stored")
        x_turned, xT_copied, xw1_done, hT_ready, hw2_done, g1_ready, xb_ready, z1_ready, x1_ready = (
            sem(n) for n in ("x_turned", "xT_copied", "xw1_done", "hT_ready", "hw2_done", "g1_ready", "xb_ready",
                             "z1_ready", "x1_ready"))
        stats1_ready, scale_step, mv1_ready, sd1_ready, scale1_ready, idx_ready, kept = (
            sem(n) for n in ("stats1_ready", "scale_step", "mv1_ready", "sd1_ready", "scale1_ready", "idx_ready",
                             "kept"))
        T, H, U = m.psum[0:2], m.psum[2:4], m.psum[4:6]
        X1_STORES = (32, 16)
        END = NCH - 1
        LOAD_AHEAD, LAST_BEHIND = 2, 4
        flat = lambda t: t.rearrange("p b d -> p (b d)")
        ctx.callback(sem.clear)
        block = ctx.enter_context(nc.Block())

        def chunks(eng, body):
            lo = 2 * 4
            hi = lo + (NCH - LOAD_AHEAD - lo) // 4 * 4
            for c in range(-LOAD_AHEAD, lo):
                body(c, c % 4)
            with eng.Fori(lo // 4, hi // 4) as j:
                for i in range(4):
                    body(j * 4 + i, i)
            for c in range(hi, NCH + LAST_BEHIND):
                body(c, c % 4)

        @block.sync
        def _(sp):
            def store(s, q, ready, name, buf, stored):
                if runs(s, 0, END):
                    hold(sp, ready, s + 1)
                    sp.dma_start(rows_of(m.tables[name], s), buf[:, q]).then_inc(stored[q], 16)

            def body(c, slot):
                q, o = slot % 2, 1 - slot % 2
                s = c + LOAD_AHEAD
                if runs(s, 0, END):
                    if runs(s, 4, END):
                        hold(sp, z1_ready, s - 3)
                    sp.dma_start(xc[:, (slot + LOAD_AHEAD) % 4], rows_of(io["x"], s))\
                        .then_inc(loaded[(slot + LOAD_AHEAD) % 4], 16)
                store(c - 2, q, g1_ready, "G1", g1, g1_stored)
                store(c - 4, q, x1_ready, "X1", x1, x1_stored)
                if q == 0:
                    store(c - 4, q, x1_ready, "X1_EVEN", x1, x1_stored)
            chunks(sp, body)
            for q in range(2):
                hold(sp, g1_stored[q], NCH // 2 * 16)
                hold(sp, x1_stored[q], NCH // 2 * X1_STORES[q])

        @block.gpsimd
        def _(pool):
            def body(c, slot):
                q = slot % 2
                if not runs(c, 0, END):
                    return
                hold(pool, idx_ready, c + 1)
                if runs(c, 2, END):
                    hold(pool, kept, c - 1)
                for t in range(2):
                    pool.indirect_dma_start(xs[:, q, t, :], None, io["x"],
                                            bass.IndirectOffsetOnAxis(ap=gi[:, q, 0, t:t + 1], axis=0))\
                        .then_inc(gathered[q], 16)
                    pool.indirect_dma_start(ds[:, q, t:t + 1], None, m.dinv_table,
                                            bass.IndirectOffsetOnAxis(ap=gi[:, q, 1, t:t + 1], axis=0))\
                        .then_inc(gathered[q], 16)
            chunks(pool, body)

        @block.tensor
        def _(pe):
            def body(c, slot):
                q, o = slot % 2, 1 - slot % 2
                s = c
                if runs(s, 0, END):
                    pe.wait_ge(loaded[slot], (s - slot) * 4 + 16)
                    if runs(s, 2, END):
                        pe.wait_ge(xT_copied, s - 1)
                    for j in range(BT):
                        last = pe.transpose(T[q][:, j * D:(j + 1) * D], xc[:, slot, j, :], m.ident[:, :])
                    last.then_inc(x_turned, 1)
                s = c - 1
                if runs(s, 0, END):
                    pe.wait_ge(hT_ready, s + 1)
                    if runs(s, 2, END):
                        pe.wait_ge(g1_ready, s - 1)
                    for j in range(BT):
                        last = pe.matmul(U[o][:, j * D:(j + 1) * D], hT[:, o, j * D:(j + 1) * D], m.w2[:, :],
                                         start=True, stop=True)
                    last.then_inc(hw2_done, 1)
                s = c
                if runs(s, 0, END):
                    pe.wait_ge(xT_copied, s + 1)
                    if runs(s, 2, END):
                        pe.wait_ge(hT_ready, s - 1)
                    pe.matmul(H[q][:, :], m.w1[:, :], xT[:, q, :], start=True, stop=True).then_inc(xw1_done, 1)
            chunks(pe, body)

        @block.scalar
        def _(act):
            def body(c, slot):
                q, o = slot % 2, 1 - slot % 2
                s = c - 2
                if runs(s, 0, END):
                    act.wait_ge(gathered[q], of_slot(s, q, 64))
                    act.activation(m.xd[:, bass.ds(s * (2 * D), 2 * D)], flat(xs[:, q]), ACT.Copy)
                    act.activation(at(m.ds_col, s, 2), ds[:, q, :], ACT.Copy).then_inc(kept, 1)
                s = c
                if runs(s, 0, END):
                    if runs(s, 2, END):
                        act.wait_ge(gathered[q], of_slot(s - 2, q, 64))
                    act.activation(gi[:, q, 0, :], at(m.dst_col, s, 2), ACT.Copy)
                    act.activation(gi[:, q, 1, :], at(m.src_col, s, 2), ACT.Copy).then_inc(idx_ready, 1)
                s = c
                if runs(s, 0, END):
                    act.wait_ge(x_turned, s + 1)
                    if runs(s, 2, END):
                        act.wait_ge(xw1_done, s - 1)
                    act.activation(xT[:, q, :], T[q][:, :], ACT.Copy).then_inc(xT_copied, 1)
                s = c - 1
                if runs(s, 0, END):
                    act.wait_ge(hw2_done, s + 1)
                    if runs(s, 2, END):
                        act.wait_ge(g1_stored[o], of_slot(s - 2, o, 16))
                        act.wait_ge(z1_ready, s - 1)
                    act.activation(flat(g1[:, o]), U[o][:, :], ACT.Copy).then_inc(g1_ready, 1)
                s = c - 3
                if runs(s, 0, END):
                    act.wait_ge(scale1_ready, s + 1)
                    if runs(s, 2, END):
                        act.wait_ge(x1_stored[o], of_slot(s - 2, o, X1_STORES[o]))
                    for j in range(BT):
                        last = act.activation(x1[:, o, j, :], z1[:, o, j, :], ACT.Identity,
                                              bias=shift1[:, o, j:j + 1], scale=scale1[:, o, j:j + 1])
                    last.then_inc(x1_ready, 1)
                s = c - 2
                if runs(s, 0, END):
                    act.wait_ge(mv1_ready, s + 1)
                    if runs(s, 1, END):
                        act.wait_ge(scale1_ready, s)
                    act.activation(sd1[:, :], mv1[:, :, 1], ACT.Sqrt, bias=m.eps[:, 0:1]).then_inc(sd1_ready, 1)
                s = c
                if runs(s, 0, END):
                    act.wait_ge(xw1_done, s + 1)
                    if runs(s, 2, END):
                        act.wait_ge(hw2_done, s - 1)
                    act.activation(hT[:, q, :], H[q][:, :], ACT.Relu, bias=m.b1[:, 0:1]).then_inc(hT_ready, 1)
            chunks(act, body)

        @block.vector
        def _(v):
            def scales(s, q):
                if not runs(s, 0, END):
                    return
                v.wait_ge(sd1_ready, s + 1)
                if runs(s, 2, END):
                    v.wait_ge(x1_ready, s - 1)
                v.reciprocal(scale1[:, q, :], sd1[:, :]).then_inc(scale_step, 1)
                v.wait_ge(scale_step, s + 1)
                v.scalar_tensor_tensor(out=shift1[:, q, :], in0=mv1[:, :, 0], scalar=-1.0, in1=scale1[:, q, :],
                                       op0=ALU.mult, op1=ALU.mult).then_inc(scale1_ready, 1)

            def layer0(s, slot):
                q = slot % 2
                if not runs(s, 0, END):
                    return
                v.wait_ge(loaded[slot], (s - slot) * 4 + 16)
                if runs(s, 1, END):
                    v.wait_ge(z1_ready, s)
                v.tensor_tensor(xb[:, :, :], xc[:, slot], m.b2_rows, ALU.add).then_inc(xb_ready, 1)
                v.wait_ge(xb_ready, s + 1)
                v.wait_ge(g1_ready, s + 1)
                if runs(s, 2, END):
                    v.wait_ge(x1_ready, s - 1)
                v.tensor_tensor(z1[:, q], g1[:, q], xb[:, :, :], ALU.add).then_inc(z1_ready, 1)
                v.wait_ge(z1_ready, s + 1)
                if runs(s, 1, END):
                    v.wait_ge(scale1_ready, s)
                row_stats(v, z1[:, q], (stats1, mv1), stats1_ready, s).then_inc(mv1_ready, 1)

            def body(c, slot):
                scales(c - 3, 1 - slot % 2)
                layer0(c - 2, (slot + 2) % 4)
            chunks(v, body)


def rows_of(table, chunk):
    return table.rearrange("(p r) d -> p r d", p=P)[:, bass.ds(chunk * BT, BT), :]


class DenseLayers:
    E2 = NB - 1

    def __init__(self, nc, m, sb, sem, banks, parity, source):
        pair = lambda n: [sem(n + "_even"), sem(n + "_odd")]
        self.m, self.Y, self.parity, self.source = m, banks, parity, source
        self.x1, self.x2, self.x3, self.x4 = (sb("dense_" + n, [P, 2, BT, D]) for n in ("x1", "x2", "x3", "x4"))
        self.x1T, self.z = sb("dense_x1T", [P, 2, BE]), sb("dense_z", [P, 2, BT, D])
        self.stats, self.mv = sb("dense_stats", [P, BT, 6]), sb("dense_mv", [P, BT, 2])
        self.var, self.sd = sb("dense_var", [P, 3, BT]), sb("dense_sd", [P, 3, BT])
        self.scale, self.shift = sb("dense_scale", [P, 2, 3, BT]), sb("dense_shift", [P, 2, 3, BT])
        self.loaded, self.x2_stored, self.x3_stored, self.x4_stored = (
            pair("dense_" + n) for n in ("loaded", "x2_stored", "x3_stored", "x4_stored"))
        self.turned, self.copied, self.root_done, self.z_ready, self.x2_ready, self.x3_ready, self.x4_ready = (
            sem("dense_" + n) for n in ("turned", "copied", "root_done", "z_ready", "x2_ready", "x3_ready",
                                        "x4_ready"))
        self.stats_ready, self.mv_ready, self.var_step, self.var_ready, self.sd_ready, self.scale_ready, self.shift_ready = (
            sem("dense_" + n) for n in ("stats_ready", "mv_ready", "var_step", "var_ready", "sd_ready",
                                        "scale_ready", "shift_ready"))

    def load(self, sp, s, q):
        if runs(s):
            if runs(s, 2):
                hold(sp, self.turned, s - 1)
            sp.dma_start(self.x1[:, q], rows_of(self.source, s * 2 + self.parity)).then_inc(self.loaded[q], 16)

    def store(self, sp, s, q, name, ready, rows, stored):
        if runs(s):
            hold(sp, ready, s + 1)
            sp.dma_start(rows_of(self.m.tables[name], s * 2 + self.parity), rows[:, q]).then_inc(stored[q], 16)

    def stores(self, sp, b, q):
        self.store(sp, b - 3, 1 - q, "X2", self.x2_ready, self.x2, self.x2_stored)
        self.store(sp, b - 3, 1 - q, "X3", self.x3_ready, self.x3, self.x3_stored)
        self.store(sp, b - 3, 1 - q, "OUT", self.x4_ready, self.x4, self.x4_stored)

    def all_stored(self, sp):
        for stored in (self.x2_stored, self.x3_stored, self.x4_stored):
            for q in range(2):
                hold(sp, stored[q], of_slot(self.E2 - (self.E2 - q) % 2, q, 16))

    def turn(self, pe, s, q):
        if runs(s):
            pe.wait_ge(self.loaded[q], of_slot(s, q, 16))
            if runs(s, 2):
                pe.wait_ge(self.z_ready, s - 1)
            for j in range(BT):
                last = pe.transpose(self.Y[q][:, j * D:(j + 1) * D], self.x1[:, q, j, :], self.m.ident[:, :])
            last.then_inc(self.turned, 1)

    def times_root(self, pe, s, q):
        if runs(s):
            pe.wait_ge(self.copied, s + 1)
            for j in range(BT):
                last = pe.matmul(self.Y[q][:, j * D:(j + 1) * D], self.x1T[:, q, j * D:(j + 1) * D],
                                 self.m.root1[:, :], start=True, stop=True)
            last.then_inc(self.root_done, 1)

    def columns(self, act, s, q):
        if runs(s):
            act.wait_ge(self.turned, s + 1)
            if runs(s, 2):
                act.wait_ge(self.root_done, s - 1)
            act.activation(self.x1T[:, q, :], self.Y[q][:, :], ACT.Copy).then_inc(self.copied, 1)

    def second_and_third(self, act, s, q):
        if runs(s):
            act.wait_ge(self.shift_ready, s + 1)
            for i, (rows, stored, ready) in enumerate(((self.x2, self.x2_stored, self.x2_ready),
                                                       (self.x3, self.x3_stored, self.x3_ready))):
                if runs(s, 2):
                    act.wait_ge(stored[q], of_slot(s - 2, q, 16))
                for j in range(BT):
                    last = act.activation(rows[:, q, j, :], self.z[:, q, j, :], ACT.Identity,
                                          bias=self.shift[:, q, i, j:j + 1], scale=self.scale[:, q, i, j:j + 1])
                last.then_inc(ready, 1)

    def roots(self, act, s):
        if runs(s):
            act.wait_ge(self.var_ready, s + 1)
            if runs(s, 1):
                act.wait_ge(self.scale_ready, s)
            act.activation(self.sd[:, :, :], self.var[:, :, :], ACT.Sqrt).then_inc(self.sd_ready, 1)

    def sum(self, v, s, q):
        if runs(s):
            v.wait_ge(self.root_done, s + 1)
            if runs(s, 2):
                v.wait_ge(self.x3_ready, s - 1)
                v.wait_ge(self.x4_ready, s - 1)
            v.tensor_tensor(self.z[:, q], self.Y[q][:, :].rearrange("p (b d) -> p b d", d=D), self.m.bias_rows,
                            ALU.add).then_inc(self.z_ready, 1)

    def variances(self, v, s, q):
        if runs(s):
            v.wait_ge(self.z_ready, s + 1)
            if runs(s, 1):
                v.wait_ge(self.shift_ready, s)
            row_stats(v, self.z[:, q], (self.stats, self.mv), self.stats_ready, s).then_inc(self.mv_ready, 1)
            v.wait_ge(self.mv_ready, s + 1)
            v.tensor_scalar(self.var[:, 0, :], self.mv[:, :, 1], EPS, None, ALU.add).then_inc(self.var_step, 1)
            for i in range(1, 3):
                v.wait_ge(self.var_step, s * 2 + i)
                v.scalar_tensor_tensor(out=self.var[:, i, :], in0=self.var[:, i - 1, :], scalar=EPS,
                                       in1=self.mv[:, :, 1], op0=ALU.mult, op1=ALU.add)\
                    .then_inc(self.var_step if i == 1 else self.var_ready, 1)

    def scales(self, v, s, q):
        if runs(s):
            v.wait_ge(self.sd_ready, s + 1)
            v.reciprocal(self.scale[:, q], self.sd[:, :, :]).then_inc(self.scale_ready, 1)

    def shifts(self, v, s, q):
        if runs(s):
            v.wait_ge(self.scale_ready, s + 1)
            v.scalar_tensor_tensor(out=self.shift[:, q], in0=self.mv[:, :, 0].unsqueeze(1).to_broadcast([P, 3, BT]),
                                   scalar=-1.0, in1=self.scale[:, q], op0=ALU.mult, op1=ALU.mult)\
                .then_inc(self.shift_ready, 1)

    def fourth(self, v, s, q):
        if runs(s):
            v.wait_ge(self.shift_ready, s + 1)
            if runs(s, 2):
                v.wait_ge(self.x4_stored[q], of_slot(s - 2, q, 16))
            for j in range(BT):
                last = v.tensor_scalar(self.x4[:, q, j, :], self.z[:, q, j, :], self.scale[:, q, 2, j:j + 1],
                                       self.shift[:, q, 2, j:j + 1], ALU.mult, ALU.add)
            last.then_inc(self.x4_ready, 1)


CONV1, CONV2, MEAN, ATTEND, SUM = "c1", "c2", "mean", "att", "sum"


def edge_stage(nc, io, m, kind, source, out, weights=None, n_rel=0):
    conv = kind in (CONV1, CONV2)
    MASKS = 8
    lag = 4 if kind == CONV1 else 3
    with ExitStack() as ctx:
        sb = lambda n, s, d=F32: ctx.enter_context(nc.sbuf_tensor(f"{kind}_{n}", s, d))
        sem = Semaphores(nc, f"{kind}_")
        pair = lambda n: [sem(n + "_even"), sem(n + "_odd")]
        flat = lambda t: t.rearrange("p b d -> p (b d)")
        wide = lambda t: t.rearrange("p (b d) -> p b d", d=D)
        gi = sb("gi", [P, 2, BT], I32)
        rows = sb("rows", [P, 2, BT, D])
        scaled = sb("scaled", [P, 2, BT, D]) if kind == CONV1 else rows
        same = sb("same", [P, 2, BE], BF16)
        if n_rel:
            typ = sb("typ", [P, 2, BE], BF16)
            wgt = sb("wgt", [P, 2, BE])
            col = sb("col", [P, 2, BE])
        masked = sb("masked", [P, MASKS, BE]) if n_rel else None
        run = sb("run", [P, 2, BE])
        if conv:
            t2, t3, y = (sb(n, [P, BT, D]) for n in ("t2", "t3", "y"))
            yT, hT = sb("yT", [P, BE]), sb("hT", [P, BE])
        z = sb("z", [P, 2, BT, D])
        norm = (sb("st", [P, BT, 6]), sb("mv", [P, BT, 2]))
        sd = sb("sd", [P, BT])
        scale, shift = sb("scale", [P, 2, BT]), sb("shift", [P, 2, BT])
        new = sb("new", [P, 2, BT, D])
        si = sb("si", [P, 2, BT], I32)
        w = sb("w", [P, n_rel, D]) if n_rel else None
        w_loaded = sem("w_loaded")
        gathered, scattered = sem.of_pool("gathered"), sem.of_pool("scattered")
        same_loaded, typ_loaded, wgt_loaded, col_loaded = (
            pair(n) for n in ("same_loaded", "typ_loaded", "wgt_loaded", "col_loaded"))
        idx_ready, scaled_ready, turned, col_ready, mask_ready, mask_used, related, scanned = (
            sem(n) for n in ("idx_ready", "scaled_ready", "turned", "col_ready", "mask_ready", "mask_used",
                             "related", "scanned"))
        rows_back, y_ready, y_turned, yT_copied, yw1_done, hT_ready, post_done, new_ready, xd_ready = (
            sem(n) for n in ("rows_back", "y_ready", "y_turned", "yT_copied", "yw1_done", "hT_ready",
                             "post_done", "new_ready", "xd_ready"))
        y_sum_ready, summed, stats_ready, scale_ready, t3_ready = (
            sem(n) for n in ("y_sum_ready", "summed", "stats_ready", "scale_ready", "t3_ready"))
        sums_used = y_sum_ready if kind == CONV1 else summed
        var_ready, sd_ready, shift_ready = sem("var_ready"), sem("sd_ready"), sem("shift_ready")
        T, H, B, S = m.psum[0:2], m.psum[2:4], m.psum[4:6], m.psum[6:8]
        E2 = NB - 1
        xd_at = lambda s: m.xd[:, bass.ds(s * BE, BE)]
        xd_of = lambda s, j: m.xd[:, bass.ds(s * BE + j * D, D)]
        dinv_of = lambda s, j: m.dinv_col[:, bass.ds(s * BT + j, 1)]
        if conv:
            dense = DenseLayers(nc, m, sb, sem, H, *((1, m.tables["X1"]) if kind == CONV1 else (0, m.tables["X1_EVEN"])))
        ctx.callback(sem.clear)
        block = ctx.enter_context(nc.Block())
        go = lambda eng, body: pipeline(eng, body, -2, NB + 3, 2, 4)

        @block.sync
        def _(sp):
            if n_rel:
                sp.dma_start(w[:, :, :], weights.rearrange("r i o -> i r o")).then_inc(w_loaded, 16)

            def spread(plane, s):
                return plane[bass.ds(s * BE, BE)].rearrange("(a n) -> a n", a=1).to_broadcast([P, BE])

            def body(b, q):
                s = b + 2
                if runs(s, 0, E2):
                    if n_rel:
                        if runs(s, 2):
                            hold(sp, mask_ready, (s - 1) * n_rel)
                        sp.dma_start(typ[:, q, :], spread(m.type_plane[n_rel], s)).then_inc(typ_loaded[q], 16)
                    if kind in (MEAN, ATTEND):
                        if runs(s, 2):
                            hold(sp, col_ready, s - 1)
                        plane = m.weight_plane if kind == MEAN else m.alpha_plane
                        sp.dma_start(wgt[:, q, :], spread(plane, s)).then_inc(wgt_loaded[q], 16)
                    if kind == ATTEND:
                        sp.dma_start(flat(rows[:, q]), m.source_columns[:, bass.ds(s * BE, BE)]).then_inc(col_loaded[q], 16)
                s = b + 1
                if runs(s, 0, E2):
                    if runs(s, 2):
                        hold(sp, scanned, s - 1)
                    sp.dma_start(same[:, 1 - q, :], spread(m.same_plane, s)).then_inc(same_loaded[1 - q], 16)
                if conv:
                    dense.load(sp, b + 2, q)
                    dense.stores(sp, b, q)
            go(sp, body)
            if conv:
                dense.all_stored(sp)

        @block.gpsimd
        def _(pool):
            def body(b, q):
                s = b + 2
                if kind != ATTEND and runs(s, 0, E2):
                    hold(pool, idx_ready, s + 1)
                    if runs(s, 2):
                        hold(pool, scaled_ready if kind == CONV1 else turned, s - 1)
                    for j in range(BT):
                        pool.indirect_dma_start(rows[:, q, j, :], None, source,
                                                bass.IndirectOffsetOnAxis(ap=gi[:, q, j:j + 1], axis=0))\
                            .then_inc(gathered[q], 16)
                s = b - lag
                qs = (q + lag) % 2
                if runs(s, 0, E2):
                    hold(pool, new_ready, s + 1)
                    for j in range(BT):
                        pool.indirect_dma_start(out, bass.IndirectOffsetOnAxis(ap=si[:, qs, j:j + 1], axis=0),
                                                new[:, qs, j, :], None, bounds_check=NP - 1, oob_is_err=False)\
                            .then_inc(scattered[qs], 16)
            go(pool, body)
            for q in range(2):
                hold(pool, scattered[q], of_slot(E2 - (E2 - q) % 2, q, 16 * BT))

        @block.scalar
        def _(act):
            def body(b, q):
                o = 1 - q
                s = b + 2
                if kind != ATTEND and runs(s, 0, E2):
                    if runs(s, 2):
                        act.wait_ge(gathered[q], of_slot(s - 2, q, 16 * BT))
                    act.activation(gi[:, q, :], at(m.src_col, s), ACT.Copy).then_inc(idx_ready, 1)
                if conv:
                    dense.roots(act, b - 2)
                s = b + 1
                if kind == CONV1 and runs(s, 0, E2):
                    act.wait_ge(gathered[o], of_slot(s, o, 16 * BT))
                    if runs(s, 2):
                        act.wait_ge(turned, s - 1)
                    for j in range(BT):
                        last = act.activation(scaled[:, o, j, :], rows[:, o, j, :], ACT.Copy,
                                              scale=m.ds_col[:, bass.ds(s * BT + j, 1)])
                    last.then_inc(scaled_ready, 1)
                if kind == SUM and runs(s, 0, E2):
                    act.wait_ge(turned, s + 1)
                    if runs(s, 2):
                        act.wait_ge(mask_ready, (s - 1) * n_rel)
                    act.activation(col[:, o, :], T[o][:, :], ACT.Copy).then_inc(col_ready, 1)
                s = b - 3
                if conv and runs(s, 0, E2):
                    act.wait_ge(y_turned, s + 1)
                    if runs(s, 1):
                        act.wait_ge(yw1_done if kind == CONV1 else post_done, s)
                    act.activation(yT[:, :], S[0][:, :], ACT.Copy).then_inc(yT_copied, 1)
                if conv:
                    dense.columns(act, b, q)
                s = b - 3
                if kind == CONV1 and runs(s, 0, E2):
                    act.wait_ge(yw1_done, s + 1)
                    if runs(s, 1):
                        act.wait_ge(post_done, s)
                    act.activation(hT[:, :], S[1][:, :], ACT.Relu, bias=m.b1[:, 0:1]).then_inc(hT_ready, 1)
                s = b - 2
                if kind != CONV1 and runs(s, 0, E2):
                    act.wait_ge(var_ready, s + 1)
                    if runs(s, 1):
                        act.wait_ge(shift_ready, s)
                    act.activation(sd[:, :], norm[1][:, :, 1], ACT.Sqrt, bias=m.eps[:, 0:1]).then_inc(sd_ready, 1)
                    if runs(s, 2):
                        act.wait_ge(scattered[q], of_slot(s - 2, q, 16 * BT))
                    if kind == CONV2 and runs(s, 2):
                        act.wait_ge(xd_ready, s - 1)
                    act.activation(si[:, q, :], at(m.last_col, s), ACT.Copy)
                    act.wait_ge(shift_ready, s + 1)
                    for j in range(BT):
                        last = act.activation(new[:, q, j, :], z[:, q, j, :], ACT.Identity,
                                              bias=shift[:, q, j:j + 1], scale=scale[:, q, j:j + 1])
                    last.then_inc(new_ready, 1)
                    if kind in (MEAN, ATTEND):
                        act.wait_ge(new_ready, s + 1)
                        act.activation(xd_at(s), flat(new[:, q]), ACT.Copy).then_inc(xd_ready, 1)
                if conv:
                    dense.second_and_third(act, b - 2, q)
                s = b - 3
                if kind == CONV1 and runs(s, 0, E2):
                    if runs(s, 2):
                        act.wait_ge(scattered[o], of_slot(s - 2, o, 16 * BT))
                        act.wait_ge(xd_ready, s - 1)
                    act.activation(si[:, o, :], at(m.last_col, s), ACT.Copy)
                    act.wait_ge(post_done, s + 1)
                    for j in range(BT):
                        last = act.activation(new[:, o, j, :], S[1][:, j * D:(j + 1) * D], ACT.Copy, scale=dinv_of(s, j))
                    last.then_inc(new_ready, 1)
            go(act, body)

        @block.tensor
        def _(pe):
            if n_rel:
                pe.wait_ge(w_loaded, 16)

            def back(s, q):
                if not runs(s, 0, E2):
                    return
                pe.wait_ge(scanned, s + 1)
                if runs(s, 2):
                    pe.wait_ge(sums_used, s - 1)
                for j in range(BT):
                    last = pe.transpose(B[q][:, j * D:(j + 1) * D], run[:, q, j * TE:(j + 1) * TE], m.ident[:, :])
                last.then_inc(rows_back, 1)

            def turn_product_rows(s, q):
                if not runs(s, 0, E2):
                    return
                pe.wait_ge(y_ready if kind == CONV1 else new_ready, s + 1)
                y_rows = y if kind == CONV1 else new[:, q]
                if runs(s, 1):
                    pe.wait_ge(yT_copied, s)
                for j in range(BT):
                    last = pe.transpose(S[0][:, j * TE:(j + 1) * TE], y_rows[:, j, :], m.ident[:, :])
                last.then_inc(y_turned, 1)

            def body(b, q):
                o = 1 - q
                if n_rel:
                    back(b - 2, q)
                if conv:
                    if kind == CONV2:
                        turn_product_rows(b - 3, o)
                    dense.times_root(pe, b - 1, o)
                    dense.turn(pe, b, q)
                s = b - 3
                if kind == CONV1 and runs(s, 0, E2):
                    pe.wait_ge(yT_copied, s + 1)
                    if runs(s, 1):
                        pe.wait_ge(new_ready, s)
                    pe.matmul(S[1][:, :], m.w1[:, :], yT[:, :], start=True, stop=True).then_inc(yw1_done, 1)
                s = b + 1
                if kind != ATTEND and runs(s, 0, E2):
                    if kind == CONV1:
                        pe.wait_ge(scaled_ready, s + 1)
                    else:
                        pe.wait_ge(gathered[o], of_slot(s, o, 16 * BT))
                    if runs(s, 2):
                        pe.wait_ge(scanned if conv else col_ready, s - 1)
                    for j in range(BT):
                        last = pe.transpose(T[o][:, j * TE:(j + 1) * TE], scaled[:, o, j, :], m.ident[:, :])
                    last.then_inc(turned, 1)
                s = b
                if n_rel and runs(s, 0, E2):
                    if runs(s, 2):
                        pe.wait_ge(scanned, s - 1)
                    for r in range(n_rel):
                        pe.wait_ge(mask_ready, s * n_rel + r + 1)
                        pe.matmul(H[q][:, :], w[:, r, :], masked[:, r % MASKS, :], start=(r == 0), stop=(r == n_rel - 1))\
                            .then_inc(mask_used, 1)
                s = b - 3
                if kind == CONV1 and runs(s, 0, E2):
                    pe.wait_ge(hT_ready, s + 1)
                    for j in range(BT):
                        last = pe.matmul(S[1][:, j * D:(j + 1) * D], hT[:, j * TE:(j + 1) * TE], m.w2[:, :],
                                         start=True, stop=True)
                    last.then_inc(post_done, 1)
                if conv:
                    back(b - 1, o)
                if kind == CONV1:
                    turn_product_rows(b - 2, q)
                s = b - 3
                if kind == CONV2 and runs(s, 0, E2):
                    pe.wait_ge(yT_copied, s + 1)
                    if runs(s, 1):
                        pe.wait_ge(xd_ready, s)
                    for j in range(BT):
                        last = pe.matmul(S[1][:, j * D:(j + 1) * D], yT[:, j * TE:(j + 1) * TE], m.root[:, :],
                                         start=True, stop=True)
                    last.then_inc(post_done, 1)
            go(pe, body)

        @block.vector
        def _(v):
            def prepare(s, q):
                if not runs(s, 0, E2):
                    return
                if kind == MEAN:
                    v.wait_ge(turned, s + 1)
                    v.wait_ge(wgt_loaded[q], of_slot(s, q, 16))
                    v.tensor_tensor(col[:, q, :], T[q][:, :], wgt[:, q, :], ALU.mult).then_inc(col_ready, 1)
                if kind == ATTEND:
                    v.wait_ge(wgt_loaded[q], of_slot(s, q, 16))
                    v.wait_ge(col_loaded[q], of_slot(s, q, 16))
                    v.tensor_tensor(col[:, q, :], flat(rows[:, q]), wgt[:, q, :], ALU.mult).then_inc(col_ready, 1)

            def relate(s, q, relations):
                if not runs(s, 0, E2):
                    return
                for r in relations:
                    if r == 0:
                        v.wait_ge(col_ready, s + 1)
                        v.wait_ge(typ_loaded[q], of_slot(s, q, 16))
                    if r >= MASKS or runs(s, 1):
                        v.wait_ge(mask_used, s * n_rel + r + 1 - MASKS)
                    v.scalar_tensor_tensor(out=masked[:, r % MASKS, :], in0=typ[:, q, :], scalar=float(r),
                                           in1=col[:, q, :], op0=ALU.is_equal, op1=ALU.mult).then_inc(mask_ready, 1)

            def scan(s, q):
                if not runs(s, 0, E2):
                    return
                v.wait_ge(same_loaded[q], of_slot(s, q, 16))
                if n_rel:
                    v.wait_ge(mask_used, (s + 1) * n_rel)
                    new_part = H[q][:, :]
                elif conv:
                    v.wait_ge(turned, s + 1)
                    new_part = T[q][:, :]
                else:
                    v.wait_ge(col_ready, s + 1)
                    new_part = col[:, q, :]
                if runs(s, 2):
                    v.wait_ge(rows_back, s - 1)
                if runs(s, 1):
                    v.wait_ge(scanned, s)
                start = 0.0 if static(s) and s == 0 else run[:, 1 - q, BE - 1:BE]
                v.tensor_tensor_scan(run[:, q, :], same[:, q, :], new_part, start, ALU.mult, ALU.add)\
                    .then_inc(scanned, 1)

            def update(s, q):
                if not runs(s, 0, E2):
                    return
                v.wait_ge(rows_back, s + 1)
                if kind == CONV1:
                    if runs(s, 1):
                        v.wait_ge(y_ready, s)
                    for j in range(BT):
                        last = v.scalar_tensor_tensor(out=t2[:, j, :], in0=xd_of(s, j), scalar=dinv_of(s, j),
                                                      in1=B[q][:, j * D:(j + 1) * D], op0=ALU.mult, op1=ALU.add)
                    last.then_inc(y_sum_ready, 1)
                    v.wait_ge(y_sum_ready, s + 1)
                    if runs(s, 1):
                        v.wait_ge(y_turned, s)
                    v.tensor_tensor(y[:, :, :], t2[:, :, :], bc(at(m.dinv_col, s), D), ALU.mult).then_inc(y_ready, 1)
                    return
                if runs(s, 2):
                    v.wait_ge(new_ready, s - 1)
                if kind == CONV2:
                    for j in range(BT):
                        last = v.scalar_tensor_tensor(out=z[:, q, j, :], in0=B[q][:, j * D:(j + 1) * D],
                                                      scalar=dinv_of(s, j), in1=xd_of(s, j), op0=ALU.mult, op1=ALU.add)
                    last.then_inc(summed, 1)
                elif kind == SUM:
                    v.scalar_tensor_tensor(out=flat(z[:, q]), in0=B[q][:, :], scalar=0.0, in1=xd_at(s),
                                           op0=ALU.max, op1=ALU.add).then_inc(summed, 1)
                else:
                    v.tensor_tensor(z[:, q], wide(B[q][:, :]), wide(xd_at(s)), ALU.add).then_inc(summed, 1)

            def statistics(s, q):
                if not runs(s, 0, E2):
                    return
                v.wait_ge(summed, s + 1)
                if runs(s, 1):
                    v.wait_ge(shift_ready, s)
                row_stats(v, z[:, q], norm, stats_ready, s).then_inc(var_ready, 1)

            def normalise(s, q):
                if kind == CONV1 or not runs(s, 0, E2):
                    return
                v.wait_ge(sd_ready, s + 1)
                v.reciprocal(scale[:, q, :], sd[:, :]).then_inc(scale_ready, 1)
                v.wait_ge(scale_ready, s + 1)
                v.scalar_tensor_tensor(out=shift[:, q, :], in0=norm[1][:, :, 0], scalar=-1.0, in1=scale[:, q, :],
                                       op0=ALU.mult, op1=ALU.mult).then_inc(shift_ready, 1)

            def prepare_next(s, q):
                if not runs(s, 0, E2):
                    return
                if runs(s, 1):
                    v.wait_ge(xd_ready, s)
                if kind == CONV1:
                    rows_now, bias = wide(xd_at(s)), m.b2_rows
                else:
                    v.wait_ge(new_ready, s + 1)
                    rows_now, bias = new[:, q], m.bias_rows
                v.tensor_tensor(t3[:, :, :], rows_now, bias, ALU.add).then_inc(t3_ready, 1)

            def finish(s, q):
                if not runs(s, 0, E2):
                    return
                v.wait_ge(t3_ready, s + 1)
                if kind == CONV1:
                    v.wait_ge(new_ready, s + 1)
                    for j in range(BT):
                        last = v.scalar_tensor_tensor(out=xd_of(s, j), in0=new[:, q, j, :], scalar=dinv_of(s, j),
                                                      in1=t3[:, j, :], op0=ALU.mult, op1=ALU.add)
                    last.then_inc(xd_ready, 1)
                else:
                    v.wait_ge(post_done, s + 1)
                    v.tensor_tensor(wide(xd_at(s)), wide(S[1][:, :]), t3[:, :, :], ALU.add).then_inc(xd_ready, 1)

            def body(b, q):
                o = 1 - q
                if conv:
                    prepare_next(b - 4, q)
                    scan(b - 1, o)
                    finish(b - 4, q)
                    update(b - 2, q)
                    dense.scales(v, b - 2, q)
                    dense.sum(v, b - 1, o)
                    dense.shifts(v, b - 2, q)
                    if kind == CONV2:
                        statistics(b - 2, q)
                    dense.fourth(v, b - 2, q)
                    if kind == CONV2:
                        normalise(b - 2, q)
                    dense.variances(v, b - 1, o)
                else:
                    prepare(b, q)
                    relate(b, q, range(0, n_rel // 4))
                    scan(b - 1, o)
                    relate(b, q, range(n_rel // 4, n_rel // 2))
                    update(b - 2, q)
                    relate(b, q, range(n_rel // 2, n_rel // 2 + 1))
                    statistics(b - 2, q)
                    relate(b, q, range(n_rel // 2 + 1, n_rel * 3 // 4))
                    normalise(b - 2, q)
                    relate(b, q, range(n_rel * 3 // 4, n_rel))
            go(v, body)


def attention_stage(nc, io, m):
    with ExitStack() as ctx:
        sb = lambda n, s, d=F32: ctx.enter_context(nc.sbuf_tensor("at_" + n, s, d))
        sem = Semaphores(nc, "at_")
        pair = lambda n: [sem(n + "_even"), sem(n + "_odd")]
        MASKS = 8
        gi = sb("gi", [P, 2, 2, BT], I32)
        rows = sb("rows", [P, 2, 2, BT, D])
        typ = sb("typ", [P, 2, BE], BF16)
        col = sb("col", [P, 2, 2, BE])
        masked = sb("masked", [P, MASKS, BE])
        prod = sb("prod", [P, 2, BE])
        w, wT, ww = (sb(n, [P, R8, D]) for n in ("w", "wT", "ww"))
        w_loaded, w_turned, wT_copied, ww_done, ww_copied = (
            sem(n) for n in ("w_loaded", "w_turned", "wT_copied", "ww_done", "ww_copied"))
        gathered, typ_loaded, stored = sem.of_pool("gathered"), pair("typ_loaded"), pair("stored")
        idx_ready, turned, col_ready, mask_ready, mask_used, prod_ready, scored, kept = (
            sem(n) for n in ("idx_ready", "turned", "col_ready", "mask_ready", "mask_used", "prod_ready", "scored",
                             "kept"))
        T, WB, U, SC = m.psum[0:2], m.psum[2:4], m.psum[4:6], m.psum[6:8]
        E2 = NB - 1
        ctx.callback(sem.clear)
        block = ctx.enter_context(nc.Block())
        go = lambda eng, body: pipeline(eng, body, -2, NB + 1, 2, 2)

        @block.sync
        def _(sp):
            sp.dma_start(w[:, :, :], io["W_att"].rearrange("r i o -> i r o")).then_inc(w_loaded, 16)

            def body(b, q):
                s = b + 2
                if runs(s, 0, E2):
                    if runs(s, 2):
                        hold(sp, mask_ready, (s - 1) * R8)
                    plane = m.type_plane[R8][bass.ds(s * BE, BE)]
                    sp.dma_start(typ[:, q, :], plane.rearrange("(a n) -> a n", a=1).to_broadcast([P, BE]))\
                        .then_inc(typ_loaded[q], 16)
                s = b
                if runs(s, 0, E2):
                    hold(sp, col_ready, s + 1)
                    sp.dma_start(m.source_columns[:, bass.ds(s * BE, BE)], col[:, q, 0, :]).then_inc(stored[q], 16)
            go(sp, body)
            for q in range(2):
                hold(sp, stored[q], of_slot(E2 - (E2 - q) % 2, q, 16))

        @block.gpsimd
        def _(pool):
            def body(b, q):
                s = b + 2
                if runs(s, 0, E2):
                    hold(pool, idx_ready, s + 1)
                    if runs(s, 2):
                        hold(pool, turned, s - 1)
                    for side in range(2):
                        for j in range(BT):
                            pool.indirect_dma_start(rows[:, q, side, j, :], None, m.tables["X2"],
                                                    bass.IndirectOffsetOnAxis(ap=gi[:, q, side, j:j + 1], axis=0))\
                                .then_inc(gathered[q], 16)
            go(pool, body)

        @block.scalar
        def _(act):
            act.wait_ge(w_turned, 1)
            for i in range(2):
                last = act.activation(wT[:, i * 4:(i + 1) * 4, :].rearrange("p r d -> p (r d)"), WB[i][:, :], ACT.Copy)
            last.then_inc(wT_copied, 1)
            act.wait_ge(ww_done, 1)
            for i in range(2):
                last = act.activation(ww[:, i * 4:(i + 1) * 4, :].rearrange("p r d -> p (r d)"), WB[i][:, :], ACT.Copy)
            last.then_inc(ww_copied, 1)

            def body(b, q):
                o = 1 - q
                s = b + 2
                if runs(s, 0, E2):
                    if runs(s, 2):
                        act.wait_ge(gathered[q], of_slot(s - 2, q, 32 * BT))
                    act.activation(gi[:, q, 0, :], at(m.src_col, s), ACT.Copy)
                    act.activation(gi[:, q, 1, :], at(m.dst_col, s), ACT.Copy).then_inc(idx_ready, 1)
                s = b - 2
                if runs(s, 0, E2):
                    act.wait_ge(scored, s + 1)
                    act.activation(at(m.score_col, s), SC[q][:, 0:BT], ACT.Copy).then_inc(kept, 1)
                s = b + 1
                if runs(s, 0, E2):
                    act.wait_ge(turned, s + 1)
                    if runs(s, 2):
                        act.wait_ge(prod_ready, s - 1)
                        act.wait_ge(stored[o], of_slot(s - 2, o, 16))
                    act.activation(col[:, o, 0, :], T[0][:, :], ACT.Copy)
                    act.activation(col[:, o, 1, :], T[1][:, :], ACT.Copy).then_inc(col_ready, 1)
            go(act, body)

        @block.tensor
        def _(pe):
            pe.wait_ge(w_loaded, 16)
            for r in range(R8):
                last = pe.transpose(WB[r // 4][:, (r % 4) * D:(r % 4 + 1) * D], w[:, r, :], m.ident[:, :])
            last.then_inc(w_turned, 1)
            pe.wait_ge(wT_copied, 1)
            for r in range(R8):
                last = pe.matmul(WB[r // 4][:, (r % 4) * D:(r % 4 + 1) * D], wT[:, r, :], wT[:, r, :],
                                 start=True, stop=True)
            last.then_inc(ww_done, 1)
            pe.wait_ge(ww_copied, 1)

            def relate(s, q, relations):
                if not runs(s, 0, E2):
                    return
                for r in relations:
                    if r == 0 and runs(s, 2):
                        pe.wait_ge(prod_ready, s - 1)
                    pe.wait_ge(mask_ready, s * R8 + r + 1)
                    pe.matmul(U[q][:, :], ww[:, r, :], masked[:, r % MASKS, :], start=(r == 0), stop=(r == R8 - 1))\
                        .then_inc(mask_used, 1)

            def body(b, q):
                o = 1 - q
                s = b - 2
                if runs(s, 0, E2):
                    pe.wait_ge(prod_ready, s + 1)
                    if runs(s, 2):
                        pe.wait_ge(kept, s - 1)
                    for j in range(BT):
                        last = pe.matmul(SC[q][:, j:j + 1], prod[:, q, j * TE:(j + 1) * TE], m.ones[:, 0:1],
                                         start=True, stop=True)
                    last.then_inc(scored, 1)
                relate(b, q, range(0, R8 // 2))
                s = b + 1
                if runs(s, 0, E2):
                    pe.wait_ge(gathered[o], of_slot(s, o, 32 * BT))
                    if runs(s, 1):
                        pe.wait_ge(col_ready, s)
                    for side in range(2):
                        for j in range(BT):
                            last = pe.transpose(T[side][:, j * TE:(j + 1) * TE], rows[:, o, side, j, :], m.ident[:, :])
                    last.then_inc(turned, 1)
                relate(b, q, range(R8 // 2, R8))
            go(pe, body)

        @block.vector
        def _(v):
            def relate(s, q, relations):
                if not runs(s, 0, E2):
                    return
                for r in relations:
                    if r == 0:
                        v.wait_ge(col_ready, s + 1)
                        v.wait_ge(typ_loaded[q], of_slot(s, q, 16))
                    if r >= MASKS or runs(s, 1):
                        v.wait_ge(mask_used, s * R8 + r + 1 - MASKS)
                    v.scalar_tensor_tensor(out=masked[:, r % MASKS, :], in0=typ[:, q, :], scalar=float(r),
                                           in1=col[:, q, 1, :], op0=ALU.is_equal, op1=ALU.mult).then_inc(mask_ready, 1)

            def body(b, q):
                o = 1 - q
                relate(b, q, range(0, R8 // 2))
                s = b - 1
                if runs(s, 0, E2):
                    v.wait_ge(mask_used, (s + 1) * R8)
                    if runs(s, 2):
                        v.wait_ge(scored, s - 1)
                    v.tensor_tensor(prod[:, o, :], col[:, o, 0, :], U[o][:, :], ALU.mult).then_inc(prod_ready, 1)
                relate(b, q, range(R8 // 2, R8))
            go(v, body)


def softmax_stage(nc, io, m):
    with ExitStack() as ctx:
        sb = lambda n, s, d=F32: ctx.enter_context(nc.sbuf_tensor("sm_" + n, s, d))
        sem = Semaphores(nc, "sm_")
        isrel = sb("isrel", [P, R8, KT])
        tmp = sb("tmp", [P, R8, KT])
        low = sb("low", [P, R8, KT])
        score = sb("score", [P, KT])
        best = sb("best", [P, R8])
        top = sb("top", [R8, 1])
        diag = sb("diag", [R8, R8])
        every = sb("every", [P, R8])
        own = sb("own", [P, KT])
        ex = sb("ex", [P, KT])
        part = sb("part", [P, R8])
        alpha = sb("alpha", [P, KT])
        turned = sb("turned", [QR, 2, TE])
        chain, ready, exped, pe_done, stored = (sem(n) for n in ("chain", "ready", "exped", "pe_done", "stored"))
        ps = m.psum
        ctx.callback(sem.clear)
        block = ctx.enter_context(nc.Block())

        @block.vector
        def _(v):
            n = [0]

            def link(ins):
                n[0] += 1
                ins.then_inc(chain, 1)
                v.wait_ge(chain, n[0])

            def over(col):
                return col.unsqueeze(1).to_broadcast([P, R8, KT])

            v.tensor_scalar(own[:, :], m.score_col[:, :], SLOPE, None, ALU.mult)
            for r in range(R8):
                last = v.tensor_scalar(isrel[:, r, :], m.type_col[:, :], float(r), None, ALU.is_equal)
            link(last)
            v.tensor_tensor(score[:, :], m.score_col[:, :], own[:, :], ALU.max)
            link(v.tensor_scalar(low[:, :, :], isrel[:, :, :], -LOW, LOW, ALU.mult, ALU.add))
            link(v.tensor_tensor(tmp[:, :, :], isrel[:, :, :], over(score[:, :]), ALU.mult))
            link(v.tensor_tensor(tmp[:, :, :], tmp[:, :, :], low[:, :, :], ALU.add))
            v.tensor_reduce(best[:, :], tmp[:, :, :], AX.X, ALU.max).then_inc(ready, 1)
            v.wait_ge(pe_done, 1)
            link(v.tensor_reduce(top[:, :], ps[0][0:R8, 0:P], AX.X, ALU.max))
            v.tensor_scalar(diag[:, :], m.ident[0:R8, 0:R8], top[:, 0:1], None, ALU.mult).then_inc(ready, 1)
            v.wait_ge(pe_done, 2)
            link(v.tensor_copy(every[:, :], ps[1][:, 0:R8]))
            link(v.tensor_tensor(tmp[:, :, :], isrel[:, :, :], bc(every[:, :], KT), ALU.mult))
            link(v.tensor_reduce(own[:, :], tmp[:, :, :].rearrange("p r k -> p k r"), AX.X, ALU.add))
            v.tensor_tensor(score[:, :], score[:, :], own[:, :], ALU.subtract).then_inc(ready, 1)
            v.wait_ge(exped, 1)
            link(v.tensor_tensor(tmp[:, :, :], isrel[:, :, :], over(ex[:, :]), ALU.mult))
            v.tensor_reduce(part[:, :], tmp[:, :, :], AX.X, ALU.add).then_inc(ready, 1)
            v.wait_ge(pe_done, 3)
            link(v.tensor_copy(every[:, :], ps[2][:, 0:R8]))
            link(v.tensor_tensor(tmp[:, :, :], isrel[:, :, :], bc(every[:, :], KT), ALU.mult))
            link(v.tensor_reduce(own[:, :], tmp[:, :, :].rearrange("p r k -> p k r"), AX.X, ALU.add))
            link(v.tensor_scalar(own[:, :], own[:, :], 1e-30, None, ALU.max))
            link(v.reciprocal(own[:, :], own[:, :]))
            v.tensor_tensor(alpha[:, :], ex[:, :], own[:, :], ALU.mult).then_inc(ready, 1)
            v.wait_ge(pe_done, 4)
            v.tensor_copy(turned[:, :, :].rearrange("q b e -> q (b e)"), ps[3][0:QR, 0:2 * TE]).then_inc(ready, 1)

        @block.scalar
        def _(act):
            act.wait_ge(ready, 3)
            act.activation(ex[:, :], score[:, :], ACT.Exp).then_inc(exped, 1)

        @block.tensor
        def _(pe):
            pe.wait_ge(ready, 1)
            pe.transpose(ps[0][0:R8, 0:P], best[:, :], m.ident[:, :]).then_inc(pe_done, 1)
            pe.wait_ge(ready, 2)
            pe.matmul(ps[1][:, 0:R8], m.ones[0:R8, :], diag[:, :], start=True, stop=True).then_inc(pe_done, 1)
            pe.wait_ge(ready, 4)
            pe.matmul(ps[2][:, 0:R8], m.ones[:, :], part[:, :], start=True, stop=True).then_inc(pe_done, 1)
            pe.wait_ge(ready, 5)
            for b in range(2):
                last = pe.transpose(ps[3][0:QR, b * TE:(b + 1) * TE], alpha[:, b * QR:(b + 1) * QR], m.ident[:, :])
            last.then_inc(pe_done, 1)

        @block.sync
        def _(sp):
            hold(sp, ready, 6)
            sp.dma_start(m.alpha_plane.rearrange("(b q n) -> q b n", b=2, n=TE), turned[:, :, :]).then_inc(stored, 16)
            hold(sp, stored, 16)


def build(nc, io):
    m = Memory()
    dram = lambda name, shape, dt=F32: nc.dram_tensor(name, shape, dt, kind="Internal").ap()
    m.tables = {"G1": dram("t_g1", (NP, D)), "X1": dram("t_x1", (NP, D)), "X1_EVEN": dram("t_x1_even", (NP, D)),
                "X2": dram("t_x2", (NP, D)),
                "X3": dram("t_x3", (NP, D)), "OUT": io["out"]}
    m.dinv_table = dram("t_dinv", (NP, 1))
    m.same_plane = dram("p_same", (EP,), BF16)
    m.type_plane = {R8: dram("p_type8", (EP,), BF16), R16: dram("p_type16", (EP,), BF16)}
    m.weight_plane = dram("p_weight", (EP,))
    m.alpha_plane = dram("p_alpha", (EP,))
    m.source_columns = dram("source_columns", (P, EP))
    m.records = dram("records", (EP, 4), I32)
    m.sorted_dst = dram("sorted_dst", (EP,), I32)
    with ExitStack() as ctx:
        sb = lambda n, s, d=F32: ctx.enter_context(nc.sbuf_tensor("m_" + n, s, d))
        m.psum = [ctx.enter_context(nc.psum_tensor(f"bank{i}", [P, 512], F32)) for i in range(8)]
        m.ident, m.ones, m.iota = sb("ident", [P, P]), sb("ones", [P, P]), sb("iota", [P, RPP])
        m.eps = sb("eps", [P, 1])
        m.w1, m.w2, m.root, m.root1 = (sb(n, [P, D]) for n in ("w1", "w2", "root", "root1"))
        m.b1, m.b2, m.bias = sb("b1", [P, 1]), sb("b2", [P, D]), sb("bias", [P, D])
        m.b2_rows, m.bias_rows = (t[:, :].unsqueeze(1).to_broadcast([P, BT, D]) for t in (m.b2, m.bias))
        column = lambda name: sb(name + "_col", [P, KT])
        m.src_col, m.dst_col, m.last_col, m.dinv_col, m.type_col = map(column, ("src", "dst", "last", "dinv", "type"))
        m.dstraw_col, m.hi_col, m.lo_col, m.ds_col, m.score_col = map(column, ("dstraw", "hi", "lo", "ds", "score"))
        m.dst_int, m.hi_int, m.lo_int = (sb(n, [P, KT], I32) for n in ("dst_int", "hi_int", "lo_int"))
        m.xd = sb("xd", [P, KT * D])
        m.halo = sb("halo", [QR, 258], I32)
        m.rows = sb("rows", [QR, 4, 256], I32)
        constants_stage(nc, m)
        order_stage(nc, io, m)
        setup_stage(nc, io, m)
        degree_stage(nc, io, m)
        prefill_stage(nc, io, m)
        edge_stage(nc, io, m, CONV1, io["x"], m.tables["G1"])
        edge_stage(nc, io, m, CONV2, m.tables["G1"], m.tables["X1"])
        edge_stage(nc, io, m, MEAN, m.tables["X1"], m.tables["X2"], io["W_mean"], R8)
        attention_stage(nc, io, m)
        softmax_stage(nc, io, m)
        edge_stage(nc, io, m, ATTEND, None, m.tables["X3"], io["W_att"], R8)
        edge_stage(nc, io, m, SUM, m.tables["X3"], m.tables["OUT"], io["W_sum"], R16)


def kernel(x, src, dst, edge_type_16, edge_type_8, L0_gnn_W1, L0_gnn_b1, L0_gnn_W2, L0_gnn_b2,
           L1_gnn_W, L1_gnn_root, L1_gnn_bias, L2_gnn_W, L3_gnn_weight):
    import numpy as np
    import concourse.bacc as bacc
    from concourse.bass_utils import run_bass_kernel_spmd

    def padded(a, n, fill):
        a = np.asarray(a)
        return np.concatenate([a, np.full((n - a.shape[0],) + a.shape[1:], fill, a.dtype)])

    arrays = {
        "x": padded(x, NP, 0),
        "edges": np.stack([padded(src, EP, PAD_SRC), padded(dst, EP, PAD_DST),
                           padded(edge_type_8, EP, PAD_TYPE), padded(edge_type_16, EP, PAD_TYPE)]),
        "W1": np.asarray(L0_gnn_W1), "b1": np.asarray(L0_gnn_b1),
        "W2": np.asarray(L0_gnn_W2), "b2": np.asarray(L0_gnn_b2),
        "W_mean": np.asarray(L1_gnn_W), "root": np.asarray(L1_gnn_root), "bias": np.asarray(L1_gnn_bias),
        "W_att": np.asarray(L2_gnn_W), "W_sum": np.asarray(L3_gnn_weight),
    }
    arrays = {k + "_dram": np.ascontiguousarray(a) for k, a in arrays.items()}
    nc = bacc.Bacc("TRN2", target_bir_lowering=False, num_devices=1)
    io = {k[:-5]: nc.dram_tensor(k, a.shape, mybir.dt.from_np(a.dtype), kind="ExternalInput").ap()
          for k, a in arrays.items()}
    io["out"] = nc.dram_tensor("out_dram", (NP, D), F32, kind="ExternalOutput").ap()
    build(nc, io)
    got = run_bass_kernel_spmd(nc, [arrays], core_ids=[0])
    return got.results[0]["out_dram"][:N]
```

```python
from contextlib import ExitStack

import concourse.bass as bass
from concourse import mybir
from concourse.alu_op_type import AluOpType as ALU

F32 = mybir.dt.float32
BF16 = mybir.dt.bfloat16
F16 = mybir.dt.float16
I32 = mybir.dt.int32
ACT = mybir.ActivationFunctionType
AX = mybir.AxisListType

N, D, E = 50000, 128, 25000
P = 128
TE = P
BT = 4
BE = BT * TE
NB = -(-E // BE)
EP = NB * BE
KT = EP // TE
RPP = -(-N // (P * BT)) * BT
NP = P * RPP
NCH = RPP // BT
QR = EP // 256
R8, R16 = 8, 16
FAR = 65536
PAD_DST, PAD_SRC, PAD_TYPE = 60000, 0, -1
EPS = 1e-5
SLOPE = 0.2
LOW = -1.0e30
SRC, DST, T8, T16 = range(4)


def static(b):
    return isinstance(b, int)


def runs(b, first=0, last=NB - 1):
    return not static(b) or first <= b <= last


def bc(ap, width):
    return ap.rearrange("p (n o) -> p n o", o=1).to_broadcast([ap.shape[0], ap.shape[1], width])


def hold(eng, sem, value):
    eng.wait_ge(sem, value)
    if not static(value):
        eng.nop(nofuse=True)


def of_slot(b, q, inc):
    return (b - q) * (inc // 2) + inc


def pipeline(eng, body, first, last, ahead, behind):
    lo = behind + 2 + (behind % 2)
    hi = NB - ahead
    hi -= (hi - lo) % 2
    for b in range(first, lo):
        body(b, b % 2)
    with eng.Fori(lo // 2, hi // 2) as pair:
        body(pair * 2, 0)
        body(pair * 2 + 1, 1)
    for b in range(hi, last + 1):
        body(b, b % 2)


class Semaphores:

    def __init__(self, nc, prefix):
        self.nc, self.prefix, self.mine = nc, prefix, []

    def __call__(self, name):
        self.mine.append(self.nc.alloc_semaphore(self.prefix + name))
        return self.mine[-1]

    def of_pool(self, name):
        return [self.nc.alloc_semaphore(f"{self.prefix}{name}_{slot}") for slot in ("even", "odd")]

    def clear(self):
        with self.nc.Block() as block:
            @block.gpsimd
            def _(pool):
                for s in self.mine:
                    pool.sem_clear(s)
        for s in self.mine:
            self.nc.release_semaphore(s)


class Memory:
    pass


def at(col, b, n=BT):
    return col[:, bass.ds(b * n, n)]


def constants_stage(nc, m):
    with ExitStack() as ctx:
        sem = Semaphores(nc, "co_")
        consts = sem("consts")
        ctx.callback(sem.clear)
        block = ctx.enter_context(nc.Block())

        @block.gpsimd
        def _(pool):
            pool.memset(m.ident[:, :], 0.0).then_inc(consts, 1)
            hold(pool, consts, 1)
            pool.affine_select(out=m.ident[:, :], in_=m.ident[:, :], compare_op=ALU.not_equal, fill=1.0,
                               base=0, pattern=[[-1, P]], channel_multiplier=1).then_inc(consts, 1)
            pool.iota(m.iota[:, :], pattern=[[1, RPP]], base=0, channel_multiplier=0,
                      allow_small_or_imprecise_dtypes=True).then_inc(consts, 1)
            pool.memset(m.ones[:, :], 1.0).then_inc(consts, 1)
            pool.memset(m.eps[:, :], EPS).then_inc(consts, 1)


def order_stage(nc, io, m):
    with ExitStack() as ctx:
        sb = lambda n, s, d=F32: ctx.enter_context(nc.sbuf_tensor("or_" + n, s, d))
        sem = Semaphores(nc, "or_")
        halof = sb("halof", [QR, 257])
        falls = sb("falls", [QR, 256])
        fell = sb("fell", [QR, 1])
        unsorted = sb("unsorted", [1, 1], I32)
        rowf = sb("rowf", [QR, 4, 256])
        col = sb("col", [P, 4, KT])
        number = sb("number", [P, KT])
        place = sb("place", [P, KT])
        others = sb("others", [P, BE], I32)
        othersf = sb("othersf", [P, BE])
        numbers = sb("numbers", [P, BE])
        less, equal, before = (sb(n, [P, BT, BE]) for n in ("less", "equal", "before"))
        count = sb("count", [P, BT])
        record = sb("record", [P, 4], I32)
        where = sb("where", [P, 1], I32)
        packed = sb("packed", [QR, 256, 4], I32)
        loaded, prep, counted, flagged, turned = (
            sem(n) for n in ("loaded", "prep", "counted", "flagged", "turned"))
        spread, used, numbered, staged, sorted_rows, unpacked, halo_set = (
            sem(n) for n in ("spread", "used", "numbered", "staged", "sorted_rows", "unpacked", "halo_set"))
        placed, vc = sem.of_pool("placed")[0], sem("chain")
        edges, halo, rows, ps = io["edges"], m.halo, m.rows, m.psum
        ctx.callback(sem.clear)
        block = ctx.enter_context(nc.Block())

        def neighbours(sp, dst, done):
            with nc.allow_non_contiguous_dma(reason="one element per partition"):
                sp.dma_start(halo[1:QR, 0:1], dst[255:EP - 1:256].rearrange("(q n) -> q n", n=1)).then_inc(done, 16)
                sp.dma_start(halo[0:QR - 1, 257:258], dst[256:EP:256].rearrange("(q n) -> q n", n=1)).then_inc(done, 16)

        def out_of_order(eng):
            eng.wait_ge(flagged, 1)
            return eng.value_load(unsorted[0:1, 0:1], min_val=0, max_val=1) > 0

        @block.sync
        def _(sp):
            sp.wait_ge(prep, 1)
            neighbours(sp, edges[DST, :], loaded)
            sp.dma_start(halo[:, 1:257], edges[DST, :].rearrange("(q n) -> q n", n=256)).then_inc(loaded, 16)
            for f in range(4):
                sp.dma_start(rows[:, f, :], edges[f, :].rearrange("(q n) -> q n", n=256)).then_inc(loaded, 16)
            sp.wait_ge(loaded, 16 * 7)
            with sp.If(out_of_order(sp)):
                with sp.Fori(0, NB) as b:
                    hold(sp, used, b + 1)
                    sp.dma_start(others[:, :], edges[DST, bass.ds(b * BE, BE)].rearrange("(a n) -> a n", a=1)
                                 .to_broadcast([P, BE])).then_inc(spread, 16)
                sp.wait_ge(placed, 16 * KT)
                sp.dma_start(packed[:, :, :], m.records.rearrange("(q n) f -> q n f", n=256)).then_inc(sorted_rows, 16)
                sp.wait_ge(unpacked, 1)
                sp.dma_start(m.sorted_dst.rearrange("(q n) -> q n", n=256), rows[:, DST, :]).then_inc(sorted_rows, 16)
                sp.wait_ge(sorted_rows, 32)
                neighbours(sp, m.sorted_dst, halo_set)
                sp.wait_ge(halo_set, 32)

        @block.gpsimd
        def _(pool):
            pool.iota(number[:, :], pattern=[[TE, KT]], base=0, channel_multiplier=1,
                      allow_small_or_imprecise_dtypes=True).then_inc(numbered, 1)
            pool.iota(numbers[:, :], pattern=[[1, BE]], base=0, channel_multiplier=0,
                      allow_small_or_imprecise_dtypes=True).then_inc(numbered, 1)
            with pool.If(out_of_order(pool)):
                with pool.Fori(0, KT) as k:
                    hold(pool, staged, k + 1)
                    pool.indirect_dma_start(m.records, bass.IndirectOffsetOnAxis(ap=where[:, 0:1], axis=0),
                                            record[:, :], None, bounds_check=EP - 1, oob_is_err=False)\
                        .then_inc(placed, 16)

        @block.tensor
        def _(pe):
            pe.wait_ge(counted, 1)
            pe.matmul(ps[0][0:1, 0:1], fell[:, :], m.ones[0:QR, 0:1], start=True, stop=True).then_inc(turned, 1)
            with pe.If(out_of_order(pe)):
                pe.wait_ge(counted, 2)
                for f in range(4):
                    for b in range(2):
                        last = pe.transpose(ps[1 + f][:, b * QR:(b + 1) * QR], rowf[:, f, b * TE:(b + 1) * TE],
                                            m.ident[0:QR, 0:QR])
                last.then_inc(turned, 1)

        @block.vector
        def _(v):
            n = [0]

            def link(ins):
                n[0] += 1
                ins.then_inc(vc, 1)
                v.wait_ge(vc, n[0])

            v.memset(halo[:, 257:258], FAR)
            v.memset(halo[:, 0:1], -1).then_inc(prep, 1)
            v.wait_ge(loaded, 16 * 7)
            link(v.tensor_copy(halof[:, :], halo[:, 1:258]))
            link(v.tensor_tensor(falls[:, :], halof[:, 1:257], halof[:, 0:256], ALU.is_lt))
            v.tensor_reduce(fell[:, :], falls[:, :], AX.X, ALU.add).then_inc(counted, 1)
            v.wait_ge(turned, 1)
            v.tensor_scalar(unsorted[:, :], ps[0][0:1, 0:1], 0.0, None, ALU.is_gt).then_inc(flagged, 1)
            with v.If(out_of_order(v)):
                v.tensor_copy(rowf[:, :, :], rows[:, :, :]).then_inc(counted, 1)
                v.wait_ge(turned, 2)
                for f in range(4):
                    v.tensor_copy(col[:, f, :].rearrange("p (q b) -> p b q", b=2),
                                  ps[1 + f][:, 0:2 * QR].rearrange("p (b q) -> p b q", b=2))
                v.wait_ge(numbered, 2)
                v.memset(place[:, :], 0.0)
                v.drain()
                v.tensor_copy(count[:, :], place[:, 0:BT]).then_inc(used, 1)
                wide_others = othersf[:, :].unsqueeze(1).to_broadcast([P, BT, BE])
                wide_numbers = numbers[:, :].unsqueeze(1).to_broadcast([P, BT, BE])
                with v.Fori(0, NB) as b:
                    hold(v, spread, b * 16 + 16)
                    v.tensor_copy(othersf[:, :], others[:, :])
                    v.drain()
                    v.tensor_copy(count[:, :], place[:, 0:BT]).then_inc(used, 1)
                    with v.Fori(0, NB) as own:
                        dst = bc(col[:, DST, bass.ds(own * BT, BT)], BE)
                        v.drain()
                        v.tensor_tensor(less[:, :, :], wide_others, dst, ALU.is_lt)
                        v.tensor_tensor(equal[:, :, :], wide_others, dst, ALU.is_equal)
                        v.tensor_tensor(before[:, :, :], wide_numbers, bc(at(number, own), BE), ALU.is_lt)
                        v.drain()
                        v.tensor_tensor(equal[:, :, :], equal[:, :, :], before[:, :, :], ALU.mult)
                        v.drain()
                        v.tensor_tensor(less[:, :, :], less[:, :, :], equal[:, :, :], ALU.add)
                        v.drain()
                        v.tensor_reduce(count[:, :], less[:, :, :], AX.X, ALU.add)
                        v.drain()
                        v.tensor_tensor(at(place, own), at(place, own), count[:, :], ALU.add)
                    v.drain()
                    v.tensor_scalar(numbers[:, :], numbers[:, :], float(BE), None, ALU.add)
                    v.drain()
                with v.Fori(0, KT) as k:
                    v.tensor_copy(where[:, :], place[:, bass.ds(k, 1)])
                    v.tensor_copy(record[:, :], col[:, :, bass.ds(k, 1)].rearrange("p f o -> p (f o)")).then_inc(staged, 1)
                    hold(v, placed, k * 16 + 16)
                v.wait_ge(sorted_rows, 16)
                v.tensor_copy(rows[:, :, :], packed[:, :, :].rearrange("q n f -> q f n")).then_inc(unpacked, 1)
                v.wait_ge(unpacked, 1)
                v.tensor_copy(halo[:, 1:257], rows[:, DST, :])
                v.drain()


def setup_stage(nc, io, m):
    with ExitStack() as ctx:
        sb = lambda n, s, d=F32: ctx.enter_context(nc.sbuf_tensor("su_" + n, s, d))
        sem = Semaphores(nc, "su_")
        halo, rows = m.halo, m.rows
        rowf = sb("rowf", [QR, 4, 256])
        dstf = sb("dstf", [QR, 258])
        same = sb("same", [QR, 256])
        nxt = sb("nxt", [QR, 256])
        flag = sb("flag", [QR, 2, 256])
        through = sb("through", [QR, 2, 256])
        zero = sb("zero", [QR, 256])
        relid = sb("relid", [QR, R8 + 1, 256])
        cnt = sb("cnt", [QR, 2, R8 + 1, 256])
        ends = sb("ends", [QR, 2, 2, R8 + 1])
        endT = sb("endT", [R8 + 1, 2, 2, QR])
        carryT = sb("carryT", [R8 + 1, 2, QR + 1])
        carry = sb("carry", [QR, 2, R8 + 1])
        field = sb("field", [QR, 7, 256])
        typ = sb("typ", [QR, 3, 256], BF16)
        own = sb("own", [QR, 256])
        root_of = sb("root_of", [QR, 256])
        rooted = sem("rooted")
        ps = m.psum
        lin, prep = sem("lin"), sem("prep")
        tr, back, colT, colC, stored = sem("tr"), sem("back"), sem("colT"), sem("colC"), sem("stored")
        wl = sem("wl")
        vc = sem("chain")
        SRC_F, CL_F, LAST_F, DINV_F, T8_F, DST_F, WEIGHT_F = range(7)
        col_bank = lambda f: ps[(2 + f) % 8]
        ctx.callback(sem.clear)
        block = ctx.enter_context(nc.Block())

        @block.sync
        def _(sp):
            for dst, src in ((m.w1, io["W1"]), (m.w2, io["W2"]), (m.root, io["root"])):
                sp.dma_start(dst[:, :], src).then_inc(wl, 16)
            sp.dma_start(m.b1[:, :], io["b1"].rearrange("(p n) -> p n", n=1)).then_inc(wl, 16)
            for dst, src in ((m.b2, io["b2"]), (m.bias, io["bias"])):
                sp.dma_start(dst[:, :], src.rearrange("(a n) -> a n", a=1).to_broadcast([P, D])).then_inc(wl, 16)
            hold(sp, lin, 1)
            for f, plane in enumerate((m.same_plane, m.type_plane[R8], m.type_plane[R16])):
                sp.dma_start(plane.rearrange("(q n) -> q n", n=256), typ[:, f, :]).then_inc(stored, 16)
            hold(sp, stored, 48)
            hold(sp, wl, 96)

        @block.vector
        def _(v):
            n = [0]

            def link(ins):
                n[0] += 1
                ins.then_inc(vc, 1)
                v.wait_ge(vc, n[0])

            v.memset(zero[:, :], 0.0)
            v.memset(carryT[:, :, :], 0.0)
            link(v.memset(relid[:, R8, :], 1.0))
            v.tensor_copy(dstf[:, :], halo[:, :])
            link(v.tensor_copy(rowf[:, :, :], rows[:, :, :]))
            v.tensor_tensor(same[:, :], dstf[:, 1:257], dstf[:, 0:256], ALU.is_equal)
            link(v.tensor_tensor(nxt[:, :], dstf[:, 1:257], dstf[:, 2:258], ALU.is_equal))
            v.tensor_copy(typ[:, 0, :], same[:, :])
            v.tensor_copy(typ[:, 1:3, :], rowf[:, T8:T16 + 1, :]).then_inc(lin, 1)
            v.tensor_copy(flag[:, 0, :], same[:, :])
            v.tensor_copy(flag[:, 1, :], nxt[:, :])
            v.tensor_copy(field[:, SRC_F, :], rowf[:, SRC, :])
            v.tensor_copy(field[:, T8_F, :], rowf[:, T8, :])
            v.tensor_copy(field[:, DST_F, :], rowf[:, DST, :])
            v.tensor_scalar(field[:, CL_F, :], rowf[:, DST, :], float(N - 1), None, ALU.min)
            v.scalar_tensor_tensor(out=field[:, LAST_F, :], in0=nxt[:, :], scalar=float(FAR), in1=rowf[:, DST, :],
                                   op0=ALU.mult, op1=ALU.add)
            for r in range(R8):
                last = v.tensor_scalar(relid[:, r, :], rowf[:, T8, :], float(r), None, ALU.is_equal)
            link(last)
            v.memset(flag[:, 0, 0:1], 0.0)
            link(v.memset(flag[:, 1, 255:256], 0.0))
            v.tensor_tensor_scan(through[:, 0, :], same[:, :], zero[:, :], 1.0, ALU.mult, ALU.max)
            v.tensor_tensor_scan(through[:, 1, ::-1], nxt[:, ::-1], zero[:, :], 1.0, ALU.mult, ALU.max)
            for r in range(R8 + 1):
                v.tensor_tensor_scan(cnt[:, 0, r, :], flag[:, 0, :], relid[:, r, :], 0.0, ALU.mult, ALU.add)
                last = v.tensor_tensor_scan(cnt[:, 1, r, ::-1], flag[:, 1, ::-1], relid[:, r, ::-1], 0.0,
                                            ALU.mult, ALU.add)
            link(last)
            v.tensor_copy(ends[:, 0, 0, :], cnt[:, 0, :, 255])
            v.tensor_copy(ends[:, 1, 0, :], cnt[:, 1, :, 0])
            v.tensor_copy(ends[:, 0, 1, :], through[:, 0, 255:256].to_broadcast([QR, R8 + 1]))
            v.tensor_copy(ends[:, 1, 1, :], through[:, 1, 0:1].to_broadcast([QR, R8 + 1])).then_inc(prep, 1)
            v.wait_ge(tr, 1)
            link(v.tensor_copy(endT[:, :, :, :].rearrange("r a b q -> r (a b q)"), ps[0][0:R8 + 1, 0:4 * QR]))
            v.tensor_tensor_scan(carryT[:, 0, 1:QR + 1], endT[:, 0, 1, :], endT[:, 0, 0, :], 0.0, ALU.mult, ALU.add)
            v.tensor_tensor_scan(carryT[:, 1, QR - 1::-1], endT[:, 1, 1, ::-1], endT[:, 1, 0, ::-1], 0.0,
                                 ALU.mult, ALU.add).then_inc(prep, 1)
            v.wait_ge(back, 1)
            link(v.tensor_copy(carry[:, :, :].rearrange("q a r -> q (a r)"), ps[1][0:QR, 0:2 * (R8 + 1)]))
            for d in range(2):
                for r in range(R8 + 1):
                    last = v.scalar_tensor_tensor(out=cnt[:, d, r, :], in0=through[:, d, :], scalar=carry[:, d, r:r + 1],
                                                  in1=cnt[:, d, r, :], op0=ALU.mult, op1=ALU.add)
            link(last)
            v.tensor_tensor(cnt[:, 0, :, :], cnt[:, 0, :, :], cnt[:, 1, :, :], ALU.add).then_inc(prep, 1)
            v.wait_ge(prep, 3)
            v.wait_ge(rooted, 1)
            v.reciprocal(field[:, DINV_F, :], root_of[:, :])
            link(v.tensor_tensor(cnt[:, 1, 0:R8, :], cnt[:, 0, 0:R8, :], relid[:, 0:R8, :], ALU.mult))
            link(v.tensor_reduce(own[:, :], cnt[:, 1, 0:R8, :].rearrange("q r n -> q n r"), AX.X, ALU.add))
            link(v.tensor_scalar(own[:, :], own[:, :], -1.0, None, ALU.add))
            v.reciprocal(field[:, WEIGHT_F, :], own[:, :]).then_inc(lin, 1)
            for f, col in ((SRC_F, m.src_col), (CL_F, m.dst_col), (LAST_F, m.last_col),
                           (DINV_F, m.dinv_col), (T8_F, m.type_col), (DST_F, m.dstraw_col),
                           (WEIGHT_F, m.weight_col)):
                v.wait_ge(colT, f + 1)
                v.tensor_copy(col[:, :].rearrange("p (q b) -> p b q", b=2),
                              col_bank(f)[:, 0:2 * QR].rearrange("p (b q) -> p b q", b=2)).then_inc(colC, 1)
            v.wait_ge(colC, 7)
            link(v.tensor_copy(m.dst_int[:, :], m.dstraw_col[:, :]))
            v.tensor_scalar(m.hi_int[:, :], m.dst_int[:, :], 7, None, ALU.arith_shift_right)
            link(v.tensor_scalar(m.lo_int[:, :], m.dst_int[:, :], 127, None, ALU.bitwise_and))
            v.tensor_copy(m.hi_col[:, :], m.hi_int[:, :])
            v.tensor_copy(m.lo_col[:, :], m.lo_int[:, :])

        @block.scalar
        def _(act):
            act.wait_ge(prep, 3)
            act.activation(root_of[:, :], cnt[:, 0, R8, :], ACT.Sqrt).then_inc(rooted, 1)

        @block.tensor
        def _(pe):
            pe.wait_ge(prep, 1)
            for i in range(4):
                last = pe.transpose(ps[0][0:R8 + 1, i * QR:(i + 1) * QR], ends[:, i // 2, i % 2, :], m.ident[0:QR, 0:QR])
            last.then_inc(tr, 1)
            pe.wait_ge(prep, 2)
            pe.transpose(ps[1][0:QR, 0:R8 + 1], carryT[:, 0, 0:QR], m.ident[0:R8 + 1, 0:R8 + 1])
            pe.transpose(ps[1][0:QR, R8 + 1:2 * (R8 + 1)], carryT[:, 1, 1:QR + 1],
                         m.ident[0:R8 + 1, 0:R8 + 1]).then_inc(back, 1)
            pe.wait_ge(lin, 2)
            for f in range(7):
                for b in range(2):
                    last = pe.transpose(col_bank(f)[:, b * QR:(b + 1) * QR], field[:, f, b * TE:(b + 1) * TE],
                                        m.ident[0:QR, 0:QR])
                last.then_inc(colT, 1)


def row_stats(v, z, norm, chain, base):
    stats, mv = norm
    for j in range(BT):
        last = v.bn_stats(stats[:, j, :], z[:, j, :])
    last.then_inc(chain, 1)
    hold(v, chain, base + 1)
    for j in range(BT):
        last = v.bn_aggr(mv[:, j, :], stats[:, j, :])
    return last


def prefill_stage(nc, io, m):
    with ExitStack() as ctx:
        sb = lambda n, s, d=F32: ctx.enter_context(nc.sbuf_tensor("pf_" + n, s, d))
        sem = Semaphores(nc, "pf_")
        pair = lambda n: [sem(n + "_even"), sem(n + "_odd")]
        xc = sb("xc", [P, 4, BT, D])
        xT, hT = (sb(n, [P, 2, BE]) for n in ("xT", "hT"))
        g1, z1, x1 = (sb(n, [P, 2, BT, D]) for n in ("g1", "z1", "x1"))
        xb = sb("xb", [P, BT, D])
        stats1, mv1 = sb("stats1", [P, BT, 6]), sb("mv1", [P, BT, 2])
        sd1 = sb("sd1", [P, BT])
        scale1, shift1 = sb("scale1", [P, 2, BT]), sb("shift1", [P, 2, BT])
        gi = sb("gi", [P, 2, BT], I32)
        xs = sb("xs", [P, 2, BT, D])
        ds = sb("ds", [P, 2, BT])
        number = sb("number", [P, RPP], F16)
        low_is, high_is = sb("low_is", [P, 8, P], F16), sb("high_is", [P, 8, RPP], F16)
        root_of, dinv = sb("root_of", [P, RPP]), sb("dinv", [P, RPP])
        dinv_rows = sb("dinv_rows", [RPP // 4, 4, P])
        loaded, gathered = [sem(f"loaded_{i}") for i in range(4)], sem.of_pool("gathered")
        g1_stored, x1_stored = pair("g1_stored"), pair("x1_stored")
        x_turned, xT_copied, xw1_done, hT_ready, hw2_done, g1_ready, xb_ready, z1_ready, x1_ready = (
            sem(n) for n in ("x_turned", "xT_copied", "xw1_done", "hT_ready", "hw2_done", "g1_ready", "xb_ready",
                             "z1_ready", "x1_ready"))
        stats1_ready, scale_step, mv1_ready, sd1_ready, scale1_ready, idx_ready, kept = (
            sem(n) for n in ("stats1_ready", "scale_step", "mv1_ready", "sd1_ready", "scale1_ready", "idx_ready",
                             "kept"))
        numbered, onehot_ready, counted, rooted, dinv_ready, dinv_turned, dinv_copied, dinv_stored = (
            sem(n) for n in ("numbered", "onehot_ready", "counted", "rooted", "dinv_ready", "dinv_turned",
                             "dinv_copied", "dinv_stored"))
        T, H, U, COUNTS, TURNED = m.psum[0:2], m.psum[2:4], m.psum[4:6], m.psum[6], m.psum[7]
        HALF = NCH // 2
        HB = RPP // 4
        X1_STORES = (32, 16)
        END = NCH - 1
        LOAD_AHEAD, LAST_BEHIND = 2, 4
        flat = lambda t: t.rearrange("p b d -> p (b d)")
        ctx.callback(sem.clear)
        block = ctx.enter_context(nc.Block())

        def chunks(eng, body):
            lo = 2 * 4
            turn = HALF // 4 * 4
            again = turn + 4
            hi = again + (NCH - LOAD_AHEAD - again) // 4 * 4
            for c in range(-LOAD_AHEAD, lo):
                body(c, c % 4, True)
            with eng.Fori(lo // 4, turn // 4) as j:
                for i in range(4):
                    body(j * 4 + i, i, True)
            for c in range(turn, again):
                body(c, c % 4, c < HALF)
            with eng.Fori(again // 4, hi // 4) as j:
                for i in range(4):
                    body(j * 4 + i, i, False)
            for c in range(hi, NCH + LAST_BEHIND):
                body(c, c % 4, False)

        def looked_up(s, now_first):
            return s >= HALF if static(s) else not now_first

        @block.sync
        def _(sp):
            def store(s, q, ready, name, buf, stored):
                if runs(s, 0, END):
                    hold(sp, ready, s + 1)
                    sp.dma_start(rows_of(m.tables[name], s), buf[:, q]).then_inc(stored[q], 16)

            def body(c, slot, first_half):
                q = slot % 2
                s = c + LOAD_AHEAD
                if runs(s, 0, END):
                    if runs(s, 4, END):
                        hold(sp, z1_ready, s - 3)
                    sp.dma_start(xc[:, (slot + LOAD_AHEAD) % 4], rows_of(io["x"], s))\
                        .then_inc(loaded[(slot + LOAD_AHEAD) % 4], 16)
                store(c - 2, q, g1_ready, "G1", g1, g1_stored)
                store(c - 4, q, x1_ready, "X1", x1, x1_stored)
                if q == 0:
                    store(c - 4, q, x1_ready, "X1_EVEN", x1, x1_stored)
                if static(c) and c == HALF + 1:
                    hold(sp, dinv_copied, 1)
                    sp.dma_start(m.dinv_table.rearrange("(g p l) o -> p g (l o)", g=4, l=P), dinv_rows[:, :, :])\
                        .then_inc(dinv_stored, 16)
            chunks(sp, body)
            for q in range(2):
                hold(sp, g1_stored[q], NCH // 2 * 16)
                hold(sp, x1_stored[q], NCH // 2 * X1_STORES[q])

        @block.gpsimd
        def _(pool):
            def body(c, slot, first_half):
                q = slot % 2
                if not runs(c, 0, END):
                    return
                hold(pool, idx_ready, c + 1)
                if runs(c, 2, END):
                    hold(pool, kept, c - 1)
                if static(c) and c == HALF:
                    hold(pool, dinv_stored, 16)
                for j in range(BT):
                    index = bass.IndirectOffsetOnAxis(ap=gi[:, q, j:j + 1], axis=0)
                    if first_half:
                        pool.indirect_dma_start(xs[:, q, j, :], None, io["x"], index).then_inc(gathered[q], 16)
                    else:
                        pool.indirect_dma_start(ds[:, q, j:j + 1], None, m.dinv_table, index).then_inc(gathered[q], 16)
            chunks(pool, body)

        @block.tensor
        def _(pe):
            def body(c, slot, first_half):
                q, o = slot % 2, 1 - slot % 2
                s = c
                if runs(s, 0, END):
                    pe.wait_ge(loaded[slot], (s - slot) * 4 + 16)
                    if runs(s, 2, END):
                        pe.wait_ge(xT_copied, s - 1)
                    for j in range(BT):
                        last = pe.transpose(T[q][:, j * D:(j + 1) * D], xc[:, slot, j, :], m.ident[:, :])
                    last.then_inc(x_turned, 1)
                s = c - 1
                if runs(s, 0, END):
                    pe.wait_ge(hT_ready, s + 1)
                    if runs(s, 2, END):
                        pe.wait_ge(g1_ready, s - 1)
                    for j in range(BT):
                        last = pe.matmul(U[o][:, j * D:(j + 1) * D], hT[:, o, j * D:(j + 1) * D], m.w2[:, :],
                                         start=True, stop=True)
                    last.then_inc(hw2_done, 1)
                s = c
                if first_half and runs(s, 0, END):
                    pe.wait_ge(onehot_ready, s + 1)
                    for j in range(BT):
                        k = (slot % 2) * BT + j
                        last = pe.matmul(COUNTS[:, 0:RPP], low_is[:, k, :], high_is[:, k, :],
                                         start=static(s) and s == 0 and j == 0,
                                         stop=static(s) and s == HALF - 1 and j == BT - 1, skip_group_check=True)
                    last.then_inc(counted, 1)
                if static(c) and c == HALF:
                    pe.wait_ge(dinv_ready, 1)
                    for g in range(4):
                        last = pe.transpose(TURNED[0:HB, g * P:(g + 1) * P], dinv[:, g * HB:(g + 1) * HB], m.ident[:, :])
                    last.then_inc(dinv_turned, 1)
                s = c
                if runs(s, 0, END):
                    pe.wait_ge(xT_copied, s + 1)
                    if runs(s, 2, END):
                        pe.wait_ge(hT_ready, s - 1)
                    pe.matmul(H[q][:, :], m.w1[:, :], xT[:, q, :], start=True, stop=True).then_inc(xw1_done, 1)
            chunks(pe, body)

        @block.scalar
        def _(act):
            def body(c, slot, first_half):
                q, o = slot % 2, 1 - slot % 2
                s = c - 2
                if runs(s, 0, END):
                    act.wait_ge(gathered[q], of_slot(s, q, 64))
                    if looked_up(s, first_half):
                        act.activation(at(m.ds_col, s - HALF), ds[:, q, :], ACT.Copy).then_inc(kept, 1)
                    else:
                        act.activation(m.xd[:, bass.ds(s * BE, BE)], flat(xs[:, q]), ACT.Copy).then_inc(kept, 1)
                s = c
                if runs(s, 0, END):
                    if runs(s, 2, END):
                        act.wait_ge(gathered[q], of_slot(s - 2, q, 64))
                    tiles = at(m.dst_col, s) if first_half else at(m.src_col, s - HALF)
                    act.activation(gi[:, q, :], tiles, ACT.Copy).then_inc(idx_ready, 1)
                s = c
                if runs(s, 0, END):
                    act.wait_ge(x_turned, s + 1)
                    if runs(s, 2, END):
                        act.wait_ge(xw1_done, s - 1)
                    act.activation(xT[:, q, :], T[q][:, :], ACT.Copy).then_inc(xT_copied, 1)
                s = c - 1
                if runs(s, 0, END):
                    act.wait_ge(hw2_done, s + 1)
                    if runs(s, 2, END):
                        act.wait_ge(g1_stored[o], of_slot(s - 2, o, 16))
                        act.wait_ge(z1_ready, s - 1)
                    act.activation(flat(g1[:, o]), U[o][:, :], ACT.Copy).then_inc(g1_ready, 1)
                s = c - 3
                if runs(s, 0, END):
                    act.wait_ge(scale1_ready, s + 1)
                    if runs(s, 2, END):
                        act.wait_ge(x1_stored[o], of_slot(s - 2, o, X1_STORES[o]))
                    for j in range(BT):
                        last = act.activation(x1[:, o, j, :], z1[:, o, j, :], ACT.Identity,
                                              bias=shift1[:, o, j:j + 1], scale=scale1[:, o, j:j + 1])
                    last.then_inc(x1_ready, 1)
                s = c - 2
                if runs(s, 0, END):
                    act.wait_ge(mv1_ready, s + 1)
                    if runs(s, 1, END):
                        act.wait_ge(scale1_ready, s)
                    act.activation(sd1[:, :], mv1[:, :, 1], ACT.Sqrt, bias=m.eps[:, 0:1]).then_inc(sd1_ready, 1)
                if static(c) and c == HALF:
                    act.wait_ge(counted, HALF)
                    act.activation(root_of[:, :], COUNTS[:, 0:RPP], ACT.Sqrt, bias=m.ones[:, 0:1]).then_inc(rooted, 1)
                s = c
                if runs(s, 0, END):
                    act.wait_ge(xw1_done, s + 1)
                    if runs(s, 2, END):
                        act.wait_ge(hw2_done, s - 1)
                    act.activation(hT[:, q, :], H[q][:, :], ACT.Relu, bias=m.b1[:, 0:1]).then_inc(hT_ready, 1)
            chunks(act, body)

        @block.vector
        def _(v):
            v.tensor_tensor(m.root1[:, :], m.root[:, :], m.ident[:, :], ALU.add)
            v.tensor_copy(number[:, :], m.iota[:, :]).then_inc(numbered, 1)
            v.wait_ge(numbered, 1)

            def one_hot(s, q):
                if runs(s, 2):
                    v.wait_ge(counted, s - 1)
                for j in range(BT):
                    k = q * BT + j
                    v.tensor_scalar(low_is[:, k, :], number[:, 0:P], m.lo_col[:, bass.ds(s * BT + j, 1)], None,
                                    ALU.is_equal)
                    last = v.tensor_scalar(high_is[:, k, :], number[:, :], m.hi_col[:, bass.ds(s * BT + j, 1)], None,
                                           ALU.is_equal)
                last.then_inc(onehot_ready, 1)

            def scales(s, q):
                if not runs(s, 0, END):
                    return
                v.wait_ge(sd1_ready, s + 1)
                if runs(s, 2, END):
                    v.wait_ge(x1_ready, s - 1)
                v.reciprocal(scale1[:, q, :], sd1[:, :]).then_inc(scale_step, 1)
                v.wait_ge(scale_step, s + 1)
                v.scalar_tensor_tensor(out=shift1[:, q, :], in0=mv1[:, :, 0], scalar=-1.0, in1=scale1[:, q, :],
                                       op0=ALU.mult, op1=ALU.mult).then_inc(scale1_ready, 1)

            def layer0(s, slot):
                q = slot % 2
                if not runs(s, 0, END):
                    return
                v.wait_ge(loaded[slot], (s - slot) * 4 + 16)
                if runs(s, 1, END):
                    v.wait_ge(z1_ready, s)
                v.tensor_tensor(xb[:, :, :], xc[:, slot], m.b2_rows, ALU.add).then_inc(xb_ready, 1)
                v.wait_ge(xb_ready, s + 1)
                v.wait_ge(g1_ready, s + 1)
                if runs(s, 2, END):
                    v.wait_ge(x1_ready, s - 1)
                v.tensor_tensor(z1[:, q], g1[:, q], xb[:, :, :], ALU.add).then_inc(z1_ready, 1)
                v.wait_ge(z1_ready, s + 1)
                if runs(s, 1, END):
                    v.wait_ge(scale1_ready, s)
                row_stats(v, z1[:, q], (stats1, mv1), stats1_ready, s).then_inc(mv1_ready, 1)

            def body(c, slot, first_half):
                scales(c - 3, 1 - slot % 2)
                layer0(c - 2, (slot + 2) % 4)
                if first_half and runs(c + 1, 0, HALF - 1):
                    one_hot(c + 1, 1 - slot % 2)
                if static(c) and c == HALF:
                    v.wait_ge(rooted, 1)
                    v.reciprocal(dinv[:, :], root_of[:, :]).then_inc(dinv_ready, 1)
                    v.wait_ge(dinv_turned, 1)
                    v.tensor_copy(dinv_rows[:, :, :].rearrange("p a b -> p (a b)"), TURNED[0:HB, 0:4 * P])\
                        .then_inc(dinv_copied, 1)
            chunks(v, body)


def rows_of(table, chunk):
    return table.rearrange("(p r) d -> p r d", p=P)[:, bass.ds(chunk * BT, BT), :]


class DenseLayers:
    def __init__(self, m, sb, sem, banks, parity, source):
        pair = lambda n: [sem(n + "_even"), sem(n + "_odd")]
        self.m, self.Y, self.parity, self.source = m, banks, parity, source
        self.x1, self.x2, self.x3, self.x4 = (sb("dense_" + n, [P, 2, BT, D]) for n in ("x1", "x2", "x3", "x4"))
        self.x1T, self.z = sb("dense_x1T", [P, 2, BE]), sb("dense_z", [P, 2, BT, D])
        self.stats, self.mv = sb("dense_stats", [P, BT, 6]), sb("dense_mv", [P, BT, 2])
        self.var, self.sd = sb("dense_var", [P, 3, BT]), sb("dense_sd", [P, 3, BT])
        self.scale, self.shift = sb("dense_scale", [P, 2, 3, BT]), sb("dense_shift", [P, 2, 3, BT])
        self.loaded, self.x2_stored, self.x3_stored, self.x4_stored = (
            pair("dense_" + n) for n in ("loaded", "x2_stored", "x3_stored", "x4_stored"))
        self.turned, self.copied, self.root_done, self.z_ready, self.x2_ready, self.x3_ready, self.x4_ready = (
            sem("dense_" + n) for n in ("turned", "copied", "root_done", "z_ready", "x2_ready", "x3_ready",
                                        "x4_ready"))
        self.stats_ready, self.mv_ready, self.var_step, self.var_ready, self.sd_ready, self.scale_ready, self.shift_ready = (
            sem("dense_" + n) for n in ("stats_ready", "mv_ready", "var_step", "var_ready", "sd_ready",
                                        "scale_ready", "shift_ready"))

    def load(self, sp, s, q):
        if runs(s):
            if runs(s, 2):
                hold(sp, self.turned, s - 1)
            sp.dma_start(self.x1[:, q], rows_of(self.source, s * 2 + self.parity)).then_inc(self.loaded[q], 16)

    def store(self, sp, s, q, name, ready, rows, stored):
        if runs(s):
            hold(sp, ready, s + 1)
            sp.dma_start(rows_of(self.m.tables[name], s * 2 + self.parity), rows[:, q]).then_inc(stored[q], 16)

    def stores(self, sp, b, q):
        self.store(sp, b - 3, 1 - q, "X2", self.x2_ready, self.x2, self.x2_stored)
        self.store(sp, b - 3, 1 - q, "X3", self.x3_ready, self.x3, self.x3_stored)
        self.store(sp, b - 3, 1 - q, "OUT", self.x4_ready, self.x4, self.x4_stored)

    def all_stored(self, sp):
        for stored in (self.x2_stored, self.x3_stored, self.x4_stored):
            for q in range(2):
                hold(sp, stored[q], of_slot(NB - 1 - (NB - 1 - q) % 2, q, 16))

    def turn(self, pe, s, q):
        if runs(s):
            pe.wait_ge(self.loaded[q], of_slot(s, q, 16))
            if runs(s, 2):
                pe.wait_ge(self.z_ready, s - 1)
            for j in range(BT):
                last = pe.transpose(self.Y[q][:, j * D:(j + 1) * D], self.x1[:, q, j, :], self.m.ident[:, :])
            last.then_inc(self.turned, 1)

    def times_root(self, pe, s, q):
        if runs(s):
            pe.wait_ge(self.copied, s + 1)
            for j in range(BT):
                last = pe.matmul(self.Y[q][:, j * D:(j + 1) * D], self.x1T[:, q, j * D:(j + 1) * D],
                                 self.m.root1[:, :], start=True, stop=True)
            last.then_inc(self.root_done, 1)

    def columns(self, act, s, q):
        if runs(s):
            act.wait_ge(self.turned, s + 1)
            if runs(s, 2):
                act.wait_ge(self.root_done, s - 1)
            act.activation(self.x1T[:, q, :], self.Y[q][:, :], ACT.Copy).then_inc(self.copied, 1)

    def second_and_third(self, act, s, q):
        if runs(s):
            act.wait_ge(self.shift_ready, s + 1)
            for i, (rows, stored, ready) in enumerate(((self.x2, self.x2_stored, self.x2_ready),
                                                       (self.x3, self.x3_stored, self.x3_ready))):
                if runs(s, 2):
                    act.wait_ge(stored[q], of_slot(s - 2, q, 16))
                for j in range(BT):
                    last = act.activation(rows[:, q, j, :], self.z[:, q, j, :], ACT.Identity,
                                          bias=self.shift[:, q, i, j:j + 1], scale=self.scale[:, q, i, j:j + 1])
                last.then_inc(ready, 1)

    def roots(self, act, s):
        if runs(s):
            act.wait_ge(self.var_ready, s + 1)
            if runs(s, 1):
                act.wait_ge(self.scale_ready, s)
            act.activation(self.sd[:, :, :], self.var[:, :, :], ACT.Sqrt).then_inc(self.sd_ready, 1)

    def sum(self, v, s, q):
        if runs(s):
            v.wait_ge(self.root_done, s + 1)
            if runs(s, 2):
                v.wait_ge(self.x3_ready, s - 1)
                v.wait_ge(self.x4_ready, s - 1)
            v.tensor_tensor(self.z[:, q], self.Y[q][:, :].rearrange("p (b d) -> p b d", d=D), self.m.bias_rows,
                            ALU.add).then_inc(self.z_ready, 1)

    def variances(self, v, s, q):
        if runs(s):
            v.wait_ge(self.z_ready, s + 1)
            if runs(s, 1):
                v.wait_ge(self.shift_ready, s)
            row_stats(v, self.z[:, q], (self.stats, self.mv), self.stats_ready, s).then_inc(self.mv_ready, 1)
            v.wait_ge(self.mv_ready, s + 1)
            v.tensor_scalar(self.var[:, 0, :], self.mv[:, :, 1], EPS, None, ALU.add).then_inc(self.var_step, 1)
            for i in range(1, 3):
                v.wait_ge(self.var_step, s * 2 + i)
                v.scalar_tensor_tensor(out=self.var[:, i, :], in0=self.var[:, i - 1, :], scalar=EPS,
                                       in1=self.mv[:, :, 1], op0=ALU.mult, op1=ALU.add)\
                    .then_inc(self.var_step if i == 1 else self.var_ready, 1)

    def scales(self, v, s, q):
        if runs(s):
            v.wait_ge(self.sd_ready, s + 1)
            v.reciprocal(self.scale[:, q], self.sd[:, :, :]).then_inc(self.scale_ready, 1)

    def shifts(self, v, s, q):
        if runs(s):
            v.wait_ge(self.scale_ready, s + 1)
            v.scalar_tensor_tensor(out=self.shift[:, q], in0=self.mv[:, :, 0].unsqueeze(1).to_broadcast([P, 3, BT]),
                                   scalar=-1.0, in1=self.scale[:, q], op0=ALU.mult, op1=ALU.mult)\
                .then_inc(self.shift_ready, 1)

    def fourth(self, v, s, q):
        if runs(s):
            v.wait_ge(self.shift_ready, s + 1)
            if runs(s, 2):
                v.wait_ge(self.x4_stored[q], of_slot(s - 2, q, 16))
            for j in range(BT):
                last = v.tensor_scalar(self.x4[:, q, j, :], self.z[:, q, j, :], self.scale[:, q, 2, j:j + 1],
                                       self.shift[:, q, 2, j:j + 1], ALU.mult, ALU.add)
            last.then_inc(self.x4_ready, 1)


CONV1, CONV2, MEAN, ATTEND, SUM = "c1", "c2", "mean", "att", "sum"


def edge_stage(nc, io, m, kind, source, out, weights=None, n_rel=0):
    conv = kind in (CONV1, CONV2)
    MASKS = 8
    lag = 4 if kind == CONV1 else 3
    with ExitStack() as ctx:
        sb = lambda n, s, d=F32: ctx.enter_context(nc.sbuf_tensor(f"{kind}_{n}", s, d))
        sem = Semaphores(nc, f"{kind}_")
        pair = lambda n: [sem(n + "_even"), sem(n + "_odd")]
        flat = lambda t: t.rearrange("p b d -> p (b d)")
        wide = lambda t: t.rearrange("p (b d) -> p b d", d=D)
        gi = sb("gi", [P, 2, BT], I32)
        rows = sb("rows", [P, 2, BT, D])
        factor = {CONV1: m.ds_col, MEAN: m.weight_col, ATTEND: m.alpha_col}.get(kind)
        scaled = sb("scaled", [P, 2, BT, D]) if factor is not None else rows
        same = sb("same", [P, 2, BE], BF16)
        if n_rel:
            typ = sb("typ", [P, 2, BE], BF16)
            col = sb("col", [P, 2, BE])
        masked = sb("masked", [P, MASKS, BE]) if n_rel else None
        run = sb("run", [P, 2, BE])
        if conv:
            y_sum, y = sb("y_sum", [P, BT, D]), sb("y", [P, BT, D])
            biased = sb("biased", [P, BT, D])
            yT, hT = sb("yT", [P, BE]), sb("hT", [P, BE])
        z = sb("z", [P, 2, BT, D])
        norm = (sb("st", [P, BT, 6]), sb("mv", [P, BT, 2]))
        sd = sb("sd", [P, BT])
        scale, shift = sb("scale", [P, 2, BT]), sb("shift", [P, 2, BT])
        new = sb("new", [P, 2, BT, D])
        si = sb("si", [P, 2, BT], I32)
        w = sb("w", [P, n_rel, D]) if n_rel else None
        w_loaded = sem("w_loaded")
        gathered, scattered = sem.of_pool("gathered"), sem.of_pool("scattered")
        same_loaded, typ_loaded, rows_loaded = (pair(n) for n in ("same_loaded", "typ_loaded", "rows_loaded"))
        idx_ready, scaled_ready, turned, col_ready, mask_ready, mask_used, scanned = (
            sem(n) for n in ("idx_ready", "scaled_ready", "turned", "col_ready", "mask_ready", "mask_used",
                             "scanned"))
        rows_back, y_ready, y_turned, yT_copied, yw1_done, hT_ready, post_done, new_ready, xd_ready = (
            sem(n) for n in ("rows_back", "y_ready", "y_turned", "yT_copied", "yw1_done", "hT_ready",
                             "post_done", "new_ready", "xd_ready"))
        y_sum_ready, summed, stats_ready, scale_ready, biased_ready = (
            sem(n) for n in ("y_sum_ready", "summed", "stats_ready", "scale_ready", "biased_ready"))
        sums_used = y_sum_ready if kind == CONV1 else summed
        var_ready, sd_ready, shift_ready = sem("var_ready"), sem("sd_ready"), sem("shift_ready")
        T, H, B, S = m.psum[0:2], m.psum[2:4], m.psum[4:6], m.psum[6:8]
        LAST = NB - 1
        xd_at = lambda s: m.xd[:, bass.ds(s * BE, BE)]
        xd_of = lambda s, j: m.xd[:, bass.ds(s * BE + j * D, D)]
        dinv_of = lambda s, j: m.dinv_col[:, bass.ds(s * BT + j, 1)]
        if kind == CONV1:
            dense = DenseLayers(m, sb, sem, H, 1, m.tables["X1"])
        if kind == CONV2:
            dense = DenseLayers(m, sb, sem, H, 0, m.tables["X1_EVEN"])
        ctx.callback(sem.clear)
        block = ctx.enter_context(nc.Block())
        go = lambda eng, body: pipeline(eng, body, -2, NB + 3, 2, 4)

        @block.sync
        def _(sp):
            if n_rel:
                sp.dma_start(w[:, :, :], weights.rearrange("r i o -> i r o")).then_inc(w_loaded, 16)

            def spread(plane, s):
                return plane[bass.ds(s * BE, BE)].rearrange("(a n) -> a n", a=1).to_broadcast([P, BE])

            def body(b, q):
                s = b + 2
                if runs(s, 0, LAST):
                    if n_rel:
                        if runs(s, 2):
                            hold(sp, mask_ready, (s - 1) * n_rel)
                        sp.dma_start(typ[:, q, :], spread(m.type_plane[n_rel], s)).then_inc(typ_loaded[q], 16)
                    if kind == ATTEND:
                        if runs(s, 2):
                            hold(sp, scaled_ready, s - 1)
                        sp.dma_start(flat(rows[:, q]), m.source_rows[:, bass.ds(s * BE, BE)]).then_inc(rows_loaded[q], 16)
                s = b + 1
                if runs(s, 0, LAST):
                    if runs(s, 2):
                        hold(sp, scanned, s - 1)
                    sp.dma_start(same[:, 1 - q, :], spread(m.same_plane, s)).then_inc(same_loaded[1 - q], 16)
                if conv:
                    dense.load(sp, b + 2, q)
                    dense.stores(sp, b, q)
            go(sp, body)
            if conv:
                dense.all_stored(sp)

        @block.gpsimd
        def _(pool):
            def body(b, q):
                s = b + 2
                if kind != ATTEND and runs(s, 0, LAST):
                    hold(pool, idx_ready, s + 1)
                    if runs(s, 2):
                        hold(pool, turned if factor is None else scaled_ready, s - 1)
                    for j in range(BT):
                        pool.indirect_dma_start(rows[:, q, j, :], None, source,
                                                bass.IndirectOffsetOnAxis(ap=gi[:, q, j:j + 1], axis=0))\
                            .then_inc(gathered[q], 16)
                s = b - lag
                qs = (q + lag) % 2
                if runs(s, 0, LAST):
                    hold(pool, new_ready, s + 1)
                    for j in range(BT):
                        pool.indirect_dma_start(out, bass.IndirectOffsetOnAxis(ap=si[:, qs, j:j + 1], axis=0),
                                                new[:, qs, j, :], None, bounds_check=NP - 1, oob_is_err=False)\
                            .then_inc(scattered[qs], 16)
            go(pool, body)
            for q in range(2):
                hold(pool, scattered[q], of_slot(LAST - (LAST - q) % 2, q, 16 * BT))

        @block.scalar
        def _(act):
            def body(b, q):
                o = 1 - q
                s = b + 2
                if kind != ATTEND and runs(s, 0, LAST):
                    if runs(s, 2):
                        act.wait_ge(gathered[q], of_slot(s - 2, q, 16 * BT))
                    act.activation(gi[:, q, :], at(m.src_col, s), ACT.Copy).then_inc(idx_ready, 1)
                if conv:
                    dense.roots(act, b - 2)
                s = b + 1
                if factor is not None and runs(s, 0, LAST):
                    if kind == ATTEND:
                        act.wait_ge(rows_loaded[o], of_slot(s, o, 16))
                    else:
                        act.wait_ge(gathered[o], of_slot(s, o, 16 * BT))
                    if runs(s, 2):
                        act.wait_ge(turned, s - 1)
                    for j in range(BT):
                        last = act.activation(scaled[:, o, j, :], rows[:, o, j, :], ACT.Copy,
                                              scale=factor[:, bass.ds(s * BT + j, 1)])
                    last.then_inc(scaled_ready, 1)
                if n_rel and runs(s, 0, LAST):
                    act.wait_ge(turned, s + 1)
                    if runs(s, 2):
                        act.wait_ge(mask_ready, (s - 1) * n_rel)
                    act.activation(col[:, o, :], T[o][:, :], ACT.Copy).then_inc(col_ready, 1)
                s = b - 3
                if conv and runs(s, 0, LAST):
                    act.wait_ge(y_turned, s + 1)
                    if runs(s, 1):
                        act.wait_ge(yw1_done if kind == CONV1 else post_done, s)
                    act.activation(yT[:, :], S[0][:, :], ACT.Copy).then_inc(yT_copied, 1)
                if conv:
                    dense.columns(act, b, q)
                s = b - 3
                if kind == CONV1 and runs(s, 0, LAST):
                    act.wait_ge(yw1_done, s + 1)
                    if runs(s, 1):
                        act.wait_ge(post_done, s)
                    act.activation(hT[:, :], S[1][:, :], ACT.Relu, bias=m.b1[:, 0:1]).then_inc(hT_ready, 1)
                s = b - 2
                if kind != CONV1 and runs(s, 0, LAST):
                    act.wait_ge(var_ready, s + 1)
                    if runs(s, 1):
                        act.wait_ge(shift_ready, s)
                    act.activation(sd[:, :], norm[1][:, :, 1], ACT.Sqrt, bias=m.eps[:, 0:1]).then_inc(sd_ready, 1)
                    if runs(s, 2):
                        act.wait_ge(scattered[q], of_slot(s - 2, q, 16 * BT))
                    if kind == CONV2 and runs(s, 2):
                        act.wait_ge(xd_ready, s - 1)
                    act.activation(si[:, q, :], at(m.last_col, s), ACT.Copy)
                    act.wait_ge(shift_ready, s + 1)
                    for j in range(BT):
                        last = act.activation(new[:, q, j, :], z[:, q, j, :], ACT.Identity,
                                              bias=shift[:, q, j:j + 1], scale=scale[:, q, j:j + 1])
                    last.then_inc(new_ready, 1)
                    if kind in (MEAN, ATTEND):
                        act.wait_ge(new_ready, s + 1)
                        act.activation(xd_at(s), flat(new[:, q]), ACT.Copy).then_inc(xd_ready, 1)
                if conv:
                    dense.second_and_third(act, b - 2, q)
                s = b - 3
                if kind == CONV1 and runs(s, 0, LAST):
                    if runs(s, 2):
                        act.wait_ge(scattered[o], of_slot(s - 2, o, 16 * BT))
                        act.wait_ge(xd_ready, s - 1)
                    act.activation(si[:, o, :], at(m.last_col, s), ACT.Copy)
                    act.wait_ge(post_done, s + 1)
                    for j in range(BT):
                        last = act.activation(new[:, o, j, :], S[1][:, j * D:(j + 1) * D], ACT.Copy, scale=dinv_of(s, j))
                    last.then_inc(new_ready, 1)
            go(act, body)

        @block.tensor
        def _(pe):
            if n_rel:
                pe.wait_ge(w_loaded, 16)

            def back(s, q):
                if not runs(s, 0, LAST):
                    return
                pe.wait_ge(scanned, s + 1)
                if runs(s, 2):
                    pe.wait_ge(sums_used, s - 1)
                for j in range(BT):
                    last = pe.transpose(B[q][:, j * D:(j + 1) * D], run[:, q, j * TE:(j + 1) * TE], m.ident[:, :])
                last.then_inc(rows_back, 1)

            def relate(s, q, relations):
                if not runs(s, 0, LAST):
                    return
                for r in relations:
                    if r == 0 and runs(s, 2):
                        pe.wait_ge(scanned, s - 1)
                    pe.wait_ge(mask_ready, s * n_rel + r + 1)
                    pe.matmul(H[q][:, :], w[:, r, :], masked[:, r % MASKS, :], start=(r == 0), stop=(r == n_rel - 1))\
                        .then_inc(mask_used, 1)

            def turn_product_rows(s, q):
                if not runs(s, 0, LAST):
                    return
                pe.wait_ge(y_ready if kind == CONV1 else new_ready, s + 1)
                y_rows = y if kind == CONV1 else new[:, q]
                if runs(s, 1):
                    pe.wait_ge(yT_copied, s)
                for j in range(BT):
                    last = pe.transpose(S[0][:, j * TE:(j + 1) * TE], y_rows[:, j, :], m.ident[:, :])
                last.then_inc(y_turned, 1)

            def body(b, q):
                o = 1 - q
                if n_rel:
                    back(b - 2, q)
                if conv:
                    if kind == CONV2:
                        turn_product_rows(b - 3, o)
                    dense.times_root(pe, b - 1, o)
                    dense.turn(pe, b, q)
                s = b - 3
                if kind == CONV1 and runs(s, 0, LAST):
                    pe.wait_ge(yT_copied, s + 1)
                    if runs(s, 1):
                        pe.wait_ge(new_ready, s)
                    pe.matmul(S[1][:, :], m.w1[:, :], yT[:, :], start=True, stop=True).then_inc(yw1_done, 1)
                relate(b, q, range(n_rel // 2))
                s = b + 1
                if runs(s, 0, LAST):
                    if factor is not None:
                        pe.wait_ge(scaled_ready, s + 1)
                    else:
                        pe.wait_ge(gathered[o], of_slot(s, o, 16 * BT))
                    if runs(s, 2):
                        pe.wait_ge(scanned if conv else col_ready, s - 1)
                    for j in range(BT):
                        last = pe.transpose(T[o][:, j * TE:(j + 1) * TE], scaled[:, o, j, :], m.ident[:, :])
                    last.then_inc(turned, 1)
                relate(b, q, range(n_rel // 2, n_rel))
                s = b - 3
                if kind == CONV1 and runs(s, 0, LAST):
                    pe.wait_ge(hT_ready, s + 1)
                    for j in range(BT):
                        last = pe.matmul(S[1][:, j * D:(j + 1) * D], hT[:, j * TE:(j + 1) * TE], m.w2[:, :],
                                         start=True, stop=True)
                    last.then_inc(post_done, 1)
                if conv:
                    back(b - 1, o)
                if kind == CONV1:
                    turn_product_rows(b - 2, q)
                s = b - 3
                if kind == CONV2 and runs(s, 0, LAST):
                    pe.wait_ge(yT_copied, s + 1)
                    if runs(s, 1):
                        pe.wait_ge(xd_ready, s)
                    for j in range(BT):
                        last = pe.matmul(S[1][:, j * D:(j + 1) * D], yT[:, j * TE:(j + 1) * TE], m.root[:, :],
                                         start=True, stop=True)
                    last.then_inc(post_done, 1)
            go(pe, body)

        @block.vector
        def _(v):
            def relate(s, q, relations):
                if not runs(s, 0, LAST):
                    return
                for r in relations:
                    if r == 0:
                        v.wait_ge(col_ready, s + 1)
                        v.wait_ge(typ_loaded[q], of_slot(s, q, 16))
                    if r >= MASKS or runs(s, 1):
                        v.wait_ge(mask_used, s * n_rel + r + 1 - MASKS)
                    v.scalar_tensor_tensor(out=masked[:, r % MASKS, :], in0=typ[:, q, :], scalar=float(r),
                                           in1=col[:, q, :], op0=ALU.is_equal, op1=ALU.mult).then_inc(mask_ready, 1)

            def scan(s, q):
                if not runs(s, 0, LAST):
                    return
                v.wait_ge(same_loaded[q], of_slot(s, q, 16))
                if n_rel:
                    v.wait_ge(mask_used, (s + 1) * n_rel)
                    new_part = H[q][:, :]
                elif conv:
                    v.wait_ge(turned, s + 1)
                    new_part = T[q][:, :]
                else:
                    v.wait_ge(col_ready, s + 1)
                    new_part = col[:, q, :]
                if runs(s, 2):
                    v.wait_ge(rows_back, s - 1)
                if runs(s, 1):
                    v.wait_ge(scanned, s)
                start = 0.0 if static(s) and s == 0 else run[:, 1 - q, BE - 1:BE]
                v.tensor_tensor_scan(run[:, q, :], same[:, q, :], new_part, start, ALU.mult, ALU.add)\
                    .then_inc(scanned, 1)

            def update(s, q):
                if not runs(s, 0, LAST):
                    return
                v.wait_ge(rows_back, s + 1)
                if kind == CONV1:
                    if runs(s, 1):
                        v.wait_ge(y_ready, s)
                    for j in range(BT):
                        last = v.scalar_tensor_tensor(out=y_sum[:, j, :], in0=xd_of(s, j), scalar=dinv_of(s, j),
                                                      in1=B[q][:, j * D:(j + 1) * D], op0=ALU.mult, op1=ALU.add)
                    last.then_inc(y_sum_ready, 1)
                    v.wait_ge(y_sum_ready, s + 1)
                    if runs(s, 1):
                        v.wait_ge(y_turned, s)
                    v.tensor_tensor(y[:, :, :], y_sum[:, :, :], bc(at(m.dinv_col, s), D), ALU.mult).then_inc(y_ready, 1)
                    return
                if runs(s, 2):
                    v.wait_ge(new_ready, s - 1)
                if kind == CONV2:
                    for j in range(BT):
                        last = v.scalar_tensor_tensor(out=z[:, q, j, :], in0=B[q][:, j * D:(j + 1) * D],
                                                      scalar=dinv_of(s, j), in1=xd_of(s, j), op0=ALU.mult, op1=ALU.add)
                    last.then_inc(summed, 1)
                elif kind == SUM:
                    v.scalar_tensor_tensor(out=flat(z[:, q]), in0=B[q][:, :], scalar=0.0, in1=xd_at(s),
                                           op0=ALU.max, op1=ALU.add).then_inc(summed, 1)
                else:
                    v.tensor_tensor(z[:, q], wide(B[q][:, :]), wide(xd_at(s)), ALU.add).then_inc(summed, 1)

            def statistics(s, q):
                if not runs(s, 0, LAST):
                    return
                v.wait_ge(summed, s + 1)
                if runs(s, 1):
                    v.wait_ge(shift_ready, s)
                row_stats(v, z[:, q], norm, stats_ready, s).then_inc(var_ready, 1)

            def normalise(s, q):
                if kind == CONV1 or not runs(s, 0, LAST):
                    return
                v.wait_ge(sd_ready, s + 1)
                v.reciprocal(scale[:, q, :], sd[:, :]).then_inc(scale_ready, 1)
                v.wait_ge(scale_ready, s + 1)
                v.scalar_tensor_tensor(out=shift[:, q, :], in0=norm[1][:, :, 0], scalar=-1.0, in1=scale[:, q, :],
                                       op0=ALU.mult, op1=ALU.mult).then_inc(shift_ready, 1)

            def prepare_next(s, q):
                if not runs(s, 0, LAST):
                    return
                if runs(s, 1):
                    v.wait_ge(xd_ready, s)
                if kind == CONV1:
                    rows_now, bias = wide(xd_at(s)), m.b2_rows
                else:
                    v.wait_ge(new_ready, s + 1)
                    rows_now, bias = new[:, q], m.bias_rows
                v.tensor_tensor(biased[:, :, :], rows_now, bias, ALU.add).then_inc(biased_ready, 1)

            def finish(s, q):
                if not runs(s, 0, LAST):
                    return
                v.wait_ge(biased_ready, s + 1)
                if kind == CONV1:
                    v.wait_ge(new_ready, s + 1)
                    for j in range(BT):
                        last = v.scalar_tensor_tensor(out=xd_of(s, j), in0=new[:, q, j, :], scalar=dinv_of(s, j),
                                                      in1=biased[:, j, :], op0=ALU.mult, op1=ALU.add)
                    last.then_inc(xd_ready, 1)
                else:
                    v.wait_ge(post_done, s + 1)
                    v.tensor_tensor(wide(xd_at(s)), wide(S[1][:, :]), biased[:, :, :], ALU.add).then_inc(xd_ready, 1)

            def body(b, q):
                o = 1 - q
                if conv:
                    prepare_next(b - 4, q)
                    scan(b - 1, o)
                    finish(b - 4, q)
                    update(b - 2, q)
                    dense.scales(v, b - 2, q)
                    dense.sum(v, b - 1, o)
                    dense.shifts(v, b - 2, q)
                    if kind == CONV2:
                        statistics(b - 2, q)
                    dense.fourth(v, b - 2, q)
                    if kind == CONV2:
                        normalise(b - 2, q)
                    dense.variances(v, b - 1, o)
                else:
                    relate(b, q, range(0, n_rel // 4))
                    scan(b - 1, o)
                    relate(b, q, range(n_rel // 4, n_rel // 2))
                    update(b - 2, q)
                    relate(b, q, range(n_rel // 2, n_rel // 2 + 1))
                    statistics(b - 2, q)
                    relate(b, q, range(n_rel // 2 + 1, n_rel * 3 // 4))
                    normalise(b - 2, q)
                    relate(b, q, range(n_rel * 3 // 4, n_rel))
            go(v, body)


def attention_stage(nc, io, m):
    with ExitStack() as ctx:
        sb = lambda n, s, d=F32: ctx.enter_context(nc.sbuf_tensor("at_" + n, s, d))
        sem = Semaphores(nc, "at_")
        pair = lambda n: [sem(n + "_even"), sem(n + "_odd")]
        MASKS = 8
        gi = sb("gi", [P, 2, 2, BT], I32)
        rows = sb("rows", [P, 2, 2, BT, D])
        typ = sb("typ", [P, 2, BE], BF16)
        col = sb("col", [P, 2, 2, BE])
        masked = sb("masked", [P, MASKS, BE])
        prod = sb("prod", [P, 2, BE])
        w, wT, ww = (sb(n, [P, R8, D]) for n in ("w", "wT", "ww"))
        w_loaded, w_turned, wT_copied, ww_done, ww_copied = (
            sem(n) for n in ("w_loaded", "w_turned", "wT_copied", "ww_done", "ww_copied"))
        gathered, typ_loaded, stored = sem.of_pool("gathered"), pair("typ_loaded"), pair("stored")
        idx_ready, turned, col_ready, mask_ready, mask_used, prod_ready, scored, kept = (
            sem(n) for n in ("idx_ready", "turned", "col_ready", "mask_ready", "mask_used", "prod_ready", "scored",
                             "kept"))
        T, WB, U, SC = m.psum[0:2], m.psum[2:4], m.psum[4:6], m.psum[6:8]
        LAST = NB - 1
        ctx.callback(sem.clear)
        block = ctx.enter_context(nc.Block())
        go = lambda eng, body: pipeline(eng, body, -2, NB + 1, 2, 2)

        @block.sync
        def _(sp):
            sp.dma_start(w[:, :, :], io["W_att"].rearrange("r i o -> i r o")).then_inc(w_loaded, 16)

            def body(b, q):
                s = b + 2
                if runs(s, 0, LAST):
                    if runs(s, 2):
                        hold(sp, mask_ready, (s - 1) * R8)
                    plane = m.type_plane[R8][bass.ds(s * BE, BE)]
                    sp.dma_start(typ[:, q, :], plane.rearrange("(a n) -> a n", a=1).to_broadcast([P, BE]))\
                        .then_inc(typ_loaded[q], 16)
                s = b + 1
                if runs(s, 0, LAST):
                    hold(sp, gathered[1 - q], of_slot(s, 1 - q, 32 * BT))
                    sp.dma_start(m.source_rows[:, bass.ds(s * BE, BE)],
                                 rows[:, 1 - q, 0].rearrange("p b d -> p (b d)")).then_inc(stored[1 - q], 16)
            go(sp, body)
            for q in range(2):
                hold(sp, stored[q], of_slot(LAST - (LAST - q) % 2, q, 16))

        @block.gpsimd
        def _(pool):
            def body(b, q):
                s = b + 2
                if runs(s, 0, LAST):
                    hold(pool, idx_ready, s + 1)
                    if runs(s, 2):
                        hold(pool, turned, s - 1)
                        hold(pool, stored[q], of_slot(s - 2, q, 16))
                    for side in range(2):
                        for j in range(BT):
                            pool.indirect_dma_start(rows[:, q, side, j, :], None, m.tables["X2"],
                                                    bass.IndirectOffsetOnAxis(ap=gi[:, q, side, j:j + 1], axis=0))\
                                .then_inc(gathered[q], 16)
            go(pool, body)

        @block.scalar
        def _(act):
            act.wait_ge(w_turned, 1)
            for i in range(2):
                last = act.activation(wT[:, i * 4:(i + 1) * 4, :].rearrange("p r d -> p (r d)"), WB[i][:, :], ACT.Copy)
            last.then_inc(wT_copied, 1)
            act.wait_ge(ww_done, 1)
            for i in range(2):
                last = act.activation(ww[:, i * 4:(i + 1) * 4, :].rearrange("p r d -> p (r d)"), WB[i][:, :], ACT.Copy)
            last.then_inc(ww_copied, 1)

            def body(b, q):
                o = 1 - q
                s = b + 2
                if runs(s, 0, LAST):
                    if runs(s, 2):
                        act.wait_ge(gathered[q], of_slot(s - 2, q, 32 * BT))
                    act.activation(gi[:, q, 0, :], at(m.src_col, s), ACT.Copy)
                    act.activation(gi[:, q, 1, :], at(m.dst_col, s), ACT.Copy).then_inc(idx_ready, 1)
                s = b - 2
                if runs(s, 0, LAST):
                    act.wait_ge(scored, s + 1)
                    act.activation(at(m.score_col, s), SC[q][:, 0:BT], ACT.Copy).then_inc(kept, 1)
                s = b + 1
                if runs(s, 0, LAST):
                    act.wait_ge(turned, s + 1)
                    if runs(s, 2):
                        act.wait_ge(prod_ready, s - 1)
                    act.activation(col[:, o, 0, :], T[0][:, :], ACT.Copy)
                    act.activation(col[:, o, 1, :], T[1][:, :], ACT.Copy).then_inc(col_ready, 1)
            go(act, body)

        @block.tensor
        def _(pe):
            pe.wait_ge(w_loaded, 16)
            for r in range(R8):
                last = pe.transpose(WB[r // 4][:, (r % 4) * D:(r % 4 + 1) * D], w[:, r, :], m.ident[:, :])
            last.then_inc(w_turned, 1)
            pe.wait_ge(wT_copied, 1)
            for r in range(R8):
                last = pe.matmul(WB[r // 4][:, (r % 4) * D:(r % 4 + 1) * D], wT[:, r, :], wT[:, r, :],
                                 start=True, stop=True)
            last.then_inc(ww_done, 1)
            pe.wait_ge(ww_copied, 1)

            def relate(s, q, relations):
                if not runs(s, 0, LAST):
                    return
                for r in relations:
                    if r == 0 and runs(s, 2):
                        pe.wait_ge(prod_ready, s - 1)
                    pe.wait_ge(mask_ready, s * R8 + r + 1)
                    pe.matmul(U[q][:, :], ww[:, r, :], masked[:, r % MASKS, :], start=(r == 0), stop=(r == R8 - 1))\
                        .then_inc(mask_used, 1)

            def body(b, q):
                o = 1 - q
                s = b - 2
                if runs(s, 0, LAST):
                    pe.wait_ge(prod_ready, s + 1)
                    if runs(s, 2):
                        pe.wait_ge(kept, s - 1)
                    for j in range(BT):
                        last = pe.matmul(SC[q][:, j:j + 1], prod[:, q, j * TE:(j + 1) * TE], m.ones[:, 0:1],
                                         start=True, stop=True)
                    last.then_inc(scored, 1)
                relate(b, q, range(0, R8 // 2))
                s = b + 1
                if runs(s, 0, LAST):
                    pe.wait_ge(gathered[o], of_slot(s, o, 32 * BT))
                    if runs(s, 1):
                        pe.wait_ge(col_ready, s)
                    for side in range(2):
                        for j in range(BT):
                            last = pe.transpose(T[side][:, j * TE:(j + 1) * TE], rows[:, o, side, j, :], m.ident[:, :])
                    last.then_inc(turned, 1)
                relate(b, q, range(R8 // 2, R8))
            go(pe, body)

        @block.vector
        def _(v):
            def relate(s, q, relations):
                if not runs(s, 0, LAST):
                    return
                for r in relations:
                    if r == 0:
                        v.wait_ge(col_ready, s + 1)
                        v.wait_ge(typ_loaded[q], of_slot(s, q, 16))
                    if r >= MASKS or runs(s, 1):
                        v.wait_ge(mask_used, s * R8 + r + 1 - MASKS)
                    v.scalar_tensor_tensor(out=masked[:, r % MASKS, :], in0=typ[:, q, :], scalar=float(r),
                                           in1=col[:, q, 1, :], op0=ALU.is_equal, op1=ALU.mult).then_inc(mask_ready, 1)

            def body(b, q):
                o = 1 - q
                relate(b, q, range(0, R8 // 2))
                s = b - 1
                if runs(s, 0, LAST):
                    v.wait_ge(mask_used, (s + 1) * R8)
                    if runs(s, 2):
                        v.wait_ge(scored, s - 1)
                    v.tensor_tensor(prod[:, o, :], col[:, o, 0, :], U[o][:, :], ALU.mult).then_inc(prod_ready, 1)
                relate(b, q, range(R8 // 2, R8))
            go(v, body)


def softmax_stage(nc, io, m):
    with ExitStack() as ctx:
        sb = lambda n, s, d=F32: ctx.enter_context(nc.sbuf_tensor("sm_" + n, s, d))
        sem = Semaphores(nc, "sm_")
        isrel = sb("isrel", [P, R8, KT])
        tmp = sb("tmp", [P, R8, KT])
        low = sb("low", [P, R8, KT])
        score = sb("score", [P, KT])
        best = sb("best", [P, R8])
        top = sb("top", [R8, 1])
        diag = sb("diag", [R8, R8])
        every = sb("every", [P, R8])
        own = sb("own", [P, KT])
        ex = sb("ex", [P, KT])
        part = sb("part", [P, R8])
        chain, ready, exped, pe_done = (sem(n) for n in ("chain", "ready", "exped", "pe_done"))
        ps = m.psum
        ctx.callback(sem.clear)
        block = ctx.enter_context(nc.Block())

        @block.vector
        def _(v):
            n = [0]

            def link(ins):
                n[0] += 1
                ins.then_inc(chain, 1)
                v.wait_ge(chain, n[0])

            def over(col):
                return col.unsqueeze(1).to_broadcast([P, R8, KT])

            v.tensor_scalar(own[:, :], m.score_col[:, :], SLOPE, None, ALU.mult)
            for r in range(R8):
                last = v.tensor_scalar(isrel[:, r, :], m.type_col[:, :], float(r), None, ALU.is_equal)
            link(last)
            v.tensor_tensor(score[:, :], m.score_col[:, :], own[:, :], ALU.max)
            link(v.tensor_scalar(low[:, :, :], isrel[:, :, :], -LOW, LOW, ALU.mult, ALU.add))
            link(v.tensor_tensor(tmp[:, :, :], isrel[:, :, :], over(score[:, :]), ALU.mult))
            link(v.tensor_tensor(tmp[:, :, :], tmp[:, :, :], low[:, :, :], ALU.add))
            v.tensor_reduce(best[:, :], tmp[:, :, :], AX.X, ALU.max).then_inc(ready, 1)
            v.wait_ge(pe_done, 1)
            link(v.tensor_reduce(top[:, :], ps[0][0:R8, 0:P], AX.X, ALU.max))
            v.tensor_scalar(diag[:, :], m.ident[0:R8, 0:R8], top[:, 0:1], None, ALU.mult).then_inc(ready, 1)
            v.wait_ge(pe_done, 2)
            link(v.tensor_copy(every[:, :], ps[1][:, 0:R8]))
            link(v.tensor_tensor(tmp[:, :, :], isrel[:, :, :], bc(every[:, :], KT), ALU.mult))
            link(v.tensor_reduce(own[:, :], tmp[:, :, :].rearrange("p r k -> p k r"), AX.X, ALU.add))
            v.tensor_tensor(score[:, :], score[:, :], own[:, :], ALU.subtract).then_inc(ready, 1)
            v.wait_ge(exped, 1)
            link(v.tensor_tensor(tmp[:, :, :], isrel[:, :, :], over(ex[:, :]), ALU.mult))
            v.tensor_reduce(part[:, :], tmp[:, :, :], AX.X, ALU.add).then_inc(ready, 1)
            v.wait_ge(pe_done, 3)
            link(v.tensor_copy(every[:, :], ps[2][:, 0:R8]))
            link(v.tensor_tensor(tmp[:, :, :], isrel[:, :, :], bc(every[:, :], KT), ALU.mult))
            link(v.tensor_reduce(own[:, :], tmp[:, :, :].rearrange("p r k -> p k r"), AX.X, ALU.add))
            link(v.tensor_scalar(own[:, :], own[:, :], 1e-30, None, ALU.max))
            link(v.reciprocal(own[:, :], own[:, :]))
            v.tensor_tensor(m.alpha_col[:, :], ex[:, :], own[:, :], ALU.mult)

        @block.scalar
        def _(act):
            act.wait_ge(ready, 3)
            act.activation(ex[:, :], score[:, :], ACT.Exp).then_inc(exped, 1)

        @block.tensor
        def _(pe):
            pe.wait_ge(ready, 1)
            pe.transpose(ps[0][0:R8, 0:P], best[:, :], m.ident[:, :]).then_inc(pe_done, 1)
            pe.wait_ge(ready, 2)
            pe.matmul(ps[1][:, 0:R8], m.ones[0:R8, :], diag[:, :], start=True, stop=True).then_inc(pe_done, 1)
            pe.wait_ge(ready, 4)
            pe.matmul(ps[2][:, 0:R8], m.ones[:, :], part[:, :], start=True, stop=True).then_inc(pe_done, 1)


def build(nc, io):
    m = Memory()
    dram = lambda name, shape, dt=F32: nc.dram_tensor(name, shape, dt, kind="Internal").ap()
    m.tables = {"G1": dram("t_g1", (NP, D)), "X1": dram("t_x1", (NP, D)), "X1_EVEN": dram("t_x1_even", (NP, D)),
                "X2": dram("t_x2", (NP, D)),
                "X3": dram("t_x3", (NP, D)), "OUT": io["out"]}
    m.dinv_table = dram("t_dinv", (NP, 1))
    m.same_plane = dram("p_same", (EP,), BF16)
    m.type_plane = {R8: dram("p_type8", (EP,), BF16), R16: dram("p_type16", (EP,), BF16)}
    m.source_rows = dram("source_rows", (P, KT * D))
    m.records = dram("records", (EP, 4), I32)
    m.sorted_dst = dram("sorted_dst", (EP,), I32)
    with ExitStack() as ctx:
        sb = lambda n, s, d=F32: ctx.enter_context(nc.sbuf_tensor("m_" + n, s, d))
        m.psum = [ctx.enter_context(nc.psum_tensor(f"bank{i}", [P, 512], F32)) for i in range(8)]
        m.ident, m.ones, m.iota = sb("ident", [P, P]), sb("ones", [P, P]), sb("iota", [P, RPP])
        m.eps = sb("eps", [P, 1])
        m.w1, m.w2, m.root, m.root1 = (sb(n, [P, D]) for n in ("w1", "w2", "root", "root1"))
        m.b1, m.b2, m.bias = sb("b1", [P, 1]), sb("b2", [P, D]), sb("bias", [P, D])
        m.b2_rows, m.bias_rows = (t[:, :].unsqueeze(1).to_broadcast([P, BT, D]) for t in (m.b2, m.bias))
        column = lambda name: sb(name + "_col", [P, KT])
        m.src_col, m.dst_col, m.last_col, m.dinv_col, m.type_col = map(column, ("src", "dst", "last", "dinv", "type"))
        m.dstraw_col, m.hi_col, m.lo_col, m.ds_col, m.score_col = map(column, ("dstraw", "hi", "lo", "ds", "score"))
        m.weight_col, m.alpha_col = map(column, ("weight", "alpha"))
        m.dst_int, m.hi_int, m.lo_int = (sb(n, [P, KT], I32) for n in ("dst_int", "hi_int", "lo_int"))
        m.xd = sb("xd", [P, KT * D])
        m.halo = sb("halo", [QR, 258], I32)
        m.rows = sb("rows", [QR, 4, 256], I32)
        constants_stage(nc, m)
        order_stage(nc, io, m)
        setup_stage(nc, io, m)
        prefill_stage(nc, io, m)
        edge_stage(nc, io, m, CONV1, io["x"], m.tables["G1"])
        edge_stage(nc, io, m, CONV2, m.tables["G1"], m.tables["X1"])
        edge_stage(nc, io, m, MEAN, m.tables["X1"], m.tables["X2"], io["W_mean"], R8)
        attention_stage(nc, io, m)
        softmax_stage(nc, io, m)
        edge_stage(nc, io, m, ATTEND, None, m.tables["X3"], io["W_att"], R8)
        edge_stage(nc, io, m, SUM, m.tables["X3"], m.tables["OUT"], io["W_sum"], R16)


def kernel(x, src, dst, edge_type_16, edge_type_8, L0_gnn_W1, L0_gnn_b1, L0_gnn_W2, L0_gnn_b2,
           L1_gnn_W, L1_gnn_root, L1_gnn_bias, L2_gnn_W, L3_gnn_weight):
    import numpy as np
    import concourse.bacc as bacc
    from concourse.bass_utils import run_bass_kernel_spmd

    def padded(a, n, fill):
        a = np.asarray(a)
        return np.concatenate([a, np.full((n - a.shape[0],) + a.shape[1:], fill, a.dtype)])

    arrays = {
        "x": padded(x, NP, 0),
        "edges": np.stack([padded(src, EP, PAD_SRC), padded(dst, EP, PAD_DST),
                           padded(edge_type_8, EP, PAD_TYPE), padded(edge_type_16, EP, PAD_TYPE)]),
        "W1": np.asarray(L0_gnn_W1), "b1": np.asarray(L0_gnn_b1),
        "W2": np.asarray(L0_gnn_W2), "b2": np.asarray(L0_gnn_b2),
        "W_mean": np.asarray(L1_gnn_W), "root": np.asarray(L1_gnn_root), "bias": np.asarray(L1_gnn_bias),
        "W_att": np.asarray(L2_gnn_W), "W_sum": np.asarray(L3_gnn_weight),
    }
    arrays = {k + "_dram": np.ascontiguousarray(a) for k, a in arrays.items()}
    nc = bacc.Bacc("TRN2", target_bir_lowering=False, num_devices=1)
    io = {k[:-5]: nc.dram_tensor(k, a.shape, mybir.dt.from_np(a.dtype), kind="ExternalInput").ap()
          for k, a in arrays.items()}
    io["out"] = nc.dram_tensor("out_dram", (NP, D), F32, kind="ExternalOutput").ap()
    build(nc, io)
    got = run_bass_kernel_spmd(nc, [arrays], core_ids=[0])
    return got.results[0]["out_dram"][:N]
```
